# Optimizing a Trainium2 kernel written in Bass

```python
import numpy as np
import jax
import jax.numpy as jnp

def _softmax(x, axis=-1):
    return jax.nn.softmax(x, axis=axis)

def _gelu(x):
    return jax.nn.gelu(x, approximate=True)

def _silu(x):
    return jax.nn.silu(x)

def _sigmoid(x):
    return jax.nn.sigmoid(x)

def _layernorm(x, axis=-1, eps=1e-05):
    m = jnp.mean(x, axis=axis, keepdims=True)
    v = jnp.var(x, axis=axis, keepdims=True)
    return (x - m) / jnp.sqrt(v + eps)

def _scatter_add(tgt, idx, src, axis=0):
    return tgt.at[idx].add(src)

def _segment_sum(src, seg, n):
    return jax.ops.segment_sum(src, seg, n)
kernel_name = 'mk_decoder_postln_d2_seqx_r8_d02ddf'

def setup_inputs(seed: int=0):
    np.random.seed(seed)
    _w = jnp.asarray

    def _rec_inputs():
        import jax
        import jax.numpy as jnp
        _rk = jax.random.key(seed)
        x = -0.0003929 + 0.9999 * jax.random.normal(jax.random.fold_in(_rk, 1), (32, 128, 128), jnp.float32)
        _lenS = 128 - jax.random.randint(jax.random.fold_in(_rk, 7), (32,), 0, max(1, 128 // 4) + 1, jnp.int32)
        _lenS2 = 128 - jax.random.randint(jax.random.fold_in(_rk, 8), (32,), 0, max(1, 128 // 4) + 1, jnp.int32)
        _ctx_768P = jax.random.normal(jax.random.fold_in(_rk, 11), (32, 16, 96), jnp.float32)
        _ctx_768c = jax.random.dirichlet(jax.random.fold_in(_rk, 511), 0.3 * jnp.ones((16,), jnp.float32), (32, 128))
        _ctx_768t = jnp.einsum('bsk,bkd->bsd', _ctx_768c, _ctx_768P)
        _ctx_768t = _ctx_768t * jax.lax.rsqrt(jnp.mean(jnp.square(_ctx_768t)) + 1e-12) * 0.953939
        ctx_768 = 2.09791e-05 + 1.00001 * (_ctx_768t + 0.3 * jax.random.normal(jax.random.fold_in(_rk, 611), (32, 128, 96), jnp.float32))
        return (x, ctx_768)
    x, ctx_768 = _rec_inputs()

    def _L0_attn_setup():
        import math
        import jax, jax.numpy as jnp
        import numpy as np
        EPS_SUM = 1e-07
        EPS_NORM = 1e-12

        def _l2norm(x, axis):
            n = jnp.sqrt(jnp.sum(x * x, axis=axis, keepdims=True))
            return x / jnp.maximum(n, EPS_NORM)
        key = jax.random.key(seed)
        ks = jax.random.split(key, 5)
        b, N, C = (4, 512, 128)
        x = jax.random.normal(ks[0], (b, N, C), dtype=jnp.float32)
        Wqkv = jax.random.normal(ks[1], (C, 3 * C), dtype=jnp.float32) / math.sqrt(C)
        bqkv = jax.random.normal(ks[2], (3 * C,), dtype=jnp.float32) * 0.01
        Wln = jax.random.normal(ks[3], (C, C), dtype=jnp.float32) / math.sqrt(C)
        bln = jax.random.normal(ks[4], (C,), dtype=jnp.float32) * 0.01
        return {'x': x, 'Wqkv': Wqkv, 'bqkv': bqkv, 'Wln': Wln, 'bln': bln}
    _L0_attn_all = _L0_attn_setup()
    _L0_attn_in = {k: v for k, v in _L0_attn_all.items() if k in ('Wqkv', 'bqkv', 'Wln', 'bln')}
    del _L0_attn_all

    def _L0_xattn_setup():
        import jax, jax.numpy as jnp
        import numpy as np
        QUERY_DIM = 128
        KEY_DIM = 96
        NUM_HEADS = 16
        HEAD_DIM = QUERY_DIM // NUM_HEADS
        SCALE = HEAD_DIM ** (-0.5)
        key = jax.random.key(seed)
        ks = jax.random.split(key, 11)
        B, Nq, Nk = (4, 512, 128)
        s_q = QUERY_DIM ** (-0.5)
        s_k = KEY_DIM ** (-0.5)
        return {'query': jax.random.normal(ks[0], (B, Nq, QUERY_DIM), jnp.float32), 'key': jax.random.normal(ks[1], (B, Nk, KEY_DIM), jnp.float32), 'value': jax.random.normal(ks[2], (B, Nk, KEY_DIM), jnp.float32), 'Wq': jax.random.normal(ks[3], (QUERY_DIM, QUERY_DIM), jnp.float32) * s_q, 'bq': jnp.zeros((QUERY_DIM,), jnp.float32), 'Wk': jax.random.normal(ks[4], (KEY_DIM, QUERY_DIM), jnp.float32) * s_k, 'bk': jnp.zeros((QUERY_DIM,), jnp.float32), 'Wv': jax.random.normal(ks[5], (KEY_DIM, QUERY_DIM), jnp.float32) * s_k, 'bv': jnp.zeros((QUERY_DIM,), jnp.float32), 'Wo': jax.random.normal(ks[6], (QUERY_DIM, QUERY_DIM), jnp.float32) * s_q, 'bo': jnp.zeros((QUERY_DIM,), jnp.float32)}
    _L0_xattn_all = _L0_xattn_setup()
    _L0_xattn_in = {k: v for k, v in _L0_xattn_all.items() if k in ('Wq', 'bq', 'Wk', 'bk', 'Wv', 'bv', 'Wo', 'bo')}
    del _L0_xattn_all

    def _L0_ffn_setup():
        import jax, jax.numpy as jnp
        import numpy as np
        B, T, C, I, E = (4, 256, 128, 352, 7)

        def _swiglu(h, w1, w2, w3):
            return jax.nn.silu(h @ w1.T) * (h @ w3.T) @ w2.T
        key = jax.random.key(seed)
        ks = jax.random.split(key, 9)
        sc_c = 1.0 / np.sqrt(C)
        sc_i = 1.0 / np.sqrt(I)
        return {'x': jax.random.normal(ks[0], (B, T, C), jnp.float32), 'router_w': jax.random.normal(ks[1], (E, C), jnp.float32) * sc_c, 'routing_bias': jnp.zeros((E,), jnp.float32), 'sw1': jax.random.normal(ks[2], (I, C), jnp.float32) * sc_c, 'sw2': jax.random.normal(ks[3], (C, I), jnp.float32) * sc_i, 'sw3': jax.random.normal(ks[4], (I, C), jnp.float32) * sc_c, 'ew1': jax.random.normal(ks[5], (E, I, C), jnp.float32) * sc_c, 'ew2': jax.random.normal(ks[6], (E, C, I), jnp.float32) * sc_i, 'ew3': jax.random.normal(ks[7], (E, I, C), jnp.float32) * sc_c}
    _L0_ffn_all = _L0_ffn_setup()
    _L0_ffn_in = {k: v for k, v in _L0_ffn_all.items() if k in ('router_w', 'routing_bias', 'sw1', 'sw2', 'sw3', 'ew1', 'ew2', 'ew3')}
    del _L0_ffn_all

    def _L1_attn_setup():
        import jax, jax.numpy as jnp
        import numpy as np
        B, L, D_IN, D_OUT, H, WIN = (1, 256, 128, 128, 16, 64)
        D_H = D_OUT // H
        key = jax.random.key(seed)
        ks = jax.random.split(key, 5)
        s = 0.02
        return {'x': jax.random.normal(ks[0], (B, L, D_IN), dtype=jnp.float32), 'Wq': jax.random.normal(ks[1], (D_IN, D_OUT), dtype=jnp.float32) * s, 'Wk': jax.random.normal(ks[2], (D_IN, D_OUT), dtype=jnp.float32) * s, 'Wv': jax.random.normal(ks[3], (D_IN, D_OUT), dtype=jnp.float32) * s, 'Wo': jax.random.normal(ks[4], (D_OUT, D_IN), dtype=jnp.float32) * s}
    _L1_attn_all = _L1_attn_setup()
    _L1_attn_in = {k: v for k, v in _L1_attn_all.items() if k in ('Wq', 'Wk', 'Wv', 'Wo')}
    del _L1_attn_all

    def _L1_xattn_setup():
        import jax, jax.numpy as jnp
        import numpy as np
        NUM_HEADS = 16
        EMB_DIM = 128
        CTX_DIM = 96
        D_HEAD = EMB_DIM // NUM_HEADS
        key = jax.random.key(seed)
        ks = jax.random.split(key, 6)
        B, SQ, SKV = (4, 256, 256)
        x = jax.random.normal(ks[0], (B, SQ, EMB_DIM), dtype=jnp.float32)
        ctx = jax.random.normal(ks[1], (B, SKV, CTX_DIM), dtype=jnp.float32)
        sc_q = 1.0 / np.sqrt(EMB_DIM)
        sc_kv = 1.0 / np.sqrt(CTX_DIM)
        Wq = jax.random.normal(ks[2], (EMB_DIM, EMB_DIM), dtype=jnp.float32) * sc_q
        Wk = jax.random.normal(ks[3], (CTX_DIM, EMB_DIM), dtype=jnp.float32) * sc_kv
        Wv = jax.random.normal(ks[4], (CTX_DIM, EMB_DIM), dtype=jnp.float32) * sc_kv
        Wo = jax.random.normal(ks[5], (EMB_DIM, EMB_DIM), dtype=jnp.float32) * sc_q
        return {'x': x, 'contenoised_img': ctx, 'Wq': Wq, 'Wk': Wk, 'Wv': Wv, 'Wo': Wo}
    _L1_xattn_all = _L1_xattn_setup()
    _L1_xattn_in = {k: v for k, v in _L1_xattn_all.items() if k in ('Wq', 'Wk', 'Wv', 'Wo')}
    del _L1_xattn_all

    def _L1_ffn_setup():
        import jax, jax.numpy as jnp
        import numpy as np
        TOP_K = 2
        NUM_EXPERTS = 8
        key = jax.random.key(seed)
        ks = jax.random.split(key, 8)
        h, d, ds, E = (128, 64, 128, NUM_EXPERTS)
        s = 1.0 / np.sqrt(h)
        return {'x': jax.random.normal(ks[0], (2, 256, h), jnp.float32), 'router': jax.random.normal(ks[1], (h, E), jnp.float32) * s, 'experts_gate': jax.random.normal(ks[2], (E, h, d), jnp.float32) * s, 'experts_up': jax.random.normal(ks[3], (E, h, d), jnp.float32) * s, 'experts_down': jax.random.normal(ks[4], (E, d, h), jnp.float32) * (1.0 / np.sqrt(d)), 'shared_gate': jax.random.normal(ks[5], (h, ds), jnp.float32) * s, 'shared_up': jax.random.normal(ks[6], (h, ds), jnp.float32) * s, 'shared_down': jax.random.normal(ks[7], (ds, h), jnp.float32) * (1.0 / np.sqrt(ds))}
    _L1_ffn_all = _L1_ffn_setup()
    _L1_ffn_in = {k: v for k, v in _L1_ffn_all.items() if k in ('router', 'experts_gate', 'experts_up', 'experts_down', 'shared_gate', 'shared_up', 'shared_down')}
    del _L1_ffn_all
    return {'x': x, 'ctx_768': ctx_768, 'L0_attn_Wqkv': _L0_attn_in['Wqkv'], 'L0_attn_bqkv': _L0_attn_in['bqkv'], 'L0_attn_Wln': _L0_attn_in['Wln'], 'L0_attn_bln': _L0_attn_in['bln'], 'L0_xattn_Wq': _L0_xattn_in['Wq'], 'L0_xattn_bq': _L0_xattn_in['bq'], 'L0_xattn_Wk': _L0_xattn_in['Wk'], 'L0_xattn_bk': _L0_xattn_in['bk'], 'L0_xattn_Wv': _L0_xattn_in['Wv'], 'L0_xattn_bv': _L0_xattn_in['bv'], 'L0_xattn_Wo': _L0_xattn_in['Wo'], 'L0_xattn_bo': _L0_xattn_in['bo'], 'L0_ffn_router_w': _L0_ffn_in['router_w'], 'L0_ffn_routing_bias': _L0_ffn_in['routing_bias'], 'L0_ffn_sw1': _L0_ffn_in['sw1'], 'L0_ffn_sw2': _L0_ffn_in['sw2'], 'L0_ffn_sw3': _L0_ffn_in['sw3'], 'L0_ffn_ew1': _L0_ffn_in['ew1'], 'L0_ffn_ew2': _L0_ffn_in['ew2'], 'L0_ffn_ew3': _L0_ffn_in['ew3'], 'L1_attn_Wq': _L1_attn_in['Wq'], 'L1_attn_Wk': _L1_attn_in['Wk'], 'L1_attn_Wv': _L1_attn_in['Wv'], 'L1_attn_Wo': _L1_attn_in['Wo'], 'L1_xattn_Wq': _L1_xattn_in['Wq'], 'L1_xattn_Wk': _L1_xattn_in['Wk'], 'L1_xattn_Wv': _L1_xattn_in['Wv'], 'L1_xattn_Wo': _L1_xattn_in['Wo'], 'L1_ffn_router': _L1_ffn_in['router'], 'L1_ffn_experts_gate': _L1_ffn_in['experts_gate'], 'L1_ffn_experts_up': _L1_ffn_in['experts_up'], 'L1_ffn_experts_down': _L1_ffn_in['experts_down'], 'L1_ffn_shared_gate': _L1_ffn_in['shared_gate'], 'L1_ffn_shared_up': _L1_ffn_in['shared_up'], 'L1_ffn_shared_down': _L1_ffn_in['shared_down']}

def reference(x, ctx_768, L0_attn_Wqkv, L0_attn_bqkv, L0_attn_Wln, L0_attn_bln, L0_xattn_Wq, L0_xattn_bq, L0_xattn_Wk, L0_xattn_bk, L0_xattn_Wv, L0_xattn_bv, L0_xattn_Wo, L0_xattn_bo, L0_ffn_router_w, L0_ffn_routing_bias, L0_ffn_sw1, L0_ffn_sw2, L0_ffn_sw3, L0_ffn_ew1, L0_ffn_ew2, L0_ffn_ew3, L1_attn_Wq, L1_attn_Wk, L1_attn_Wv, L1_attn_Wo, L1_xattn_Wq, L1_xattn_Wk, L1_xattn_Wv, L1_xattn_Wo, L1_ffn_router, L1_ffn_experts_gate, L1_ffn_experts_up, L1_ffn_experts_down, L1_ffn_shared_gate, L1_ffn_shared_up, L1_ffn_shared_down):
    import jax
    import jax.numpy as jnp

    def _L0_attn_ref(x, Wqkv, bqkv, Wln, bln):
        import math
        import jax, jax.numpy as jnp
        import numpy as np
        EPS_SUM = 1e-07
        EPS_NORM = 1e-12

        def _l2norm(x, axis):
            n = jnp.sqrt(jnp.sum(x * x, axis=axis, keepdims=True))
            return x / jnp.maximum(n, EPS_NORM)
        b, N, C = x.shape
        qkv = x @ Wqkv + bqkv
        q, k, v = jnp.split(qkv, 3, axis=2)
        q = q - q.mean(axis=2, keepdims=True)
        k = k - k.mean(axis=2, keepdims=True)
        q2 = q * q
        k2 = k * k
        q2 = q2 / (q2.sum(axis=2, keepdims=True) + EPS_SUM)
        q2 = _l2norm(q2, axis=-1)
        k2 = k2 / (k2.sum(axis=2, keepdims=True) + EPS_SUM)
        k2 = _l2norm(k2, axis=-2)
        kv = jnp.einsum('bnc,bnd->bcd', k2, v)
        t2 = jnp.einsum('bnc,bcd->bnd', q2, kv) / math.sqrt(N)
        return (v + t2) @ Wln + bln

    def _L0_xattn_ref(query, key, value, Wq, bq, Wk, bk, Wv, bv, Wo, bo):
        import jax, jax.numpy as jnp
        import numpy as np
        QUERY_DIM = 128
        KEY_DIM = 96
        NUM_HEADS = 16
        HEAD_DIM = QUERY_DIM // NUM_HEADS
        SCALE = HEAD_DIM ** (-0.5)
        B, Nq, _ = query.shape
        Nk = key.shape[1]
        q = (query @ Wq + bq).reshape(B, Nq, NUM_HEADS, HEAD_DIM).transpose(0, 2, 1, 3)
        k = (key @ Wk + bk).reshape(B, Nk, NUM_HEADS, HEAD_DIM).transpose(0, 2, 1, 3)
        v = (value @ Wv + bv).reshape(B, Nk, NUM_HEADS, HEAD_DIM).transpose(0, 2, 1, 3)
        attn = jnp.einsum('bhqd,bhkd->bhqk', q, k) * SCALE
        attn = jax.nn.softmax(attn, axis=-1)
        out = jnp.einsum('bhqk,bhkd->bhqd', attn, v)
        out = out.transpose(0, 2, 1, 3).reshape(B, Nq, QUERY_DIM)
        return out @ Wo + bo

    def _L0_ffn_ref(x, router_w, routing_bias, sw1, sw2, sw3, ew1, ew2, ew3):
        import jax, jax.numpy as jnp
        import numpy as np
        B, T, C, I, E = (4, 256, 128, 352, 7)

        def _swiglu(h, w1, w2, w3):
            return jax.nn.silu(h @ w1.T) * (h @ w3.T) @ w2.T
        b, t, c = x.shape
        shared_out = _swiglu(x, sw1, sw2, sw3)
        logits = jnp.clip(x @ router_w.T + routing_bias, -50.0, 50.0)
        probs = jax.nn.sigmoid(logits)
        num_switched = 1
        topk_probs, topk_idx = jax.lax.top_k(probs, num_switched)
        topk_probs = jnp.clip(topk_probs, 1e-08, 1.0 - 1e-08)
        xf = x.reshape(-1, c)
        sel = topk_idx.reshape(-1)
        p = topk_probs.reshape(-1)
        switched = jnp.zeros_like(xf)
        n_experts = ew1.shape[0]
        for e in range(n_experts):
            y = _swiglu(xf, ew1[e], ew2[e], ew3[e])
            w = jnp.where(sel == e, p, 0.0)
            switched = switched + w[:, None] * y
        switched = switched.reshape(b, t, c)
        total_weight = 0.5 + topk_probs.sum(axis=-1)
        total_weight = jnp.clip(total_weight[..., None] + 1e-08, 0.5, 2.0)
        return 0.5 / total_weight * shared_out + switched / total_weight

    def _L1_attn_ref(x, Wq, Wk, Wv, Wo):
        import jax, jax.numpy as jnp
        import numpy as np
        B, L, D_IN, D_OUT, H, WIN = (1, 256, 128, 128, 16, 64)
        D_H = D_OUT // H
        Bx, Lx, _ = x.shape
        W = min(WIN, Lx)
        scale = D_H ** (-0.5)

        def split_heads(t):
            return t.reshape(Bx, Lx, H, D_H).transpose(0, 2, 1, 3)
        q = split_heads(x @ Wq)
        k = split_heads(x @ Wk)
        v = split_heads(x @ Wv)
        offsets = jnp.arange(W) - (W - 1)
        idx = jnp.arange(Lx)[:, None] + offsets[None, :]
        invalid = idx < 0
        idx = jnp.clip(idx, 0, Lx - 1)
        k_win = jnp.take(k, idx, axis=2)
        v_win = jnp.take(v, idx, axis=2)
        scores = jnp.einsum('bhld,bhlwd->bhlw', q, k_win) * scale
        scores = jnp.where(invalid[None, None, :, :], -jnp.inf, scores)
        attn = jax.nn.softmax(scores, axis=-1)
        ctx = jnp.einsum('bhlw,bhlwd->bhld', attn, v_win)
        ctx = ctx.transpose(0, 2, 1, 3).reshape(Bx, Lx, D_OUT)
        return ctx @ Wo

    def _L1_xattn_ref(x, contenoised_img, Wq, Wk, Wv, Wo):
        import jax, jax.numpy as jnp
        import numpy as np
        NUM_HEADS = 16
        EMB_DIM = 128
        CTX_DIM = 96
        D_HEAD = EMB_DIM // NUM_HEADS
        B, SQ, E = x.shape
        SKV = contenoised_img.shape[1]
        q = x @ Wq
        k = contenoised_img @ Wk
        v = contenoised_img @ Wv
        q = q.reshape(B, SQ, NUM_HEADS, D_HEAD).transpose(0, 2, 1, 3)
        k = k.reshape(B, SKV, NUM_HEADS, D_HEAD).transpose(0, 2, 1, 3)
        v = v.reshape(B, SKV, NUM_HEADS, D_HEAD).transpose(0, 2, 1, 3)
        scale = 1.0 / jnp.sqrt(jnp.asarray(D_HEAD, dtype=q.dtype))
        scores = jnp.einsum('bhqd,bhkd->bhqk', q, k) * scale
        weights = jax.nn.softmax(scores, axis=-1)
        out = jnp.einsum('bhqk,bhkd->bhqd', weights, v)
        out = out.transpose(0, 2, 1, 3).reshape(B, SQ, E)
        return out @ Wo

    def _L1_ffn_ref(x, router, experts_gate, experts_up, experts_down, shared_gate, shared_up, shared_down):
        import jax, jax.numpy as jnp
        import numpy as np
        TOP_K = 2
        NUM_EXPERTS = 8
        b, s, h = x.shape
        E = router.shape[1]
        shared_act = jax.nn.silu(jnp.einsum('bsh,hd->bsd', x, shared_gate))
        shared_up_out = jnp.einsum('bsh,hd->bsd', x, shared_up)
        shared_out = jnp.einsum('bsd,dh->bsh', shared_act * shared_up_out, shared_down)
        router_probs = jax.nn.softmax(jnp.einsum('bsh,he->bse', x, router), axis=-1)
        topk_probs, topk_idx = jax.lax.top_k(router_probs, TOP_K)
        coef = jnp.sum(jax.nn.one_hot(topk_idx, E, dtype=x.dtype) * topk_probs[..., None], axis=2)
        coef = coef.reshape(b * s, E)
        x_flat = x.reshape(b * s, h)
        gate = jnp.einsum('th,ehd->etd', x_flat, experts_gate)
        up = jnp.einsum('th,ehd->etd', x_flat, experts_up)
        expert_out = jnp.einsum('etd,edh->eth', jax.nn.silu(gate) * up, experts_down)
        routed = jnp.einsum('eth,te->th', expert_out, coef)
        return routed.reshape(b, s, h) + shared_out
    x = _layernorm(x + _L0_attn_ref(x, L0_attn_Wqkv, L0_attn_bqkv, L0_attn_Wln, L0_attn_bln), axis=-1)
    x = _layernorm(x + _L0_xattn_ref(x, ctx_768, ctx_768, L0_xattn_Wq, L0_xattn_bq, L0_xattn_Wk, L0_xattn_bk, L0_xattn_Wv, L0_xattn_bv, L0_xattn_Wo, L0_xattn_bo), axis=-1)
    x = _layernorm(x + _L0_ffn_ref(x, L0_ffn_router_w, L0_ffn_routing_bias, L0_ffn_sw1, L0_ffn_sw2, L0_ffn_sw3, L0_ffn_ew1, L0_ffn_ew2, L0_ffn_ew3), axis=-1)
    x = _layernorm(x + _L1_attn_ref(x, L1_attn_Wq, L1_attn_Wk, L1_attn_Wv, L1_attn_Wo), axis=-1)
    x = _layernorm(x + _L1_xattn_ref(x, ctx_768, L1_xattn_Wq, L1_xattn_Wk, L1_xattn_Wv, L1_xattn_Wo), axis=-1)
    x = _layernorm(x + _L1_ffn_ref(x, L1_ffn_router, L1_ffn_experts_gate, L1_ffn_experts_up, L1_ffn_experts_down, L1_ffn_shared_gate, L1_ffn_shared_up, L1_ffn_shared_down), axis=-1)
    return x

_drawn_inputs = setup_inputs


def setup_inputs(seed=0):
    import zlib

    import numpy as np

    out = dict(_drawn_inputs(seed))
    spreads = {'L0_xattn_bq': (0.0, 0.1),
     'L0_xattn_bk': (0.0, 0.8),
     'L0_xattn_bv': (0.0, 0.1),
     'L0_xattn_bo': (0.0, 0.1),
     'L0_ffn_routing_bias': (0.0, 0.1)}
    factors = {'L1_attn_Wq': 8.0, 'L1_attn_Wk': 8.0}
    for name, (base, spread) in spreads.items():
        noise = np.random.default_rng([zlib.crc32(name.encode()), seed]).standard_normal(out[name].shape)
        drawn = base * np.exp(spread * noise) if base else spread * noise
        out[name] = jnp.asarray(drawn.astype(out[name].dtype))
    for name, factor in factors.items():
        out[name] = (out[name] * factor).astype(out[name].dtype)
    return out
```

```python
from contextlib import ExitStack

import numpy as np

import concourse.bass as bass
from concourse import mybir

B, N, C, CTX = 32, 128, 128, 96
SEQS = 4
GROUPS = B // SEQS
T = SEQS * N
H, D = 16, 8
NJ, NG = 4, 4
WIN = 64
E0, I0 = 7, 352
E1, I1, S1 = 8, 64, 128
SCALE = D ** -0.5
DVE_STEPS = 49
EPS_LN = 1e-5
EPS_SUM = 1e-7
EPS_NORM2 = 1e-24
MASKED = -1e30
SLOT = 32

CHUNKS0 = [(0, 128), (128, 128), (256, 96)]


def _ranges(parts):
    at, out = 0, {}
    for name, n in parts:
        out[name] = (at, at + n)
        at += n
    return out, at


SPLIT, SPLIT_COLS = _ranges(
    [(f"{a}_{w}", 128) for a in ("X0", "A1", "X1") for w in ("q", "k")]
    + [(f"F0_{w}{e}", I0) for e in range(E0 + 1) for w in ("gate", "up")]
    + [("F1_gate", S1 + E1 * I1), ("F1_up", S1 + E1 * I1)])
PLAIN, PLAIN_COLS = _ranges(
    [("A0_qkv", 3 * C), ("A0_out", C)]
    + [(f"{a}_{w}", C) for a in ("X0", "A1", "X1") for w in ("v", "o")]
    + [("F0_router", 8), ("F1_router", 8)]
    + [(f"F0_down{e}", 3 * C) for e in range(E0 + 1)]
    + [("F1_down", 5 * C)])
CONST, CONST_COLS = _ranges(
    [("ident", 128), ("sum", NJ * SLOT), ("first", 8),
     ("A0_bqkv", 3 * C), ("A0_bout", C), ("X0_bv", C), ("X0_bo", C), ("F0_brouter", 8),
     ("X0_bq", 1), ("X0_bk", 1), ("A0_bv", 1), ("one", 1)])
MASK_COLS = 2 * NG * N + N

ROUNDS0 = [([(c0, n) for c0, n in CHUNKS0],
            [(e, [(i, 0, n, i * C) for i, (_, n) in enumerate(CHUNKS0)])]) for e in range(E0 + 1)]
ROUNDS1 = [([(0, 128)], [(0, [(0, 0, 128, 0)])])] + [
    ([(128 * (p + 1), 128)], [(1 + 2 * p + s, [(0, I1 * s, I1, (p + 1) * C)]) for s in range(2)])
    for p in range(E1 // 2)]


def counts(rounds):
    return sum(len(c) for c, _ in rounds), sum(len(e) for _, e in rounds)


class Signal:

    def __init__(self, sem, per, base=0):
        self.sem, self.per, self.base = sem, per, base

    def at(self, it, count):
        return it * self.per + self.base + count


def decoder_kernel(nc, x_d, ctx_d, split_d, plain_d, const_d, mask_d, out_d):
    f32, f32r, bf16 = mybir.dt.float32, mybir.dt.float32r, mybir.dt.bfloat16
    ALU = mybir.AluOpType
    ACT = mybir.ActivationFunctionType
    AX = mybir.AxisListType.X

    ctx = ExitStack()
    with ctx:
        def sb(name, shape, dt=f32):
            return ctx.enter_context(nc.sbuf_tensor(name, shape, dt))

        def sig(name, per=1):
            return Signal(ctx.enter_context(nc.semaphore(name)), per)

        shared = {}

        def block_sig(name, own, per):
            if name not in shared:
                shared[name] = [ctx.enter_context(nc.semaphore(name)), 0]
            sem, used = shared[name]
            shared[name][1] += own
            assert used + own <= per
            return Signal(sem, per, used)

        w_hi = sb("w_hi", [128, SPLIT_COLS], f32r)
        w_lo = sb("w_lo", [128, SPLIT_COLS], f32r)
        plain = sb("plain", [128, PLAIN_COLS])
        const = sb("const", [128, CONST_COLS])
        masks = sb("masks", [128, MASK_COLS], bf16)
        STAGE = 960
        big = sb("big", [128, 8 * T])
        half = sb("half", [128, 8])
        wsum = sb("wsum", [128, 4])

        def W(name, rows=128):
            a, b = PLAIN[name]
            return plain[0:rows, a:b]

        def K(name):
            a, b = CONST[name]
            return const[:, a:b]

        ident = K("ident")
        one = K("one")

        x_in = sb("x_in", [128, SEQS, C])
        c_in = sb("c_in", [128, SEQS, CTX])
        x = sb("x", [128, SEQS, C])
        xb = sb("xb", [128, SEQS, C])
        z = sb("z", [128, SEQS, C])
        xT = sb("xT", [128, T])
        xT_hi = sb("xT_hi", [128, T], f32r)
        xT_lo = sb("xT_lo", [128, T], f32r)
        cT = sb("cT", [CTX, T])
        cT_hi = sb("cT_hi", [CTX, T], f32r)
        cT_lo = sb("cT_lo", [CTX, T], f32r)
        y_out = sb("y_out", [128, SEQS, C])
        bn = sb("bn", [128, SEQS, 6])
        mv = sb("mv", [128, SEQS, 2])
        var = sb("var", [128, SEQS])
        rstd = sb("rstd", [128, SEQS])
        q_hi = sb("q_hi", [128, T], f32r)
        q_lo = sb("q_lo", [128, T], f32r)
        k_hi = sb("k_hi", [128, T], f32r)
        k_lo = sb("k_lo", [128, T], f32r)
        q_stack = sb("q_stack", [128, NG, T], f32r)
        k_stack = sb("k_stack", [128, NG, T], f32r)
        q_diag = sb("q_diag", [128, 2, NG, NJ, N], f32r)
        k_diag = sb("k_diag", [128, 2, NG, NJ, N], f32r)
        zero_row = sb("zero_row", [NJ, T])
        v_pad = sb("v_pad", [128, SEQS, H, SLOT])
        row_max = sb("row_max", [128, 2, H])
        maxT = sb("maxT", [H, 2, N], f32r)
        stage = big[:, 0:2 * STAGE].rearrange("p (i n) -> p i n", i=2)
        probs = big[:].rearrange("p (i g j n) -> p i g j n", i=2, j=NJ, g=NG)
        rden = sb("rden", [128, 2, N])
        attT = sb("attT", [128, 2, N])
        qkv = big[:, 0:3 * T].rearrange("p (b c) -> p b c", b=SEQS)
        sq = big[:, 3 * T:5 * T].rearrange("p (b i c) -> p b i c", b=SEQS, i=2)
        sqn = big[:, 5 * T:7 * T].rearrange("p (b i c) -> p b i c", b=SEQS, i=2)
        sq4 = sq
        ssum = sb("ssum", [128, SEQS, 2])
        rsum = sb("rsum", [128, SEQS, 2])
        qn2 = sb("qn2", [128, SEQS])
        qn2c = sb("qn2c", [128, SEQS])
        qr = sb("qr", [128, SEQS])
        kn2c = sb("kn2c", [128, SEQS])
        kr = sb("kr", [128, SEQS])
        q2 = sb("q2", [128, SEQS, C])
        q2T = sb("q2T", [128, T])
        kv = sb("kv", [128, SEQS, C])
        uT = sb("uT", [128, T])
        act = big[:, 0:2 * T].rearrange("p (i t) -> p i t", i=2)
        hidden = big[:, 2 * T:8 * T].rearrange("p (i s t) -> p i s t", i=2, s=3)
        rt = [sb(f"rt{i}", [128, SEQS, 8]) for i in range(6)]
        rs = [sb(f"rs{i}", [128, SEQS]) for i in range(4)]
        coef = sb("coef", [128, SEQS, 16])

        bank = [ctx.enter_context(nc.psum_tensor(f"bank{i}", [128, 512], f32)) for i in range(8)]
        Y = bank[7]

        ld_const = sig("ld_const")
        ld_stage = [sig("ld_stage0"), sig("ld_stage1")]
        st_hi = sig("st_hi")
        st_lo = sig("st_lo")
        fills = sig("fills")
        centred = sig("centred")
        x_loaded = sig("x_loaded", 16)
        c_loaded = sig("c_loaded", 16)
        stored = sig("stored", 16)
        dve_step = sig("dve_step", DVE_STEPS)
        centred_step = sig("centred_step")
        cT_ps = sig("cT_ps")
        cT_f = sig("cT_f")
        cT_h = sig("cT_h")
        cT_l = sig("cT_l")

        class Ln:
            def __init__(s):
                s.stats = block_sig("ln_stats", 1, 6)
                s.rstd = block_sig("ln_rstd", 1, 6)
                s.x = block_sig("ln_x", 1, 6)

        class Tr:
            def __init__(s, split):
                s.ps = block_sig("xT_ps", 1, 6)
                s.f = block_sig("xT_f", 1, 6)
                if split:
                    s.hi = block_sig("xT_hi", 1, 5)
                    s.lo = block_sig("xT_lo", 1, 5)

        class Att:
            def __init__(s, name, windowed, biased, cross):
                s.name, s.windowed, s.biased, s.cross = name, windowed, biased, cross
                s.q_ps, s.k_ps, s.v_ps = block_sig("att_q_ps", 1, 3), block_sig("att_k_ps", 1, 3), block_sig("att_v_ps", 1, 3)
                s.q_hi, s.q_lo = block_sig("att_q_hi", 1, 3), block_sig("att_q_lo", 1, 3)
                s.k_hi, s.k_lo = block_sig("att_k_hi", 1, 3), block_sig("att_k_lo", 1, 3)
                s.v_sb = block_sig("att_v_sb", 1, 3)
                s.stacked = block_sig("att_stacked", 7 * 16, 3 * 7 * 16)
                s.k_diag = block_sig("att_k_diag", SEQS, 3 * SEQS)
                s.q_diag = block_sig("att_q_diag", SEQS, 3 * SEQS)
                s.s_ps = block_sig("att_s_ps", SEQS * NJ, 3 * SEQS * NJ)
                s.max = block_sig("att_max", SEQS * NJ, 3 * SEQS * NJ)
                s.m_ps = block_sig("att_m_ps", SEQS, 3 * SEQS)
                s.m_sb = block_sig("att_m_sb", SEQS, 3 * SEQS)
                s.m_in = [block_sig(f"att_m_in{i}", 16 * SEQS // 2, 3 * 16 * SEQS // 2) for i in range(2)]
                s.t_ps = block_sig("att_t_ps", SEQS * NJ, 3 * SEQS * NJ)
                s.exp = block_sig("att_exp", SEQS * NJ, 3 * SEQS * NJ)
                s.pv = block_sig("att_pv", SEQS, 3 * SEQS)
                s.rden = block_sig("att_rden", SEQS, 3 * SEQS)
                s.att = block_sig("att_att", SEQS, 3 * SEQS)
                s.y = block_sig("att_y", 1, 3)

        class Ffn:
            def __init__(s, name, rounds):
                s.name, s.rounds = name, rounds
                s.chunks, s.experts = counts(rounds)
                chunks, experts = (p + q for p, q in zip(counts(ROUNDS0), counts(ROUNDS1)))
                s.r_ps = block_sig("ffn_r_ps", 1, 2)
                s.r_arg = block_sig("ffn_r_arg", 1, 2)
                s.r_exp = block_sig("ffn_r_exp", 1, 2)
                s.up = block_sig("ffn_up", s.chunks, chunks)
                s.act = block_sig("ffn_act", s.chunks, chunks)
                s.hid = block_sig("ffn_hid", s.chunks, chunks)
                s.down = block_sig("ffn_down", s.experts, experts)
                s.comb = block_sig("ffn_comb", s.experts, experts)

        a0_ps = sig("a0_ps", SEQS)
        a0_qkv = sig("a0_qkv", SEQS)
        a0_sq = sig("a0_sq")
        a0_sqn = sig("a0_sqn")
        a0_sq4q = sig("a0_sq4q")
        a0_sq4k = sig("a0_sq4k")
        a0_qn = sig("a0_qn")
        a0_qr = sig("a0_qr")
        a0_q2 = sig("a0_q2")
        a0_kn_ps = sig("a0_kn_ps")
        a0_kn = sig("a0_kn")
        a0_kr = sig("a0_kr")
        a0_kv_ps = sig("a0_kv_ps")
        a0_kv = sig("a0_kv")
        a0_q2T_ps = sig("a0_q2T_ps")
        a0_q2T = sig("a0_q2T")
        a0_u_ps = sig("a0_u_ps")
        a0_u = sig("a0_u")
        a0_y = sig("a0_y")
        a0_xb = sig("a0_xb")
        x0_xb = sig("x0_xb")

        X0 = Att("x0", False, True, True)
        A1 = Att("a1", True, False, False)
        X1 = Att("x1", False, False, True)
        F0 = Ffn("f0", ROUNDS0)
        F1 = Ffn("f1", ROUNDS1)
        LN = {n: Ln() for n in ("a0", "x0", "f0", "a1", "x1", "f1")}
        TR = {n: Tr(n != "a0") for n in ("a0", "x0", "f0", "a1", "x1", "f1")}
        BEFORE = {"x0": "a0", "f0": "x0", "a1": "f0", "x1": "a1", "f1": "x1"}

        block = ctx.enter_context(nc.Block())
        n_stages = SPLIT_COLS // STAGE
        assert n_stages * STAGE == SPLIT_COLS

        @block.sync
        def _(sp):
            def load_x(first):
                sp.dma_start(x_in[:], x_d[bass.ds(first, SEQS)].rearrange("b n c -> n b c")).then_inc(x_loaded.sem, 16)

            def load_c(first):
                sp.dma_start(c_in[:], ctx_d[bass.ds(first, SEQS)].rearrange("b n c -> n b c")).then_inc(c_loaded.sem, 16)

            sp.dma_start(const[:], const_d).then_inc(ld_const.sem, 16)
            sp.dma_start(masks[:], mask_d).then_inc(ld_const.sem, 16)
            sp.dma_start(plain[:], plain_d).then_inc(ld_const.sem, 16)
            for n in range(n_stages):
                if n >= 2:
                    sp.wait_ge(st_lo.sem, n - 1)
                sp.dma_start(stage[:, n % 2, :], split_d[:, n * STAGE:(n + 1) * STAGE]).then_inc(ld_stage[n % 2].sem, 16)

            def attention(s, it):
                sp.wait_ge(s.q_hi.sem, s.q_hi.at(it, 1))
                sp.dma_start(q_stack[0::4].bitcast(f32), q_hi[:].bitcast(f32)).then_inc(s.stacked.sem, 16)
                sp.dma_start(q_stack[1::4].bitcast(f32), q_hi[:].bitcast(f32)).then_inc(s.stacked.sem, 16)
                sp.dma_start(q_stack[3::32].bitcast(f32), zero_row[:].unsqueeze(1).to_broadcast((NJ, NG, T))).then_inc(s.stacked.sem, 16)
                sp.wait_ge(s.k_hi.sem, s.k_hi.at(it, 1))
                sp.dma_start(k_stack[0::4].bitcast(f32), k_hi[:].bitcast(f32)).then_inc(s.stacked.sem, 16)
                sp.dma_start(k_stack[2::4].bitcast(f32), k_hi[:].bitcast(f32)).then_inc(s.stacked.sem, 16)
                sp.wait_ge(s.q_lo.sem, s.q_lo.at(it, 1))
                sp.dma_start(q_stack[2::4].bitcast(f32), q_lo[:].bitcast(f32)).then_inc(s.stacked.sem, 16)
                sp.wait_ge(s.k_lo.sem, s.k_lo.at(it, 1))
                sp.dma_start(k_stack[1::4].bitcast(f32), k_lo[:].bitcast(f32)).then_inc(s.stacked.sem, 16)
                for b in range(SEQS):
                    sp.wait_ge(s.m_sb.sem, s.m_sb.at(it, b + 1))
                    sp.dma_start(q_stack[3::32, :, b * N:(b + 1) * N].bitcast(f32), maxT[:, b % 2, :].bitcast(f32)).then_inc(s.m_in[b % 2].sem, 16)

            load_x(0)
            load_c(0)
            sp.wait_ge(fills.sem, 1)
            with sp.Fori(0, GROUPS) as it:
                attention(X0, it)
                sp.wait_ge(a0_xb.sem, a0_xb.at(it, 1))
                sp.wait_ge(cT_ps.sem, cT_ps.at(it, 1))
                load_x((it + 1) % GROUPS * SEQS)
                attention(A1, it)
                attention(X1, it)
                sp.wait_ge(LN["f1"].x.sem, LN["f1"].x.at(it, 1))
                sp.dma_start(out_d[bass.ds(it * SEQS, SEQS)].rearrange("b n c -> n b c"), y_out[:]).then_inc(stored.sem, 16)
                sp.wait_ge(stored.sem, stored.at(it, 16))
                load_c((it + 1) % GROUPS * SEQS)
            sp.wait_ge(stored.sem, 16 * GROUPS)
            sp.wait_ge(x_loaded.sem, 16 * (GROUPS + 1))
            sp.wait_ge(c_loaded.sem, 16 * (GROUPS + 1))

        @block.tensor
        def _(pe):
            mm = nc.tensor.matmul

            def split_matmul(out, wname, c0, n, hi, lo, rows=128):
                a = SPLIT[wname][0] + c0
                wh, wl = w_hi[0:rows, a:a + n], w_lo[0:rows, a:a + n]
                mm(out, wh, lo[:], start=True, stop=False)
                mm(out, wl, hi[:], start=False, stop=False)
                return mm(out, wh, hi[:], start=False, stop=True)

            def transpose_x(s, src):
                for b in range(SEQS):
                    last = nc.tensor.transpose(bank[6][:, b * N:(b + 1) * N], src[:, b, :], ident)
                last.then_inc(s.ps.sem, 1)

            def linear_attention(it):
                for b in range(SEQS):
                    mm(bank[b][:, 0:3 * C], xT[:, b * N:(b + 1) * N], W("A0_qkv"), start=True, stop=True).then_inc(a0_ps.sem, 1)
                pe.wait_ge(a0_sqn.sem, a0_sqn.at(it, 1))
                for b in range(SEQS):
                    last = mm(bank[5][:, b * C:(b + 1) * C], sqn[:, b, 1, :], qkv[:, b, 2 * C:3 * C], start=True, stop=True)
                last.then_inc(a0_kv_ps.sem, 1)
                pe.wait_ge(a0_sq4k.sem, a0_sq4k.at(it, 1))
                for b in range(SEQS):
                    last = mm(bank[4][:, b:b + 1], sq4[:, b, 1, :], one, start=True, stop=True)
                last.then_inc(a0_kn_ps.sem, 1)
                pe.wait_ge(a0_q2.sem, a0_q2.at(it, 1))
                for b in range(SEQS):
                    last = nc.tensor.transpose(bank[6][:, b * N:(b + 1) * N], q2[:, b, :], ident)
                last.then_inc(a0_q2T_ps.sem, 1)
                mm(bank[0][:], W("A0_qkv")[:, 2 * C:3 * C], xT[:], start=True, stop=False)
                pe.wait_ge(a0_kv.sem, a0_kv.at(it, 1))
                pe.wait_ge(a0_q2T.sem, a0_q2T.at(it, 1))
                for b in range(SEQS):
                    last = mm(bank[0][:, b * N:(b + 1) * N], kv[:, b, :], q2T[:, b * N:(b + 1) * N], start=False, stop=b == SEQS - 1)
                last.then_inc(a0_u_ps.sem, 1)
                pe.wait_ge(a0_u.sem, a0_u.at(it, 1))
                for b in range(SEQS):
                    last = mm(Y[:, b * C:(b + 1) * C], uT[:, b * N:(b + 1) * N], W("A0_out"), start=True, stop=True)
                last.then_inc(a0_y.sem, 1)

            def attention(s, t, it):
                kv_hi, kv_lo, kv_f = (cT_hi, cT_lo, cT) if s.cross else (xT_hi, xT_lo, xT)
                rows = CTX if s.cross else C
                name = s.name.upper()
                pe.wait_ge(t.hi.sem, t.hi.at(it, 1))
                pe.wait_ge(t.lo.sem, t.lo.at(it, 1))
                split_matmul(bank[0][:], name + "_q", 0, 128, xT_hi, xT_lo).then_inc(s.q_ps.sem, 1)
                if s.name == "x0":
                    pe.wait_ge(cT_l.sem, cT_l.at(it, 1))
                split_matmul(bank[1][:], name + "_k", 0, 128, kv_hi, kv_lo, rows).then_inc(s.k_ps.sem, 1)
                pe.wait_ge(t.f.sem, t.f.at(it, 1))
                for b in range(SEQS):
                    last = mm(bank[2][:, b * C:(b + 1) * C], kv_f[:, b * N:(b + 1) * N], W(name + "_v", rows), start=True, stop=True)
                last.then_inc(s.v_ps.sem, 1)

                def scores(b):
                    pe.wait_ge(s.k_diag.sem, s.k_diag.at(it, b + 1))
                    for g in range(NG):
                        u = b * NG + g
                        if u >= 2:
                            pe.wait_ge(s.max.sem, s.max.at(it, u - 1))
                        p = bank[u % 2]
                        if s.windowed:
                            mm(p[:], masks[:, 2 * NG * N:], masks[:, 0:NG * N], start=True, stop=False)
                        mm(p[:], q_stack[:, g, b * N:(b + 1) * N], k_diag[:, b % 2, g].rearrange("p j n -> p (j n)"),
                           start=not s.windowed, stop=True).then_inc(s.s_ps.sem, 1)

                def transpose_max(b):
                    pe.wait_ge(s.max.sem, s.max.at(it, NG * (b + 1)))
                    if b >= 1:
                        pe.wait_ge(s.m_sb.sem, s.m_sb.at(it, b))
                    nc.tensor.transpose(bank[6][0:H, 0:N], row_max[:, b % 2, :], ident).then_inc(s.m_ps.sem, 1)

                def scores_T(b):
                    pe.wait_ge(s.q_diag.sem, s.q_diag.at(it, b + 1))
                    for g in range(NG):
                        u = b * NG + g
                        if u == 0:
                            pe.wait_ge(s.v_sb.sem, s.v_sb.at(it, 1))
                        if u >= 2:
                            pe.wait_ge(s.exp.sem, s.exp.at(it, u - 1))
                        p = bank[2 + u % 2]
                        if s.windowed:
                            mm(p[:], masks[:, 2 * NG * N:], masks[:, NG * N:2 * NG * N], start=True, stop=False)
                        mm(p[:], k_stack[:, g, b * N:(b + 1) * N], q_diag[:, b % 2, g].rearrange("p j n -> p (j n)"),
                           start=not s.windowed, stop=True).then_inc(s.t_ps.sem, 1)

                def probs_v(b):
                    pe.wait_ge(s.exp.sem, s.exp.at(it, NG * (b + 1)))
                    if b >= 1:
                        pe.wait_ge(s.att.sem, s.att.at(it, b))
                    a = CONST["sum"][0]
                    for j in range(NJ):
                        for g in range(NG):
                            mm(bank[5][SLOT * g:SLOT * (g + 1), 0:N], const[:, a + SLOT * j:a + SLOT * (j + 1)], probs[:, b % 2, g, j, :],
                               start=j == 0, stop=j == NJ - 1, skip_group_check=True)
                    for j in range(NJ):
                        for g in range(NG):
                            last = mm(bank[4][SLOT * g:SLOT * (g + 1), 0:N], v_pad[:, b, 4 * j + g, :], probs[:, b % 2, g, j, :],
                                      start=j == 0, stop=j == NJ - 1, skip_group_check=True)
                    last.then_inc(s.pv.sem, 1)

                def project(b):
                    pe.wait_ge(s.att.sem, s.att.at(it, b + 1))
                    last = mm(Y[:, b * C:(b + 1) * C], attT[:, b % 2, :], W(name + "_o"), start=True, stop=True)
                    if b == SEQS - 1:
                        last.then_inc(s.y.sem, 1)

                for step in range(SEQS + 4):
                    if step < SEQS:
                        scores(step)
                    if 0 <= step - 4:
                        project(step - 4)
                    if 0 <= step - 2 < SEQS:
                        scores_T(step - 2)
                    if 0 <= step - 3 < SEQS:
                        probs_v(step - 3)
                    if step < SEQS:
                        transpose_max(step)

            def swiglu(s, t, it):
                name = s.name.upper()
                pe.wait_ge(t.f.sem, t.f.at(it, 1))
                for b in range(SEQS):
                    last = mm(bank[6][:, b * 8:(b + 1) * 8], xT[:, b * N:(b + 1) * N], W(name + "_router"), start=True, stop=True)
                last.then_inc(s.r_ps.sem, 1)
                pe.wait_ge(t.hi.sem, t.hi.at(it, 1))
                pe.wait_ge(t.lo.sem, t.lo.at(it, 1))
                state = {"u": 0, "e": 0}

                def up(r):
                    for c0, n in s.rounds[r][0]:
                        u = state["u"]
                        wg, wu = (f"F0_gate{r}", f"F0_up{r}") if name == "F0" else ("F1_gate", "F1_up")
                        if u >= 2:
                            pe.wait_ge(s.act.sem, s.act.at(it, u - 1))
                        split_matmul(bank[u % 2][0:n, :], wg, c0, n, xT_hi, xT_lo)
                        if u >= 2:
                            pe.wait_ge(s.hid.sem, s.hid.at(it, u - 1))
                        split_matmul(bank[2 + u % 2][0:n, :], wu, c0, n, xT_hi, xT_lo).then_inc(s.up.sem, 1)
                        state["u"] += 1

                def down(r):
                    done = sum(len(c) for c, _ in s.rounds[:r + 1])
                    pe.wait_ge(s.hid.sem, s.hid.at(it, done))
                    for e, pieces in s.rounds[r][1]:
                        k = state["e"]
                        if k >= 2:
                            pe.wait_ge(s.comb.sem, s.comb.at(it, k - 1))
                        wd = W(f"F0_down{r}" if name == "F0" else "F1_down")
                        for b in range(SEQS):
                            for i, (slot, r0, n, col) in enumerate(pieces):
                                last = mm(bank[4 + k % 2][:, b * C:(b + 1) * C], hidden[r0:r0 + n, r % 2, slot, b * N:(b + 1) * N],
                                          wd[r0:r0 + n, col:col + C], start=i == 0, stop=i == len(pieces) - 1)
                        last.then_inc(s.down.sem, 1)
                        state["e"] += 1

                for r in range(len(s.rounds) + 1):
                    if r < len(s.rounds):
                        up(r)
                    if r >= 1:
                        down(r - 1)

            pe.wait_ge(ld_const.sem, 48)
            pe.wait_ge(centred.sem, 1)
            pe.wait_ge(st_lo.sem, n_stages)
            pe.wait_ge(fills.sem, 1)
            with pe.Fori(0, GROUPS) as it:
                pe.wait_ge(x_loaded.sem, x_loaded.at(it, 16))
                transpose_x(TR["a0"], x_in)
                pe.wait_ge(c_loaded.sem, c_loaded.at(it, 16))
                for b in range(SEQS):
                    last = nc.tensor.transpose(bank[7][0:CTX, b * N:(b + 1) * N], c_in[:, b, :], ident)
                last.then_inc(cT_ps.sem, 1)
                pe.wait_ge(TR["a0"].f.sem, TR["a0"].f.at(it, 1))
                pe.wait_ge(cT_l.sem, cT_l.at(it, 1))
                linear_attention(it)
                for blk, s in (("x0", X0), ("f0", F0), ("a1", A1), ("x1", X1), ("f1", F1)):
                    pe.wait_ge(LN[BEFORE[blk]].x.sem, LN[BEFORE[blk]].x.at(it, 1))
                    transpose_x(TR[blk], x)
                    (swiglu if blk[0] == "f" else attention)(s, TR[blk], it)

        @block.scalar
        def _(sc):
            act_fn = nc.scalar.activation

            def copy_xT(t, it, split):
                sc.wait_ge(t.ps.sem, t.ps.at(it, 1))
                if split:
                    act_fn(xT_hi[:], bank[6][:], ACT.Copy).then_inc(t.hi.sem, 1)
                    sc.wait_ge(t.lo.sem, t.lo.at(it, 1))
                act_fn(xT[:], bank[6][:], ACT.Copy).then_inc(t.f.sem, 1)

            def linear_attention(it):
                for b in range(SEQS):
                    sc.wait_ge(a0_qkv.sem, a0_qkv.at(it, b + 1))
                    for i in range(2):
                        last = act_fn(sq[:, b, i, :], qkv[:, b, i * C:(i + 1) * C], ACT.Square, accum_out=ssum[:, b, i:i + 1])
                last.then_inc(a0_sq.sem, 1)
                sc.wait_ge(a0_sqn.sem, a0_sqn.at(it, 1))
                act_fn(sq4[:, :, 1, :], sqn[:, :, 1, :], ACT.Square).then_inc(a0_sq4k.sem, 1)
                for b in range(SEQS):
                    last = act_fn(sq4[:, b, 0, :], sqn[:, b, 0, :], ACT.Square, accum_out=qn2[:, b:b + 1])
                last.then_inc(a0_sq4q.sem, 1)
                sc.wait_ge(a0_q2T_ps.sem, a0_q2T_ps.at(it, 1))
                act_fn(q2T[:], bank[6][:], ACT.Copy).then_inc(a0_q2T.sem, 1)
                sc.wait_ge(a0_u_ps.sem, a0_u_ps.at(it, 1))
                act_fn(uT[:], bank[0][:], ACT.Identity, bias=K("A0_bv")).then_inc(a0_u.sem, 1)

            def attention(s, it):
                bias_q = K("X0_bq") if s.biased else 0.0
                bias_k = K("X0_bk") if s.biased else 0.0
                sc.wait_ge(s.q_ps.sem, s.q_ps.at(it, 1))
                act_fn(q_hi[:], bank[0][:], ACT.Identity, bias=bias_q).then_inc(s.q_hi.sem, 1)
                sc.wait_ge(s.k_ps.sem, s.k_ps.at(it, 1))
                act_fn(k_hi[:], bank[1][:], ACT.Identity, bias=bias_k).then_inc(s.k_hi.sem, 1)

                def max_out(b):
                    sc.wait_ge(s.m_ps.sem, s.m_ps.at(it, b + 1))
                    if b >= 2:
                        sc.wait_ge(s.m_in[b % 2].sem, s.m_in[b % 2].at(it, 16 * (b // 2)))
                    act_fn(maxT[:, b % 2, :], bank[6][0:H, 0:N], ACT.Copy).then_inc(s.m_sb.sem, 1)

                def diagonal(b):
                    sc.wait_ge(s.m_in[b % 2].sem, s.m_in[b % 2].at(it, 16 * (b // 2 + 1)))
                    if b >= 2:
                        sc.wait_ge(s.t_ps.sem, s.t_ps.at(it, NG * (b - 1)))
                    for j in range(NJ):
                        rows = slice(SLOT * j, SLOT * (j + 1))
                        last = act_fn(q_diag[rows, b % 2, :, j, :], q_stack[rows, :, b * N:(b + 1) * N].bitcast(f32), ACT.Copy)
                    last.then_inc(s.q_diag.sem, 1)

                def exps(b):
                    if b >= 2:
                        sc.wait_ge(s.pv.sem, s.pv.at(it, b - 1))
                    for g in range(NG):
                        u = b * NG + g
                        sc.wait_ge(s.t_ps.sem, s.t_ps.at(it, u + 1))
                        act_fn(probs[:, b % 2, g].rearrange("p j n -> p (j n)"), bank[2 + u % 2][:], ACT.Exp, scale=SCALE).then_inc(s.exp.sem, 1)

                for step in range(SEQS + 2):
                    if 0 <= step - 2 < SEQS:
                        exps(step - 2)
                    if 0 <= step - 1 < SEQS:
                        diagonal(step - 1)
                    if step < SEQS:
                        max_out(step)

            def swiglu(s, it):
                sc.wait_ge(s.r_arg.sem, s.r_arg.at(it, 1))
                act_fn(rt[1][:], rt[0][:], ACT.Exp, scale=-1.0 if s.name == "f0" else 1.0).then_inc(s.r_exp.sem, 1)
                u = 0
                for chunks, _ in s.rounds:
                    for _, n in chunks:
                        sc.wait_ge(s.up.sem, s.up.at(it, u + 1))
                        if u >= 2:
                            sc.wait_ge(s.hid.sem, s.hid.at(it, u - 1))
                        act_fn(act[0:n, u % 2, :], bank[u % 2][0:n, :], ACT.Silu).then_inc(s.act.sem, 1)
                        u += 1

            sc.wait_ge(ld_const.sem, 48)
            with sc.Fori(0, GROUPS) as it:
                copy_xT(TR["a0"], it, False)
                sc.wait_ge(cT_ps.sem, cT_ps.at(it, 1))
                act_fn(cT_hi[:], bank[7][0:CTX, :], ACT.Copy).then_inc(cT_h.sem, 1)
                sc.wait_ge(cT_l.sem, cT_l.at(it, 1))
                act_fn(cT[:], bank[7][0:CTX, :], ACT.Copy).then_inc(cT_f.sem, 1)
                linear_attention(it)
                copy_xT(TR["x0"], it, True)
                attention(X0, it)
                copy_xT(TR["f0"], it, True)
                swiglu(F0, it)
                copy_xT(TR["a1"], it, True)
                attention(A1, it)
                copy_xT(TR["x1"], it, True)
                attention(X1, it)
                copy_xT(TR["f1"], it, True)
                swiglu(F1, it)

        @block.gpsimd
        def _(po):
            po.memset(zero_row[:], 0.0)
            po.memset(v_pad[:], 0.0)
            po.memset(q_stack[:].bitcast(f32), 0.0)
            po.memset(k_stack[:].bitcast(f32), -1.0)
            po.memset(q_diag[:].bitcast(f32), 0.0)
            po.memset(k_diag[:].bitcast(f32), 0.0)
            po.memset(half[:], -0.5)
            po.memset(coef[:], 1.0).then_inc(fills.sem, 1)

            def rstd_of(l, it):
                po.wait_ge(l.stats.sem, l.stats.at(it, 1))
                po.tensor_tensor(rstd[:], var[:], half[:, 0:SEQS], ALU.pow).then_inc(l.rstd.sem, 1)

            def with_bias(done, src, name, it):
                bias = K(name).unsqueeze(1).to_broadcast((128, SEQS, C))
                po.tensor_tensor(xb[:], src[:], bias, ALU.add).then_inc(done.sem, 1)

            po.wait_ge(ld_const.sem, 48)
            with po.Fori(0, GROUPS) as it:
                po.wait_ge(x_loaded.sem, x_loaded.at(it, 16))
                with_bias(a0_xb, x_in, "A0_bout", it)
                po.wait_ge(a0_qn.sem, a0_qn.at(it, 1))
                po.tensor_tensor(qr[:], qn2c[:], half[:, 0:SEQS], ALU.pow).then_inc(a0_qr.sem, 1)
                po.wait_ge(a0_kn.sem, a0_kn.at(it, 1))
                po.tensor_tensor(kr[:], kn2c[:], half[:, 0:SEQS], ALU.pow).then_inc(a0_kr.sem, 1)
                rstd_of(LN["a0"], it)
                po.wait_ge(LN["a0"].x.sem, LN["a0"].x.at(it, 1))
                with_bias(x0_xb, x, "X0_bo", it)
                for n in ("x0", "f0", "a1", "x1", "f1"):
                    rstd_of(LN[n], it)

        @block.vector
        def _(dv):
            tt, ts, stt = nc.vector.tensor_tensor, nc.vector.tensor_scalar, nc.vector.scalar_tensor_tensor
            steps = [0]

            def then(ins, it):
                steps[0] += 1
                ins.then_inc(dve_step.sem, 1)
                dv.wait_ge(dve_step.sem, dve_step.at(it, steps[0]))

            def layernorm(l, it, to=x):
                for b in range(SEQS):
                    last = nc.vector.bn_stats(bn[:, b, :], z[:, b, :])
                then(last, it)
                nc.vector.memset(wsum[:, 3:4], 0.0)
                for b in range(SEQS):
                    last = nc.vector.bn_aggr(mv[:, b, :], bn[:, b, :])
                then(last, it)
                ts(var[:], mv[:, :, 1], EPS_LN, None, ALU.add).then_inc(l.stats.sem, 1)
                dv.wait_ge(l.rstd.sem, l.rstd.at(it, 1))
                for b in range(SEQS):
                    last = ts(to[:, b, :], z[:, b, :], mv[:, b, 0:1], rstd[:, b:b + 1], ALU.subtract, ALU.mult)
                last.then_inc(l.x.sem, 1)

            def split_xT(t, it):
                dv.wait_ge(t.hi.sem, t.hi.at(it, 1))
                tt(xT_lo[:], bank[6][:], xT_hi[:].bitcast(f32), ALU.subtract).then_inc(t.lo.sem, 1)

            def flat(a):
                return a[:].rearrange("p b c -> p (b c)")

            def linear_attention(it):
                bias = K("A0_bqkv")
                for b in range(SEQS):
                    dv.wait_ge(a0_ps.sem, a0_ps.at(it, b + 1))
                    tt(qkv[:, b, :], bank[b][:, 0:3 * C], bias, ALU.add).then_inc(a0_qkv.sem, 1)
                dv.wait_ge(a0_sq.sem, a0_sq.at(it, 1))
                then(ts(rsum[:], ssum[:], EPS_SUM, None, ALU.add), it)
                then(nc.vector.reciprocal(rsum[:], rsum[:]), it)
                tt(sqn.rearrange("p b i c -> p (b i) c"), sq.rearrange("p b i c -> p (b i) c"),
                   rsum[:].rearrange("p b i -> p (b i)").unsqueeze(2).to_broadcast((128, SEQS * 2, C)), ALU.mult).then_inc(a0_sqn.sem, 1)
                dv.wait_ge(a0_sq4q.sem, a0_sq4q.at(it, 1))
                ts(qn2c[:], qn2[:], EPS_NORM2, None, ALU.max).then_inc(a0_qn.sem, 1)
                dv.wait_ge(a0_kn_ps.sem, a0_kn_ps.at(it, 1))
                ts(kn2c[:], bank[4][:, 0:SEQS], EPS_NORM2, None, ALU.max).then_inc(a0_kn.sem, 1)
                dv.wait_ge(a0_qr.sem, a0_qr.at(it, 1))
                tt(q2[:], sqn[:, :, 0, :], qr[:].unsqueeze(2).to_broadcast((128, SEQS, C)), ALU.mult).then_inc(a0_q2.sem, 1)
                dv.wait_ge(a0_kr.sem, a0_kr.at(it, 1))
                dv.wait_ge(a0_kv_ps.sem, a0_kv_ps.at(it, 1))
                for b in range(SEQS):
                    last = ts(kv[:, b, :], bank[5][:, b * C:(b + 1) * C], kr[:, b:b + 1], float(N) ** -0.5, ALU.mult, ALU.mult)
                last.then_inc(a0_kv.sem, 1)
                dv.wait_ge(a0_xb.sem, a0_xb.at(it, 1))
                dv.wait_ge(a0_y.sem, a0_y.at(it, 1))
                then(tt(flat(z), Y[:], flat(xb), ALU.add), it)

            def attention(s, it):
                dv.wait_ge(s.q_hi.sem, s.q_hi.at(it, 1))
                bq = K("X0_bq") if s.biased else 0.0
                bk = K("X0_bk") if s.biased else 0.0
                stt(q_lo[:], bank[0][:], bq, q_hi[:].bitcast(f32), ALU.add, ALU.subtract).then_inc(s.q_lo.sem, 1)
                dv.wait_ge(s.k_hi.sem, s.k_hi.at(it, 1))
                stt(k_lo[:], bank[1][:], bk, k_hi[:].bitcast(f32), ALU.add, ALU.subtract).then_inc(s.k_lo.sem, 1)
                dv.wait_ge(s.v_ps.sem, s.v_ps.at(it, 1))
                for j in range(NJ):
                    to = v_pad[:, :, NG * j:NG * (j + 1), D * j:D * (j + 1)]
                    src = bank[2][:].rearrange("p (b j g d) -> p b j g d", b=SEQS, j=NJ, g=NG)[:, :, j]
                    if s.biased:
                        bv = K("X0_bv").rearrange("p (j g d) -> p j g d", j=NJ, g=NG)[:, j].unsqueeze(1)
                        last = tt(to, src, bv.to_broadcast((128, SEQS, NG, D)), ALU.add)
                    else:
                        last = nc.vector.tensor_copy(to, src)
                last.then_inc(s.v_sb.sem, 1)
                dv.wait_ge(s.stacked.sem, s.stacked.at(it, 7 * 16))

                def diagonal(b):
                    if b >= 2:
                        dv.wait_ge(s.s_ps.sem, s.s_ps.at(it, NG * (b - 1)))
                    for j in range(NJ):
                        rows = slice(SLOT * j, SLOT * (j + 1))
                        last = nc.vector.tensor_copy(k_diag[rows, b % 2, :, j, :], k_stack[rows, :, b * N:(b + 1) * N].bitcast(f32))
                    last.then_inc(s.k_diag.sem, 1)

                def maxima(b):
                    if b >= 2:
                        dv.wait_ge(s.m_ps.sem, s.m_ps.at(it, b - 1))
                    for g in range(NG):
                        u = b * NG + g
                        dv.wait_ge(s.s_ps.sem, s.s_ps.at(it, u + 1))
                        nc.vector.tensor_reduce(row_max[:, b % 2, g::NG],
                                                bank[u % 2][:].rearrange("p (j k) -> p j k", j=NJ), AX, ALU.max).then_inc(s.max.sem, 1)

                def normalise(b):
                    dv.wait_ge(s.pv.sem, s.pv.at(it, b + 1))
                    nc.vector.reciprocal(rden[:, b % 2, :], bank[5][:, 0:N]).then_inc(s.rden.sem, 1)
                    dv.wait_ge(s.rden.sem, s.rden.at(it, b + 1))
                    tt(attT[:, b % 2, :], bank[4][:, 0:N], rden[:, b % 2, :], ALU.mult).then_inc(s.att.sem, 1)

                diagonal(0)
                diagonal(1)
                for step in range(SEQS + 3):
                    if step < SEQS:
                        maxima(step)
                    if 2 <= step + 2 < SEQS:
                        diagonal(step + 2)
                    if 0 <= step - 3:
                        normalise(step - 3)
                if s.biased:
                    dv.wait_ge(x0_xb.sem, x0_xb.at(it, 1))
                dv.wait_ge(s.y.sem, s.y.at(it, 1))
                then(tt(flat(z), Y[:], flat(xb if s.biased else x), ALU.add), it)

            def first_of_max(p, n, mx, onehot, it):
                first = K("first")[:, 0:n].unsqueeze(1).to_broadcast((128, SEQS, n))
                then(nc.vector.tensor_reduce(mx[:], p, AX, ALU.max), it)
                then(tt(onehot, p, mx[:].unsqueeze(2).to_broadcast((128, SEQS, n)), ALU.is_equal), it)
                then(tt(onehot, onehot, first, ALU.mult), it)
                then(nc.vector.tensor_reduce(rs[3][:], onehot, AX, ALU.max), it)
                then(tt(onehot, rs[3][:].unsqueeze(2).to_broadcast((128, SEQS, n)), first, ALU.is_equal), it)

            def route0(s, it):
                n = E0
                logits, p, oh = rt[0][:], rt[2][:, :, 0:n], rt[3][:, :, 0:n]
                dv.wait_ge(s.r_ps.sem, s.r_ps.at(it, 1))
                then(tt(logits, bank[6][:, 0:SEQS * 8].rearrange("p (b e) -> p b e", e=8),
                        K("F0_brouter").unsqueeze(1).to_broadcast((128, SEQS, 8)), ALU.add), it)
                ts(logits, logits, -50.0, 50.0, ALU.max, ALU.min).then_inc(s.r_arg.sem, 1)
                dv.wait_ge(s.r_exp.sem, s.r_exp.at(it, 1))
                then(ts(rt[2][:], rt[1][:], 1.0, None, ALU.add), it)
                then(nc.vector.reciprocal(rt[2][:], rt[2][:]), it)
                first_of_max(p, n, rs[0], oh, it)
                then(ts(rs[0][:], rs[0][:], 1e-8, 1.0 - 1e-8, ALU.max, ALU.min), it)
                then(ts(rs[1][:], rs[0][:], 0.5, 1e-8, ALU.add, ALU.add), it)
                then(ts(rs[1][:], rs[1][:], 0.5, 2.0, ALU.max, ALU.min), it)
                then(nc.vector.reciprocal(rs[1][:], rs[1][:]), it)
                ts(coef[:, :, 0], rs[1][:], 0.5, None, ALU.mult)
                then(tt(rs[2][:], rs[0][:], rs[1][:], ALU.mult), it)
                then(tt(coef[:, :, 1:1 + n], oh, rs[2][:].unsqueeze(2).to_broadcast((128, SEQS, n)), ALU.mult), it)

            def route1(s, it):
                n = E1
                logits, p, oh1, oh2, p2 = rt[0][:], rt[2][:], rt[3][:], rt[4][:], rt[5][:]
                dv.wait_ge(s.r_ps.sem, s.r_ps.at(it, 1))
                ps = bank[6][:, 0:SEQS * 8].rearrange("p (b e) -> p b e", e=8)
                then(nc.vector.tensor_reduce(rs[0][:], ps, AX, ALU.max), it)
                tt(logits, ps, rs[0][:].unsqueeze(2).to_broadcast((128, SEQS, n)), ALU.subtract).then_inc(s.r_arg.sem, 1)
                dv.wait_ge(s.r_exp.sem, s.r_exp.at(it, 1))
                then(nc.vector.tensor_reduce(rs[1][:], rt[1][:], AX, ALU.add), it)
                then(nc.vector.reciprocal(rs[1][:], rs[1][:]), it)
                then(tt(p, rt[1][:], rs[1][:].unsqueeze(2).to_broadcast((128, SEQS, n)), ALU.mult), it)
                first_of_max(p, n, rs[0], oh1, it)
                then(stt(p2, oh1, -2.0, p, ALU.mult, ALU.add), it)
                first_of_max(p2, n, rs[0], oh2, it)
                then(tt(oh1, oh1, oh2, ALU.add), it)
                nc.vector.memset(coef[:, :, 0], 1.0)
                then(tt(coef[:, :, 1:1 + n], oh1, p, ALU.mult), it)

            def swiglu(s, it):
                (route0 if s.name == "f0" else route1)(s, it)
                u = e = 0
                for r in range(len(s.rounds) + 1):
                    if r < len(s.rounds):
                        for slot, (_, n) in enumerate(s.rounds[r][0]):
                            dv.wait_ge(s.act.sem, s.act.at(it, u + 1))
                            if r >= 2:
                                dv.wait_ge(s.down.sem, s.down.at(it, sum(len(x[1]) for x in s.rounds[:r - 1])))
                            tt(hidden[0:n, r % 2, slot, :], bank[2 + u % 2][0:n, :], act[0:n, u % 2, :], ALU.mult).then_inc(s.hid.sem, 1)
                            u += 1
                    if r >= 1:
                        for _ in s.rounds[r - 1][1]:
                            dv.wait_ge(s.down.sem, s.down.at(it, e + 1))
                            if e:
                                dv.wait_ge(s.comb.sem, s.comb.at(it, e))
                            for b in range(SEQS):
                                last = stt(z[:, b, :], bank[4 + e % 2][:, b * C:(b + 1) * C], coef[:, b, e:e + 1],
                                           (z if e else x)[:, b, :], ALU.mult, ALU.add)
                            last.then_inc(s.comb.sem, 1)
                            e += 1
                dv.wait_ge(s.comb.sem, s.comb.at(it, s.experts))

            for n in range(n_stages):
                dv.wait_ge(ld_stage[n % 2].sem, 16 * (n // 2 + 1))
                cols = slice(n * STAGE, (n + 1) * STAGE)
                nc.vector.tensor_copy(w_hi[:, cols], stage[:, n % 2, :]).then_inc(st_hi.sem, 1)
                dv.wait_ge(st_hi.sem, n + 1)
                tt(w_lo[:, cols], stage[:, n % 2, :], w_hi[:, cols].bitcast(f32), ALU.subtract).then_inc(st_lo.sem, 1)
            dv.wait_ge(ld_const.sem, 48)
            for i, m in enumerate((W("A0_qkv"), K("A0_bqkv"))):
                for j in range(2):
                    part = m[:, j * C:(j + 1) * C]
                    nc.vector.tensor_reduce(wsum[:, 0:1], part, AX, ALU.add).then_inc(centred_step.sem, 1)
                    dv.wait_ge(centred_step.sem, 3 * (2 * i + j) + 1)
                    ts(wsum[:, 1:2], wsum[:, 0:1], 1.0 / C, None, ALU.mult).then_inc(centred_step.sem, 1)
                    dv.wait_ge(centred_step.sem, 3 * (2 * i + j) + 2)
                    last = ts(part, part, wsum[:, 1:2], None, ALU.subtract)
                    last.then_inc(centred_step.sem, 1)
                    dv.wait_ge(centred_step.sem, 3 * (2 * i + j) + 3)
            nc.vector.memset(wsum[:, 2:3], 0.0).then_inc(centred.sem, 1)
            dv.wait_ge(fills.sem, 1)

            with dv.Fori(0, GROUPS) as it:
                dv.wait_ge(cT_h.sem, cT_h.at(it, 1))
                tt(cT_lo[:], bank[7][0:CTX, :], cT_hi[:].bitcast(f32), ALU.subtract).then_inc(cT_l.sem, 1)
                linear_attention(it)
                layernorm(LN["a0"], it)
                split_xT(TR["x0"], it)
                attention(X0, it)
                layernorm(LN["x0"], it)
                split_xT(TR["f0"], it)
                swiglu(F0, it)
                layernorm(LN["f0"], it)
                split_xT(TR["a1"], it)
                attention(A1, it)
                layernorm(LN["a1"], it)
                split_xT(TR["x1"], it)
                attention(X1, it)
                layernorm(LN["x1"], it)
                split_xT(TR["f1"], it)
                swiglu(F1, it)
                layernorm(LN["f1"], it, y_out)
            assert steps[0] == DVE_STEPS, steps[0]


def _packed(parts, table, cols, rows=128):
    out = np.zeros((rows, cols), np.float32)
    for name, a in parts.items():
        c0, _ = table[name]
        out[:a.shape[0], c0:c0 + a.shape[1]] = a
    return out


def _slots(w):
    return w.reshape(w.shape[0], NJ, NG, D).transpose(0, 1, 3, 2).reshape(w.shape[0], C)


def _out_rows(w):
    return w.reshape(NJ, NG, D, C).transpose(1, 0, 2, 3).reshape(C, C)


def _chunk_rows(w):
    out = np.zeros((128, 3 * C), w.dtype)
    for i, (r0, n) in enumerate(CHUNKS0):
        out[:n, i * C:(i + 1) * C] = w[r0:r0 + n]
    return out


def _rows(v):
    return np.broadcast_to(v[None, :], (128, v.shape[0]))


def _layout(a):
    split = {
        "X0_q": _slots(a["L0_xattn_Wq"]), "X0_k": _slots(a["L0_xattn_Wk"]),
        "A1_q": _slots(a["L1_attn_Wq"]), "A1_k": _slots(a["L1_attn_Wk"]),
        "X1_q": _slots(a["L1_xattn_Wq"]), "X1_k": _slots(a["L1_xattn_Wk"]),
        "F0_gate0": a["L0_ffn_sw1"].T, "F0_up0": a["L0_ffn_sw3"].T,
        "F1_gate": np.concatenate([a["L1_ffn_shared_gate"], *a["L1_ffn_experts_gate"]], 1),
        "F1_up": np.concatenate([a["L1_ffn_shared_up"], *a["L1_ffn_experts_up"]], 1)}
    plain = {
        "A0_qkv": a["L0_attn_Wqkv"], "A0_out": a["L0_attn_Wln"],
        "X0_v": a["L0_xattn_Wv"], "X0_o": _out_rows(a["L0_xattn_Wo"]),
        "A1_v": a["L1_attn_Wv"], "A1_o": _out_rows(a["L1_attn_Wo"]),
        "X1_v": a["L1_xattn_Wv"], "X1_o": _out_rows(a["L1_xattn_Wo"]),
        "F0_router": a["L0_ffn_router_w"].T, "F1_router": a["L1_ffn_router"],
        "F0_down0": _chunk_rows(a["L0_ffn_sw2"].T),
        "F1_down": np.concatenate([a["L1_ffn_shared_down"], *a["L1_ffn_experts_down"].reshape(E1 // 2, 128, C)], 1)}
    for e in range(E0):
        split[f"F0_gate{e + 1}"] = a["L0_ffn_ew1"][e].T
        split[f"F0_up{e + 1}"] = a["L0_ffn_ew3"][e].T
        plain[f"F0_down{e + 1}"] = _chunk_rows(a["L0_ffn_ew2"][e].T)
    sums = np.zeros((128, NJ, SLOT), np.float32)
    for j in range(NJ):
        sums[:, j, D * j:D * (j + 1)] = 1
    bqkv = a["L0_attn_bqkv"]
    const = {
        "ident": np.eye(128, dtype=np.float32), "sum": sums.reshape(128, -1),
        "first": _rows(np.arange(8, 0, -1).astype(np.float32)),
        "A0_bqkv": _rows(bqkv), "A0_bout": _rows(a["L0_attn_bln"]), "X0_bv": _rows(a["L0_xattn_bv"]),
        "X0_bo": _rows(a["L0_xattn_bo"]), "F0_brouter": _rows(a["L0_ffn_routing_bias"]),
        "X0_bq": _slots(a["L0_xattn_bq"][None]).T, "X0_bk": _slots(a["L0_xattn_bk"][None]).T,
        "A0_bv": bqkv[2 * C:, None], "one": np.ones((128, 1), np.float32)}
    query, key = np.arange(N)[:, None], np.arange(N)[None, :]
    seen = (query - key >= 0) & (query - key < WIN)
    mask = np.where(seen, 0.0, MASKED)
    masks = np.concatenate([np.tile(mask, (1, NG)), np.tile(mask.T, (1, NG)), np.eye(N)], 1)
    return (_packed(split, SPLIT, SPLIT_COLS), _packed(plain, PLAIN, PLAIN_COLS),
            _packed(const, CONST, CONST_COLS), masks)


def kernel(**inputs):
    import numpy as _np
    import concourse.bacc as _bacc
    from concourse import mybir as _mybir
    from concourse.bass_utils import run_bass_kernel_spmd as _run

    a = {k: _np.asarray(v) for k, v in inputs.items()}
    split, plain, const, masks = _layout(a)
    bf16 = _mybir.dt.np(_mybir.dt.bfloat16)
    arrays = {"x": _np.ascontiguousarray(a["x"]), "ctx": _np.ascontiguousarray(a["ctx_768"]), "split": split, "plain": plain,
              "const": const, "masks": masks.astype(bf16)}
    nc = _bacc.Bacc("TRN2", target_bir_lowering=False, num_devices=1)
    args = [nc.dram_tensor(f"in_{n}", v.shape, _mybir.dt.from_np(v.dtype), kind="ExternalInput").ap() for n, v in arrays.items()]
    out = nc.dram_tensor("out_x", (B, N, C), _mybir.dt.float32, kind="ExternalOutput").ap()
    decoder_kernel(nc, *args, out)
    r = _run(nc, [{f"in_{n}": v for n, v in arrays.items()}], core_ids=[0])
    return r.results[0]["out_x"]
```

```python
from contextlib import ExitStack

import numpy as np

import concourse.bass as bass
from concourse import mybir

B, N, C, CTX = 32, 128, 128, 96
SEQS = 4
GROUPS = B // SEQS
T = SEQS * N
H, D = 16, 8
NJ, NG = 4, 4
WIN = 64
E0, I0 = 7, 352
E1, I1, S1 = 8, 64, 128
SCALE = D ** -0.5
EPS_LN = 1e-5
EPS_SUM = 1e-7
EPS_NORM2 = 1e-24
MASKED = -1e30
SLOT = 32

CHUNKS0 = [(0, 128), (128, 128), (256, 96)]


def _ranges(parts):
    at, out = 0, {}
    for name, n in parts:
        out[name] = (at, at + n)
        at += n
    return out, at


SPLIT, SPLIT_COLS = _ranges(
    [(f"{a}_{w}", 128) for a in ("X0", "A1", "X1") for w in ("q", "k")]
    + [(f"F0_{w}{e}", I0) for e in range(E0 + 1) for w in ("gate", "up")]
    + [("F1_gate", S1 + E1 * I1), ("F1_up", S1 + E1 * I1)])
PLAIN, PLAIN_COLS = _ranges(
    [("A0_qkv", 3 * C), ("A0_out", C)]
    + [(f"{a}_{w}", C) for a in ("X0", "A1", "X1") for w in ("v", "o")]
    + [("F0_router", 8), ("F1_router", 8)]
    + [(f"F0_down{e}", 3 * C) for e in range(E0 + 1)]
    + [("F1_down", 5 * C)])
CONST, CONST_COLS = _ranges(
    [("ident", 128), ("sum", NJ * SLOT), ("first", 8),
     ("A0_bqkv", 3 * C), ("A0_bout", C), ("X0_bv", C), ("X0_bo", C), ("F0_brouter", 8),
     ("X0_bq", 1), ("X0_bk", 1), ("A0_bv", 1), ("one", 1)])
MASK_COLS = 2 * NG * N + N

CHUNK_LIST0 = [(f"F0_gate{e}", f"F0_up{e}", c0, n) for e in range(E0 + 1) for c0, n in CHUNKS0]
PIECES0 = [(e, len(CHUNKS0) * e + i, 0, n, f"F0_down{e}", i * C, i == 0, i == len(CHUNKS0) - 1)
           for e in range(E0 + 1) for i, (_, n) in enumerate(CHUNKS0)]
CHUNK_LIST1 = [("F1_gate", "F1_up", 128 * p, 128) for p in range(1 + E1 // 2)]
PIECES1 = [(0, 0, 0, S1, "F1_down", 0, True, True)] + [
    (1 + 2 * p + i, 1 + p, I1 * i, I1, "F1_down", (1 + p) * C, True, True) for p in range(E1 // 2) for i in range(2)]


def _units(chunks, pieces):
    units = [("split",), ("copy",), ("pause",), ("up", 0), ("router",), ("exp",), ("coef",)]
    for u in range(len(chunks)):
        if u + 1 < len(chunks):
            units.append(("up", u + 1))
        downs = [("down", k) for k, p in enumerate(pieces) if p[1] == u]
        units += downs if len(downs) == 1 else [downs[0], ("pause",), downs[1], ("pause",)]
    return units + [("stats",), ("norm",)]


UNITS0, UNITS1 = _units(CHUNK_LIST0, PIECES0), _units(CHUNK_LIST1, PIECES1)

SLOTS = [(0, 0, 1, 1, 1), (1, 0, 0, 0, 0), (0, 1, 1, 0, 0), (1, 1, 0, 1, 0)]
TURNS = GROUPS // 2
AT_NORM, AT_SPLIT, AT_STACKS, AT_SQUARES = 3, 2, 5, 3
MAX_ROW = 3
PO_QUADRANTS = 2
SOFTMAX_PLACES = AT_NORM + AT_SPLIT + AT_STACKS + (SEQS + 3) * NG
PLACES = {0: 10 + AT_SQUARES + AT_NORM + SOFTMAX_PLACES, 1: 2 * SOFTMAX_PLACES}
DVE_STEPS = 90


class Signal:

    def __init__(self, shared, base):
        self.all, self.base = shared, base
        self.sem = shared[0]

    def at(self, it, count, ago=0):
        value = it * self.all[1] + (self.all[2] + self.base + count - ago * self.all[1])
        return value


def decoder_kernel(nc, x_d, ctx_d, split_d, plain_d, const_d, mask_d, out_d):
    f32, f32r, bf16 = mybir.dt.float32, mybir.dt.float32r, mybir.dt.bfloat16
    ALU = mybir.AluOpType
    ACT = mybir.ActivationFunctionType
    AX = mybir.AxisListType.X

    ctx = ExitStack()
    with ctx:
        def sb(name, shape, dt=f32):
            return ctx.enter_context(nc.sbuf_tensor(name, shape, dt))

        shared = {}

        def sig(name, own=1, lead=0):
            if name not in shared:
                shared[name] = [ctx.enter_context(nc.semaphore(name)), 0, lead]
            record = shared[name]
            record[1] += own
            return Signal(record, record[1] - own)

        w_hi = sb("w_hi", [128, SPLIT_COLS], f32r)
        w_lo = sb("w_lo", [128, SPLIT_COLS], f32r)
        plain = sb("plain", [128, PLAIN_COLS])
        const = sb("const", [128, CONST_COLS])
        masks = sb("masks", [128, MASK_COLS], bf16)
        STAGE = 960
        half = sb("half", [128, SEQS])
        wsum = sb("wsum", [128, 6])

        def W(name, rows=128):
            a, b = PLAIN[name]
            return plain[0:rows, a:b]

        def K(name):
            a, b = CONST[name]
            return const[:, a:b]

        ident = K("ident")
        one = K("one")

        x = sb("x", [128, 2, SEQS, C])
        x_in = sb("x_in", [128, SEQS, C])
        c_in = sb("c_in", [128, SEQS, CTX])
        cT = sb("cT", [CTX, T])
        cT_hi = sb("cT_hi", [CTX, T], f32r)
        cT_lo = sb("cT_lo", [CTX, T], f32r)

        class Stream:

            def __init__(s, name, xT):
                s.xT = xT
                s.xT_hi = sb(name + "_xT_hi", [128, T], f32r)
                s.xT_lo = sb(name + "_xT_lo", [128, T], f32r)
                s.bn = sb(name + "_bn", [128, SEQS, 6])
                s.mv = sb(name + "_mv", [128, SEQS, 2])
                s.var = sb(name + "_var", [128, SEQS])
                s.rstd = sb(name + "_rstd", [128, SEQS])

        gate = sb("gate", [128, 2, T])
        hidden = sb("hidden", [128, 2, T])
        att, ffn = Stream("att", sb("att_xT", [128, T])), Stream("ffn", hidden[:, 1])
        big = sb("big", [128, 8 * T])
        q_hi = sb("q_hi", [128, T], f32r)
        q_lo = sb("q_lo", [128, T], f32r)
        k_hi = sb("k_hi", [128, T], f32r)
        k_lo = sb("k_lo", [128, T], f32r)
        q_stack = sb("q_stack", [128, NG, T], f32r)
        k_stack = sb("k_stack", [128, NG, T], f32r)
        q_diag = sb("q_diag", [128, 3, NG, NJ, N], f32r)
        k_diag = sb("k_diag", [128, 2, NG, NJ, N], f32r)
        v_pad = sb("v_pad", [128, SEQS, H, SLOT])
        row_max = sb("row_max", [128, 2, H])
        maxT = q_lo[0:H, 0:2 * N].rearrange("p (i n) -> p i n", i=2)
        stage = big[:, 0:2 * STAGE].rearrange("p (i n) -> p i n", i=2)
        probs = big[:].rearrange("p (i g j n) -> p i g j n", i=2, j=NJ, g=NG)
        rden = att.xT[:, 0:N]
        attT = att.xT[:, N:3 * N].rearrange("p (i n) -> p i n", i=2)
        qkv = big[:, 0:3 * T].rearrange("p (b c) -> p b c", b=SEQS)
        sq = big[:, 3 * T:5 * T].rearrange("p (b i c) -> p b i c", b=SEQS, i=2)
        sqn = big[:, 5 * T:7 * T].rearrange("p (b i c) -> p b i c", b=SEQS, i=2)
        sq4 = sq
        kv = big[:, 7 * T:8 * T].rearrange("p (b c) -> p b c", b=SEQS)
        uT = big[:, 3 * T:4 * T]
        q2 = q_hi[:].bitcast(f32).rearrange("p (b c) -> p b c", b=SEQS)
        q2T = q_lo[:].bitcast(f32)
        ssum = sb("ssum", [128, SEQS, 2])
        rsum = sb("rsum", [128, SEQS, 2])
        qn2 = sb("qn2", [128, SEQS])
        qn2c = sb("qn2c", [128, SEQS])
        qr = sb("qr", [128, SEQS])
        kn2c = sb("kn2c", [128, SEQS])
        kr = sb("kr", [128, SEQS])
        rt = [sb(f"rt{i}", [128, SEQS, 8]) for i in range(6)]
        rs = [sb(f"rs{i}", [128, SEQS]) for i in range(4)]
        coef = sb("coef", [128, SEQS, 9])

        bank = [ctx.enter_context(nc.psum_tensor(f"bank{i}", [128, 512], f32)) for i in range(8)]
        S_BANKS = [bank[0], bank[3]]
        ST_BANK, HEADS, Y, GATE, UP, DOWN = bank[1], bank[2], *bank[4:]
        V_BANK, K_BANK, Q_BANK = bank[0], ST_BANK, HEADS
        num, den = HEADS[:, 0:N], HEADS[:, N:2 * N]

        def score_bank(b, g):
            return S_BANKS[(b * (NG + 1) + g) % 2]

        ld_const = ctx.enter_context(nc.semaphore("ld_const"))
        ld_stage = [ctx.enter_context(nc.semaphore(f"ld_stage{i}")) for i in range(2)]
        st_hi = ctx.enter_context(nc.semaphore("st_hi"))
        st_lo = ctx.enter_context(nc.semaphore("st_lo"))
        fills = ctx.enter_context(nc.semaphore("fills"))
        centred = ctx.enter_context(nc.semaphore("centred"))
        centred_step = ctx.enter_context(nc.semaphore("centred_step"))
        dve_step = sig("dve_step", DVE_STEPS)
        x_free = [sig(f"x_free{i}", 16, 16) for i in range(2)]

        def norm_signals(s, of):
            s.stats = sig(of + "_stats")
            s.rstd = sig(of + "_rstd")
            s.normed = sig(of + "_normed", 1, 1 if of == "att" else 0)

        def split_signals(s, of, whole=True):
            s.xT_ps = sig(of + "_xT_ps")
            s.xT_hi = sig(of + "_xT_hi")
            s.xT_lo = sig(of + "_xT_lo")
            s.xT_f = sig(of + "_xT_f") if whole else None

        class Context:

            def __init__(s):
                s.loaded = sig("c_loaded", 16)
                s.ps, s.hi, s.lo, s.f = sig("cT_ps"), sig("cT_hi"), sig("cT_lo"), sig("cT_f")

        class Linear:

            def __init__(s, g):
                s.g = g
                s.loaded = sig("x_loaded", 16)
                s.xT_ps, s.xT_f = sig("a0_xT_ps"), sig("a0_xT_f")
                s.qkv_ps = sig("a0_qkv_ps", SEQS)
                s.qkv = sig("a0_qkv", SEQS)
                s.sq = sig("a0_sq")
                s.sqn = sig("a0_sqn")
                s.sq4q, s.sq4k = sig("a0_sq4q"), sig("a0_sq4k")
                s.qn, s.qr = sig("a0_qn"), sig("a0_qr")
                s.kn_ps, s.kn, s.kr = sig("a0_kn_ps"), sig("a0_kn"), sig("a0_kr")
                s.q2, s.q2T_ps, s.q2T = sig("a0_q2"), sig("a0_q2T_ps"), sig("a0_q2T")
                s.kv_ps, s.kv = sig("a0_kv_ps"), sig("a0_kv")
                s.u_ps, s.u = sig("a0_u_ps"), sig("a0_u")
                s.xb = sig("a0_xb")
                s.y = sig("a0_y")
                s.added = sig("att_added", 1, 1)
                norm_signals(s, "att")

        class Softmax:

            def __init__(s, name, g, windowed, biased, cross):
                s.g = g
                s.name, s.windowed, s.biased, s.cross = name, windowed, biased, cross
                split_signals(s, "att", not cross)
                s.q_ps, s.k_ps, s.v_ps = sig("att_q_ps"), sig("att_k_ps"), sig("att_v_ps")
                s.q_hi, s.q_lo = sig("att_q_hi"), sig("att_q_lo")
                s.k_hi, s.k_lo = sig("att_k_hi"), sig("att_k_lo")
                s.v_sb = sig("att_v_sb")
                s.q_in = sig("att_q_in", 3 * 16)
                s.k_in = sig("att_k_in", 3 * 16)
                s.k_diag = sig("att_k_diag", SEQS)
                s.k_diag_po = sig("att_k_diag_po", SEQS * PO_QUADRANTS)
                s.q_diag = sig("att_q_diag", SEQS)
                s.s_ps = sig("att_s_ps", SEQS * NG)
                s.max = sig("att_max", SEQS * NG)
                s.m_ps = sig("att_m_ps", SEQS)
                s.m_sb = sig("att_m_sb", SEQS)
                s.m_in = [sig(f"att_m_in{i}", 16 * SEQS // 2) for i in range(2)]
                s.t_ps = sig("att_t_ps", SEQS * NG)
                s.exp = sig("att_exp", SEQS * NG)
                s.pv = sig("att_pv", SEQS)
                s.rden = sig("att_rden", SEQS)
                s.att = sig("att_att", SEQS)
                s.y = sig("att_y")
                s.xb = sig("x0_xb") if biased else None
                s.added = sig("att_added", 1, 1)
                norm_signals(s, "att")

        class Experts:

            def __init__(s, g, layer, ago):
                s.g, s.ago, s.name = g, ago, f"F{layer}"
                s.chunks, s.pieces = (CHUNK_LIST0, PIECES0) if layer == 0 else (CHUNK_LIST1, PIECES1)
                s.units = UNITS0 if layer == 0 else UNITS1
                s.n = 1 + max(p[0] for p in s.pieces)
                split_signals(s, "ffn")
                s.r_ps = sig("ffn_r_ps")
                s.r_arg = sig("ffn_r_arg")
                s.r_exp = sig("ffn_r_exp")
                s.gate_ps = sig("ffn_gate_ps", len(s.chunks))
                s.up_ps = sig("ffn_up_ps", len(s.chunks))
                s.tanh = sig("ffn_tanh", len(s.chunks))
                s.silu = sig("ffn_silu", len(s.chunks))
                s.hid = sig("ffn_hid", len(s.chunks))
                s.down = sig("ffn_down", len(s.pieces))
                s.comb = sig("ffn_comb", s.n)
                norm_signals(s, "ffn")

        class Slot:
            def __init__(s, g, layer, ffn_g, ffn_layer, ago):
                s.g, s.layer = g, layer
                s.c = Context()
                s.first = Linear(g) if layer == 0 else Softmax("A1", g, True, False, False)
                s.second = Softmax(f"X{layer}", g, False, layer == 0, True)
                s.ffn = Experts(ffn_g, ffn_layer, ago)

        slots = [Slot(*s) for s in SLOTS]
        for i, s in enumerate(slots):
            s.before, s.before_ago = slots[i - 1].second, 1 if i == 0 else 0
            s.ffn.input = slots[i - 1].second
            if s.layer == 1:
                s.input = slots[i - 1].ffn

        class Beside:

            def __init__(s, layer, units, emit, lag=0):
                s.places, s.units, s.emit, s.lag, s.at, s.done = PLACES[layer], units, emit, lag, 0, 0

            def __call__(s, places=1):
                s.at += places
                while s.done < len(s.units) * s.at // s.places:
                    if s.done >= s.lag:
                        s.emit(s.units[s.done - s.lag])
                    s.done += 1
                if s.at == s.places and s.lag:
                    s.emit(s.units[-1])

            def end(s):
                assert s.at == s.places, (s.at, s.places)

        block = ctx.enter_context(nc.Block())
        n_stages = SPLIT_COLS // STAGE
        assert n_stages * STAGE == SPLIT_COLS

        @block.sync
        def _(sp):
            def rows(d, first):
                return d[bass.ds(first, SEQS)].rearrange("b n c -> n b c")

            sp.dma_start(const[:], const_d).then_inc(ld_const, 16)
            sp.dma_start(masks[:], mask_d).then_inc(ld_const, 16)
            sp.dma_start(plain[:], plain_d).then_inc(ld_const, 16)
            for n in range(n_stages):
                if n >= 2:
                    sp.wait_ge(st_lo, n - 1)
                sp.dma_start(stage[:, n % 2, :], split_d[:, n * STAGE:(n + 1) * STAGE]).then_inc(ld_stage[n % 2], 16)
            for g in range(2):
                sp.dma_start(x[:, g], rows(x_d, 0)).then_inc(x_free[g].sem, 16)
            sp.dma_start(x_in[:], rows(x_d, 0)).then_inc(slots[0].first.loaded.sem, 16)
            sp.dma_start(c_in[:], rows(ctx_d, 0)).then_inc(slots[0].c.loaded.sem, 16)
            sp.wait_ge(fills, 1)

            def load_context(c, group, it):
                sp.wait_ge(c.ps.sem, c.ps.at(it, 1))
                sp.dma_start(c_in[:], rows(ctx_d, group * SEQS)).then_inc(c.loaded.sem, 16)

            def softmax(s, it, following=None):
                sp.wait_ge(s.k_hi.sem, s.k_hi.at(it, 1))
                sp.dma_start(k_stack[0::4].bitcast(f32), k_hi[:].bitcast(f32)).then_inc(s.k_in.sem, 16)
                sp.dma_start(k_stack[2::4].bitcast(f32), k_hi[:].bitcast(f32)).then_inc(s.k_in.sem, 16)
                sp.wait_ge(s.k_lo.sem, s.k_lo.at(it, 1))
                sp.dma_start(k_stack[1::4].bitcast(f32), k_lo[:].bitcast(f32)).then_inc(s.k_in.sem, 16)
                sp.wait_ge(s.q_hi.sem, s.q_hi.at(it, 1))
                sp.dma_start(q_stack[0::4].bitcast(f32), q_hi[:].bitcast(f32)).then_inc(s.q_in.sem, 16)
                sp.dma_start(q_stack[1::4].bitcast(f32), q_hi[:].bitcast(f32)).then_inc(s.q_in.sem, 16)
                sp.wait_ge(s.q_lo.sem, s.q_lo.at(it, 1))
                sp.dma_start(q_stack[2::4].bitcast(f32), q_lo[:].bitcast(f32)).then_inc(s.q_in.sem, 16)
                if following:
                    load_context(*following)
                for b in range(SEQS):
                    sp.wait_ge(s.q_diag.sem, s.q_diag.at(it, b + 1))
                    sp.wait_ge(s.m_sb.sem, s.m_sb.at(it, b + 1))
                    to = q_diag[MAX_ROW:MAX_ROW + 1, b % 3].rearrange("p g j n -> p (g j) n")
                    sp.dma_start(to.bitcast(f32), maxT[:, b % 2, :].bitcast(f32)).then_inc(s.m_in[b % 2].sem, 16)

            def store(s, group, it):
                sp.wait_ge(s.normed.sem, s.normed.at(it, 1))
                sp.dma_start(rows(out_d, group * SEQS), x[:, s.g]).then_inc(x_free[s.g].sem, 16)

            with sp.Fori(0, TURNS) as it:
                for i, s in enumerate(slots):
                    group = (it * 2 + (1, 0, 1, 2)[i]) % GROUPS
                    if s.layer == 0:
                        load_context(s.c, group, it)
                        sp.wait_ge(s.first.xT_ps.sem, s.first.xT_ps.at(it, 1))
                        sp.wait_ge(s.first.xb.sem, s.first.xb.at(it, 1))
                        group = (it * 2 + 1 + i) % GROUPS
                        sp.dma_start(x_in[:], rows(x_d, group * SEQS)).then_inc(s.first.loaded.sem, 16)
                    else:
                        softmax(s.first, it, (s.c, group, it))
                    softmax(s.second, it)
                    if s.ffn.name == "F1":
                        store(s.ffn, (it * 2 + GROUPS - 1) % GROUPS if i == 0 else it * 2, it)
            store(slots[0].ffn, GROUPS - 1, TURNS)
            sp.wait_ge(x_free[0].sem, 16 * (TURNS + 1))
            sp.wait_ge(x_free[1].sem, 16 * (TURNS + 2))
            sp.wait_ge(slots[0].first.loaded.sem, slots[0].first.loaded.at(TURNS, 16))
            sp.wait_ge(slots[0].c.loaded.sem, slots[0].c.loaded.at(TURNS, 16))

        @block.tensor
        def _(pe):
            mm = nc.tensor.matmul

            def split_matmul(out, wname, c0, n, hi, lo, rows=128):
                a = SPLIT[wname][0] + c0
                wh, wl = w_hi[0:rows, a:a + n], w_lo[0:rows, a:a + n]
                mm(out, wh, lo[:], start=True, stop=False)
                mm(out, wl, hi[:], start=False, stop=False)
                return mm(out, wh, hi[:], start=False, stop=True)

            def transposes(to, src, rows=128):
                for b in range(SEQS):
                    last = nc.tensor.transpose(to[0:rows, b * N:(b + 1) * N], src[:, b, :], ident)
                return last

            def context(s, it):
                pe.wait_ge(s.c.loaded.sem, s.c.loaded.at(it, 16))
                transposes(Y, c_in, CTX).then_inc(s.c.ps.sem, 1)

            def keys(s, it):
                hi, lo, rows = (cT_hi, cT_lo, CTX) if s.cross else (att.xT_hi, att.xT_lo, C)
                split_matmul(K_BANK[:], s.name + "_k", 0, 128, hi, lo, rows).then_inc(s.k_ps.sem, 1)

            def values(s, it):
                src, rows = (cT, CTX) if s.cross else (att.xT, C)
                for b in range(SEQS):
                    last = mm(V_BANK[:, b * C:(b + 1) * C], src[:, b * N:(b + 1) * N], W(s.name + "_v", rows), start=True, stop=True)
                last.then_inc(s.v_ps.sem, 1)

            def linear(s, it, beside, c, following):
                TURNED = bank[3]
                pe.wait_ge(s.loaded.sem, s.loaded.at(it, 16))
                transposes(TURNED, x_in).then_inc(s.xT_ps.sem, 1)
                context(c, it)
                beside()
                pe.wait_ge(s.xT_f.sem, s.xT_f.at(it, 1))
                for b in range(SEQS):
                    if b == 3:
                        pe.wait_ge(s.qkv.sem, s.qkv.at(it, 1))
                    mm(bank[b % 3][:, 0:3 * C], att.xT[:, b * N:(b + 1) * N], W("A0_qkv"), start=True, stop=True).then_inc(s.qkv_ps.sem, 1)
                    beside()
                beside(AT_SQUARES)
                pe.wait_ge(s.sqn.sem, s.sqn.at(it, 1))
                for b in range(SEQS):
                    last = mm(bank[1][:, b * C:(b + 1) * C], sqn[:, b, 1, :], qkv[:, b, 2 * C:3 * C], start=True, stop=True)
                last.then_inc(s.kv_ps.sem, 1)
                beside()
                pe.wait_ge(s.sq4k.sem, s.sq4k.at(it, 1))
                for b in range(SEQS):
                    last = mm(bank[2][:, b:b + 1], sq4[:, b, 1, :], one, start=True, stop=True)
                last.then_inc(s.kn_ps.sem, 1)
                beside()
                pe.wait_ge(s.q2.sem, s.q2.at(it, 1))
                transposes(TURNED, q2).then_inc(s.q2T_ps.sem, 1)
                mm(bank[0][:], W("A0_qkv")[:, 2 * C:3 * C], att.xT[:], start=True, stop=False)
                beside()
                pe.wait_ge(s.kv.sem, s.kv.at(it, 1))
                pe.wait_ge(s.q2T.sem, s.q2T.at(it, 1))
                for b in range(SEQS):
                    last = mm(bank[0][:, b * N:(b + 1) * N], kv[:, b, :], q2T[:, b * N:(b + 1) * N], start=False, stop=b == SEQS - 1)
                last.then_inc(s.u_ps.sem, 1)
                pe.wait_ge(c.c.lo.sem, c.c.lo.at(it, 1))
                keys(following, it)
                beside()
                pe.wait_ge(s.u.sem, s.u.at(it, 1))
                for b in range(SEQS):
                    last = mm(Y[:, b * C:(b + 1) * C], uT[:, b * N:(b + 1) * N], W("A0_out"), start=True, stop=True)
                last.then_inc(s.y.sem, 1)
                values(following, it)
                beside()
                beside(AT_NORM)

            def softmax(s, it, beside, inputs, slot=None, following=None):
                pe.wait_ge(inputs.normed.sem, inputs.normed.at(it, 1))
                transposes(Y, x[:, s.g]).then_inc(s.xT_ps.sem, 1)
                beside(AT_SPLIT)
                pe.wait_ge(s.xT_hi.sem, s.xT_hi.at(it, 1))
                pe.wait_ge(s.xT_lo.sem, s.xT_lo.at(it, 1))
                if not s.cross:
                    keys(s, it)
                split_matmul(Q_BANK[:], s.name + "_q", 0, 128, att.xT_hi, att.xT_lo).then_inc(s.q_ps.sem, 1)
                if not s.cross:
                    pe.wait_ge(s.xT_f.sem, s.xT_f.at(it, 1))
                    values(s, it)
                if following:
                    pe.wait_ge(s.xT_f.sem, s.xT_f.at(it, 1))
                    context(slot, it)
                beside(AT_STACKS)

                def score(b, g):
                    u = b * NG + g
                    if g == 0:
                        pe.wait_ge(s.k_diag.sem, s.k_diag.at(it, b + 1))
                        pe.wait_ge(s.k_diag_po.sem, s.k_diag_po.at(it, PO_QUADRANTS * (b + 1)))
                    if u == 0:
                        pe.wait_ge(s.v_sb.sem, s.v_sb.at(it, 1))
                        pe.wait_ge(s.q_in.sem, s.q_in.at(it, 3 * 16))
                    elif g == 1 and b >= 1:
                        pe.wait_ge(s.m_sb.sem, s.m_sb.at(it, b))
                    elif u >= 2:
                        pe.wait_ge(s.max.sem, s.max.at(it, u if g == 0 else u - 1))
                    to = score_bank(b, g)
                    if s.windowed:
                        mm(to[:], masks[:, 2 * NG * N:], masks[:, 0:NG * N], start=True, stop=False)
                    mm(to[:], q_stack[:, g, b * N:(b + 1) * N], k_diag[:, b % 2, g].rearrange("p j n -> p (j n)"),
                       start=not s.windowed, stop=True).then_inc(s.s_ps.sem, 1)

                def transpose_max(b):
                    pe.wait_ge(s.max.sem, s.max.at(it, NG * (b + 1)))
                    nc.tensor.transpose(score_bank(b, NG)[0:H, 0:N], row_max[:, b % 2, :], ident).then_inc(s.m_ps.sem, 1)

                def score_T(b, g):
                    u = b * NG + g
                    if g == 0:
                        pe.wait_ge(s.m_in[b % 2].sem, s.m_in[b % 2].at(it, 16 * (b // 2 + 1)))
                    if u >= 1:
                        pe.wait_ge(s.exp.sem, s.exp.at(it, u))
                    if s.windowed:
                        mm(ST_BANK[:], masks[:, 2 * NG * N:], masks[:, NG * N:2 * NG * N], start=True, stop=False)
                    mm(ST_BANK[:], k_stack[:, g, b * N:(b + 1) * N], q_diag[:, b % 3, g].rearrange("p j n -> p (j n)"),
                       start=not s.windowed, stop=True).then_inc(s.t_ps.sem, 1)

                def probs_v(b, j):
                    if j == 0:
                        pe.wait_ge(s.exp.sem, s.exp.at(it, NG * (b + 1)))
                        if b >= 1:
                            pe.wait_ge(s.att.sem, s.att.at(it, b))
                    a = CONST["sum"][0]
                    for g in range(NG):
                        mm(den[SLOT * g:SLOT * (g + 1)], const[:, a + SLOT * j:a + SLOT * (j + 1)], probs[:, b % 2, g, j, :],
                           start=j == 0, stop=j == NJ - 1, skip_group_check=True)
                    for g in range(NG):
                        last = mm(num[SLOT * g:SLOT * (g + 1)], v_pad[:, b, 4 * j + g, :], probs[:, b % 2, g, j, :],
                                  start=False, stop=j == NJ - 1, skip_group_check=True)
                    if j == NJ - 1:
                        last.then_inc(s.pv.sem, 1)

                def project(b):
                    pe.wait_ge(s.att.sem, s.att.at(it, b + 1))
                    if b == 0 and following:
                        pe.wait_ge(slot.c.f.sem, slot.c.f.at(it, 1))
                    return mm(Y[:, b * C:(b + 1) * C], attT[:, b % 2, :], W(s.name + "_o"), start=True, stop=True)

                for step in range(SEQS + 3):
                    for g in range(NG):
                        if step < SEQS:
                            score(step, g)
                        if 0 <= step - 2 < SEQS:
                            score_T(step - 2, g)
                        if g == 1 and step >= 4:
                            project(step - 4)
                        if g >= 1 and step >= 3:
                            probs_v(step - 3, g - 1)
                        if g == NG - 1 and step >= 3:
                            probs_v(step - 3, NJ - 1)
                        beside()
                    if step < SEQS:
                        transpose_max(step)
                if following:
                    keys(following, it)
                    values(following, it)
                project(SEQS - 1).then_inc(s.y.sem, 1)
                beside(AT_NORM)

            def experts(s, it, unit):
                kind, *k = unit
                if kind == "split":
                    pe.wait_ge(s.input.normed.sem, s.input.normed.at(it, 1, s.ago))
                    transposes(GATE, x[:, s.g]).then_inc(s.xT_ps.sem, 1)
                elif kind == "router":
                    pe.wait_ge(s.xT_f.sem, s.xT_f.at(it, 1))
                    for b in range(SEQS):
                        last = mm(DOWN[:, b * 8:(b + 1) * 8], ffn.xT[:, b * N:(b + 1) * N], W(s.name + "_router"), start=True, stop=True)
                    last.then_inc(s.r_ps.sem, 1)
                elif kind == "up":
                    u, = k
                    wg, wu, c0, n = s.chunks[u]
                    if u == 0:
                        pe.wait_ge(s.xT_f.sem, s.xT_f.at(it, 1))
                    else:
                        pe.wait_ge(s.silu.sem, s.silu.at(it, u))
                    split_matmul(GATE[0:n, :], wg, c0, n, ffn.xT_hi, ffn.xT_lo).then_inc(s.gate_ps.sem, 1)
                    if u >= 1:
                        pe.wait_ge(s.hid.sem, s.hid.at(it, u))
                    split_matmul(UP[0:n, :], wu, c0, n, ffn.xT_hi, ffn.xT_lo).then_inc(s.up_ps.sem, 1)
                elif kind == "down":
                    e, u, r0, n, wname, col, first, end = s.pieces[k[0]]
                    pe.wait_ge(s.hid.sem, s.hid.at(it, u + 1))
                    if k[0] == 0:
                        pe.wait_ge(s.r_arg.sem, s.r_arg.at(it, 1))
                    if first and e >= 1:
                        pe.wait_ge(s.comb.sem, s.comb.at(it, e))
                    for b in range(SEQS):
                        last = mm(DOWN[:, b * C:(b + 1) * C], hidden[r0:r0 + n, u % 2, b * N:(b + 1) * N],
                                  W(wname)[r0:r0 + n, col:col + C], start=first and b == 0, stop=end, skip_group_check=True)
                    last.then_inc(s.down.sem, 1)

            pe.wait_ge(ld_const, 48)
            pe.wait_ge(centred, 1)
            pe.wait_ge(st_lo, n_stages)
            pe.wait_ge(fills, 1)
            with pe.Fori(0, TURNS) as it:
                for s in slots:
                    beside = Beside(s.layer, s.ffn.units, lambda unit: experts(s.ffn, it, unit))
                    pe.wait_ge(s.before.added.sem, s.before.added.at(it, 1, s.before_ago))
                    if s.layer == 0:
                        linear(s.first, it, beside, s, s.second)
                    else:
                        softmax(s.first, it, beside, s.input, s, s.second)
                    softmax(s.second, it, beside, s.first)
                    beside.end()
            for unit in slots[0].ffn.units:
                experts(slots[0].ffn, TURNS, unit)

        @block.scalar
        def _(sc):
            act_fn = nc.scalar.activation

            def context(s, it):
                sc.wait_ge(s.c.ps.sem, s.c.ps.at(it, 1))
                act_fn(cT_hi[:], Y[0:CTX, :], ACT.Copy).then_inc(s.c.hi.sem, 1)
                sc.wait_ge(s.c.lo.sem, s.c.lo.at(it, 1))
                act_fn(cT[:], Y[0:CTX, :], ACT.Copy).then_inc(s.c.f.sem, 1)

            def keys(s, it):
                sc.wait_ge(s.k_ps.sem, s.k_ps.at(it, 1))
                act_fn(k_hi[:], K_BANK[:], ACT.Identity, bias=K("X0_bk") if s.biased else 0.0).then_inc(s.k_hi.sem, 1)

            def linear(s, it, beside, c, following):
                TURNED = bank[3]
                sc.wait_ge(s.xT_ps.sem, s.xT_ps.at(it, 1))
                act_fn(att.xT[:], TURNED[:], ACT.Copy).then_inc(s.xT_f.sem, 1)
                context(c, it)
                beside()
                for b in range(SEQS):
                    sc.wait_ge(s.qkv.sem, s.qkv.at(it, b + 1))
                    for i in range(2):
                        last = act_fn(sq[:, b, i, :], qkv[:, b, i * C:(i + 1) * C], ACT.Square, accum_out=ssum[:, b, i:i + 1])
                    if b == SEQS - 1:
                        last.then_inc(s.sq.sem, 1)
                    beside()
                beside(AT_SQUARES)
                sc.wait_ge(s.sqn.sem, s.sqn.at(it, 1))
                act_fn(sq4[:, :, 1, :], sqn[:, :, 1, :], ACT.Square).then_inc(s.sq4k.sem, 1)
                for b in range(SEQS):
                    last = act_fn(sq4[:, b, 0, :], sqn[:, b, 0, :], ACT.Square, accum_out=qn2[:, b:b + 1])
                last.then_inc(s.sq4q.sem, 1)
                beside()
                beside()
                sc.wait_ge(s.q2T_ps.sem, s.q2T_ps.at(it, 1))
                act_fn(q2T, TURNED[:], ACT.Copy).then_inc(s.q2T.sem, 1)
                beside()
                sc.wait_ge(s.u_ps.sem, s.u_ps.at(it, 1))
                act_fn(uT, bank[0][:], ACT.Identity, bias=K("A0_bv")).then_inc(s.u.sem, 1)
                keys(following, it)
                beside()
                beside()
                beside(AT_NORM)

            def softmax(s, it, beside, slot=None, following=None):
                sc.wait_ge(s.xT_ps.sem, s.xT_ps.at(it, 1))
                act_fn(att.xT_hi[:], Y[:], ACT.Copy).then_inc(s.xT_hi.sem, 1)
                if not s.cross:
                    sc.wait_ge(s.xT_lo.sem, s.xT_lo.at(it, 1))
                    act_fn(att.xT[:], Y[:], ACT.Copy).then_inc(s.xT_f.sem, 1)
                beside(AT_SPLIT)
                if not s.cross:
                    keys(s, it)
                sc.wait_ge(s.q_ps.sem, s.q_ps.at(it, 1))
                act_fn(q_hi[:], Q_BANK[:], ACT.Identity, bias=K("X0_bq") if s.biased else 0.0).then_inc(s.q_hi.sem, 1)
                if following:
                    context(slot, it)
                beside(AT_STACKS)

                def max_out(b):
                    sc.wait_ge(s.m_ps.sem, s.m_ps.at(it, b + 1))
                    if b >= 2:
                        sc.wait_ge(s.m_in[b % 2].sem, s.m_in[b % 2].at(it, 16 * (b // 2)))
                    act_fn(maxT[:, b % 2, :], score_bank(b, NG)[0:H, 0:N], ACT.Copy).then_inc(s.m_sb.sem, 1)

                def diagonal(b, j):
                    if b == 0 and j == 0:
                        sc.wait_ge(s.q_in.sem, s.q_in.at(it, 3 * 16))
                    if b >= 3 and j == 0:
                        sc.wait_ge(s.t_ps.sem, s.t_ps.at(it, NG * (b - 2)))
                    rows = slice(SLOT * j, SLOT * (j + 1))
                    last = act_fn(q_diag[rows, b % 3, :, j, :], q_stack[rows, :, b * N:(b + 1) * N].bitcast(f32), ACT.Copy)
                    if j == NJ - 1:
                        last.then_inc(s.q_diag.sem, 1)

                def exp(b, g):
                    if g == 0 and b >= 2:
                        sc.wait_ge(s.pv.sem, s.pv.at(it, b - 1))
                    u = b * NG + g
                    sc.wait_ge(s.t_ps.sem, s.t_ps.at(it, u + 1))
                    act_fn(probs[:, b % 2, g].rearrange("p j n -> p (j n)"), ST_BANK[:], ACT.Exp, scale=SCALE).then_inc(s.exp.sem, 1)

                for step in range(SEQS + 3):
                    for g in range(NG):
                        beside()
                        if 0 <= step - 2 < SEQS:
                            exp(step - 2, g)
                        if step < SEQS:
                            diagonal(step, g)
                    if step < SEQS:
                        max_out(step)
                if following:
                    keys(following, it)
                beside(AT_NORM)

            def experts(s, it, unit):
                kind, *k = unit
                if kind == "split":
                    sc.wait_ge(s.xT_ps.sem, s.xT_ps.at(it, 1))
                    act_fn(ffn.xT_hi[:], GATE[:], ACT.Copy).then_inc(s.xT_hi.sem, 1)
                elif kind == "copy":
                    sc.wait_ge(s.xT_lo.sem, s.xT_lo.at(it, 1))
                    act_fn(ffn.xT, GATE[:], ACT.Copy).then_inc(s.xT_f.sem, 1)
                elif kind == "exp":
                    sc.wait_ge(s.r_arg.sem, s.r_arg.at(it, 1))
                    act_fn(rt[1][:], rt[0][:], ACT.Exp, scale=-1.0 if s.name == "F0" else 1.0).then_inc(s.r_exp.sem, 1)
                elif kind == "up":
                    u, = k
                    n = s.chunks[u][3]
                    sc.wait_ge(s.gate_ps.sem, s.gate_ps.at(it, u + 1))
                    if u >= 2:
                        sc.wait_ge(s.hid.sem, s.hid.at(it, u - 1))
                    act_fn(gate[0:n, u % 2, :], GATE[0:n, :], ACT.Tanh, scale=0.5).then_inc(s.tanh.sem, 1)

            sc.wait_ge(ld_const, 48)
            with sc.Fori(0, TURNS) as it:
                for s in slots:
                    beside = Beside(s.layer, s.ffn.units, lambda unit: experts(s.ffn, it, unit), 1)
                    if s.layer == 0:
                        linear(s.first, it, beside, s, s.second)
                    else:
                        softmax(s.first, it, beside, s, s.second)
                    softmax(s.second, it, beside)
                    beside.end()
            for unit in slots[0].ffn.units:
                experts(slots[0].ffn, TURNS, unit)

        @block.gpsimd
        def _(po):
            po.memset(v_pad[:], 0.0)
            po.memset(q_stack[:].bitcast(f32), 0.0)
            po.memset(k_stack[:].bitcast(f32), -1.0)
            po.memset(q_diag[:].bitcast(f32), 0.0)
            po.memset(k_diag[:].bitcast(f32), 0.0)
            po.memset(half[:], -0.5).then_inc(fills, 1)

            def rstd_of(s, scratch, it):
                po.wait_ge(s.stats.sem, s.stats.at(it, 1))
                po.tensor_tensor(scratch.rstd[:], scratch.var[:], half[:], ALU.pow).then_inc(s.rstd.sem, 1)

            def diagonal(s, b, it):
                if b == 0:
                    po.wait_ge(s.k_in.sem, s.k_in.at(it, 3 * 16))
                if b >= 2:
                    po.wait_ge(s.s_ps.sem, s.s_ps.at(it, NG * (b - 1)))
                for j in range(PO_QUADRANTS):
                    rows = slice(SLOT * j, SLOT * (j + 1))
                    src = k_stack[rows, :, b * N:(b + 1) * N].bitcast(f32)
                    ones = one[rows].unsqueeze(2).to_broadcast((SLOT, NG, N))
                    po.tensor_tensor(k_diag[rows, b % 2, :, j, :], src, ones, ALU.mult).then_inc(s.k_diag_po.sem, 1)
                    po.wait_ge(s.k_diag_po.sem, s.k_diag_po.at(it, b * PO_QUADRANTS + j + 1))

            def add_bias(to, src, name):
                bias = K(name).unsqueeze(1).to_broadcast((128, SEQS, C))
                return po.tensor_tensor(to, src, bias, ALU.add)

            po.wait_ge(ld_const, 48)
            with po.Fori(0, TURNS) as it:
                for s in slots:
                    if s.layer == 0:
                        a = s.first
                        po.wait_ge(a.loaded.sem, a.loaded.at(it, 16))
                        po.wait_ge(x_free[s.g].sem, it * 16 + 16 * (1 + s.g))
                        add_bias(x[:, s.g], x_in[:], "A0_bout").then_inc(a.xb.sem, 1)
                        po.wait_ge(a.qn.sem, a.qn.at(it, 1))
                        po.tensor_tensor(qr[:], qn2c[:], half[:], ALU.pow).then_inc(a.qr.sem, 1)
                        po.wait_ge(a.kn.sem, a.kn.at(it, 1))
                        po.tensor_tensor(kr[:], kn2c[:], half[:], ALU.pow).then_inc(a.kr.sem, 1)
                    else:
                        for b in range(SEQS):
                            diagonal(s.first, b, it)
                    rstd_of(s.first, att, it)
                    diagonal(s.second, 0, it)
                    if s.layer == 0:
                        po.wait_ge(s.second.xT_ps.sem, s.second.xT_ps.at(it, 1))
                        add_bias(x[:, s.g], x[:, s.g], "X0_bo").then_inc(s.second.xb.sem, 1)
                    for b in range(1, SEQS):
                        diagonal(s.second, b, it)
                    rstd_of(s.ffn, ffn, it)
                    rstd_of(s.second, att, it)
            rstd_of(slots[0].ffn, ffn, TURNS)

        @block.vector
        def _(dv):
            tt, ts, stt = nc.vector.tensor_tensor, nc.vector.tensor_scalar, nc.vector.scalar_tensor_tensor
            steps = [0]

            def then(ins, it):
                steps[0] += 1
                ins.then_inc(dve_step.sem, 1)
                dv.wait_ge(dve_step.sem, dve_step.at(it, steps[0]))

            def stats(s, r, g, it):
                for b in range(SEQS):
                    last = nc.vector.bn_stats(r.bn[:, b, :], x[:, g, b, :])
                then(last, it)
                nc.vector.memset(wsum[:, 2:3], 0.0)
                for b in range(SEQS):
                    last = nc.vector.bn_aggr(r.mv[:, b, :], r.bn[:, b, :])
                then(last, it)
                ts(r.var[:], r.mv[:, :, 1], EPS_LN, None, ALU.add).then_inc(s.stats.sem, 1)

            def normalise_x(s, r, g, it):
                dv.wait_ge(s.rstd.sem, s.rstd.at(it, 1))
                for b in range(SEQS):
                    last = ts(x[:, g, b, :], x[:, g, b, :], r.mv[:, b, 0:1], r.rstd[:, b:b + 1], ALU.subtract, ALU.mult)
                last.then_inc(s.normed.sem, 1)

            def flat(g):
                return x[:, g].rearrange("p b c -> p (b c)")

            def add_output(s, g, it, beside):
                dv.wait_ge(s.y.sem, s.y.at(it, 1))
                tt(flat(g), Y[:], flat(g), ALU.add).then_inc(s.added.sem, 1)
                dv.wait_ge(s.added.sem, s.added.at(it, 1))
                stats(s, att, g, it)
                beside(AT_NORM)
                normalise_x(s, att, g, it)

            def context(s, it):
                dv.wait_ge(s.c.hi.sem, s.c.hi.at(it, 1))
                tt(cT_lo[:], Y[0:CTX, :], cT_hi[:].bitcast(f32), ALU.subtract).then_inc(s.c.lo.sem, 1)

            def keys(s, it):
                dv.wait_ge(s.k_hi.sem, s.k_hi.at(it, 1))
                stt(k_lo[:], K_BANK[:], K("X0_bk") if s.biased else 0.0, k_hi[:].bitcast(f32), ALU.add, ALU.subtract).then_inc(s.k_lo.sem, 1)

            def values(s, it):
                dv.wait_ge(s.v_ps.sem, s.v_ps.at(it, 1))
                for j in range(NJ):
                    to = v_pad[:, :, NG * j:NG * (j + 1), D * j:D * (j + 1)]
                    src = V_BANK[:].rearrange("p (b j g d) -> p b j g d", b=SEQS, j=NJ, g=NG)[:, :, j]
                    if s.biased:
                        bv = K("X0_bv").rearrange("p (j g d) -> p j g d", j=NJ, g=NG)[:, j].unsqueeze(1)
                        last = tt(to, src, bv.to_broadcast((128, SEQS, NG, D)), ALU.add)
                    else:
                        last = nc.vector.tensor_copy(to, src)
                last.then_inc(s.v_sb.sem, 1)

            def linear(s, g, it, beside, c, following):
                context(c, it)
                beside()
                for b in range(SEQS):
                    dv.wait_ge(s.qkv_ps.sem, s.qkv_ps.at(it, b + 1))
                    tt(qkv[:, b, :], bank[b % 3][:, 0:3 * C], K("A0_bqkv"), ALU.add).then_inc(s.qkv.sem, 1)
                    beside()
                beside(AT_SQUARES)
                dv.wait_ge(s.sq.sem, s.sq.at(it, 1))
                then(ts(rsum[:], ssum[:], EPS_SUM, None, ALU.add), it)
                then(nc.vector.reciprocal(rsum[:], rsum[:]), it)
                tt(sqn.rearrange("p b i c -> p (b i) c"), sq.rearrange("p b i c -> p (b i) c"),
                   rsum[:].rearrange("p b i -> p (b i)").unsqueeze(2).to_broadcast((128, SEQS * 2, C)), ALU.mult).then_inc(s.sqn.sem, 1)
                beside()
                dv.wait_ge(s.sq4q.sem, s.sq4q.at(it, 1))
                ts(qn2c[:], qn2[:], EPS_NORM2, None, ALU.max).then_inc(s.qn.sem, 1)
                dv.wait_ge(s.kn_ps.sem, s.kn_ps.at(it, 1))
                ts(kn2c[:], bank[2][:, 0:SEQS], EPS_NORM2, None, ALU.max).then_inc(s.kn.sem, 1)
                beside()
                dv.wait_ge(s.qr.sem, s.qr.at(it, 1))
                tt(q2, sqn[:, :, 0, :], qr[:].unsqueeze(2).to_broadcast((128, SEQS, C)), ALU.mult).then_inc(s.q2.sem, 1)
                dv.wait_ge(s.kr.sem, s.kr.at(it, 1))
                dv.wait_ge(s.kv_ps.sem, s.kv_ps.at(it, 1))
                for b in range(SEQS):
                    last = ts(kv[:, b, :], bank[1][:, b * C:(b + 1) * C], kr[:, b:b + 1], float(N) ** -0.5, ALU.mult, ALU.mult)
                last.then_inc(s.kv.sem, 1)
                beside()
                keys(following, it)
                beside()
                values(following, it)
                beside()
                dv.wait_ge(s.xb.sem, s.xb.at(it, 1))
                add_output(s, g, it, beside)

            def softmax(s, g, it, beside, slot=None, following=None):
                dv.wait_ge(s.xT_hi.sem, s.xT_hi.at(it, 1))
                tt(att.xT_lo[:], Y[:], att.xT_hi[:].bitcast(f32), ALU.subtract).then_inc(s.xT_lo.sem, 1)
                beside(AT_SPLIT)

                def diagonal(b, j):
                    if j == PO_QUADRANTS and b >= 2:
                        dv.wait_ge(s.s_ps.sem, s.s_ps.at(it, NG * (b - 1)))
                    rows = slice(SLOT * j, SLOT * (j + 1))
                    last = nc.vector.tensor_copy(k_diag[rows, b % 2, :, j, :], k_stack[rows, :, b * N:(b + 1) * N].bitcast(f32))
                    if j == NJ - 1:
                        last.then_inc(s.k_diag.sem, 1)

                def maximum(b, g):
                    if g == 0 and b >= 2:
                        dv.wait_ge(s.m_ps.sem, s.m_ps.at(it, b - 1))
                    dv.wait_ge(s.s_ps.sem, s.s_ps.at(it, b * NG + g + 1))
                    nc.vector.tensor_reduce(row_max[:, b % 2, NJ * g:NJ * (g + 1)],
                                            score_bank(b, g)[:].rearrange("p (j k) -> p j k", j=NJ), AX, ALU.max).then_inc(s.max.sem, 1)

                def normalise(b):
                    dv.wait_ge(s.pv.sem, s.pv.at(it, b + 1))
                    nc.vector.reciprocal(rden, den).then_inc(s.rden.sem, 1)
                    dv.wait_ge(s.rden.sem, s.rden.at(it, b + 1))
                    tt(attT[:, b % 2, :], num, rden, ALU.mult).then_inc(s.att.sem, 1)

                if s.cross:
                    dv.wait_ge(s.k_in.sem, s.k_in.at(it, 3 * 16))
                    for j in range(PO_QUADRANTS, NJ):
                        diagonal(0, j)
                else:
                    keys(s, it)
                dv.wait_ge(s.q_hi.sem, s.q_hi.at(it, 1))
                stt(q_lo[:], Q_BANK[:], K("X0_bq") if s.biased else 0.0, q_hi[:].bitcast(f32), ALU.add, ALU.subtract).then_inc(s.q_lo.sem, 1)
                if not s.cross:
                    values(s, it)
                if following:
                    context(slot, it)
                beside(AT_STACKS)
                if not s.cross:
                    dv.wait_ge(s.k_in.sem, s.k_in.at(it, 3 * 16))
                    for j in range(PO_QUADRANTS, NJ):
                        diagonal(0, j)
                for step in range(SEQS + 3):
                    for j in range(NG):
                        if step < SEQS:
                            maximum(step, j)
                        if step + 1 < SEQS and j >= PO_QUADRANTS:
                            diagonal(step + 1, j)
                        beside()
                    if 0 <= step - 3:
                        normalise(step - 3)
                if following:
                    keys(following, it)
                    values(following, it)
                if s.biased:
                    dv.wait_ge(s.xb.sem, s.xb.at(it, 1))
                add_output(s, g, it, beside)

            def first_of_max(p, n, mx, onehot, it):
                first = K("first")[:, 0:n].unsqueeze(1).to_broadcast((128, SEQS, n))
                then(nc.vector.tensor_reduce(mx[:], p, AX, ALU.max), it)
                then(tt(onehot, p, mx[:].unsqueeze(2).to_broadcast((128, SEQS, n)), ALU.is_equal), it)
                then(tt(onehot, onehot, first, ALU.mult), it)
                then(nc.vector.tensor_reduce(rs[3][:], onehot, AX, ALU.max), it)
                then(tt(onehot, rs[3][:].unsqueeze(2).to_broadcast((128, SEQS, n)), first, ALU.is_equal), it)

            def logits0(s, it):
                dv.wait_ge(s.r_ps.sem, s.r_ps.at(it, 1))
                then(tt(rt[0][:], DOWN[:, 0:SEQS * 8].rearrange("p (b e) -> p b e", e=8),
                        K("F0_brouter").unsqueeze(1).to_broadcast((128, SEQS, 8)), ALU.add), it)
                ts(rt[0][:], rt[0][:], -50.0, 50.0, ALU.max, ALU.min).then_inc(s.r_arg.sem, 1)

            def coef0(s, it):
                n = E0
                p, oh = rt[2][:, :, 0:n], rt[3][:, :, 0:n]
                dv.wait_ge(s.r_exp.sem, s.r_exp.at(it, 1))
                then(ts(rt[2][:], rt[1][:], 1.0, None, ALU.add), it)
                then(nc.vector.reciprocal(rt[2][:], rt[2][:]), it)
                first_of_max(p, n, rs[0], oh, it)
                then(ts(rs[0][:], rs[0][:], 1e-8, 1.0 - 1e-8, ALU.max, ALU.min), it)
                then(ts(rs[1][:], rs[0][:], 0.5, 1e-8, ALU.add, ALU.add), it)
                then(ts(rs[1][:], rs[1][:], 0.5, 2.0, ALU.max, ALU.min), it)
                then(nc.vector.reciprocal(rs[1][:], rs[1][:]), it)
                ts(coef[:, :, 0], rs[1][:], 0.5, 0.5, ALU.mult, ALU.mult)
                then(stt(rs[2][:], rs[0][:], 0.5, rs[1][:], ALU.mult, ALU.mult), it)
                then(tt(coef[:, :, 1:1 + n], oh, rs[2][:].unsqueeze(2).to_broadcast((128, SEQS, n)), ALU.mult), it)

            def logits1(s, it):
                dv.wait_ge(s.r_ps.sem, s.r_ps.at(it, 1))
                ps = DOWN[:, 0:SEQS * 8].rearrange("p (b e) -> p b e", e=8)
                then(nc.vector.tensor_reduce(rs[0][:], ps, AX, ALU.max), it)
                tt(rt[0][:], ps, rs[0][:].unsqueeze(2).to_broadcast((128, SEQS, E1)), ALU.subtract).then_inc(s.r_arg.sem, 1)

            def coef1(s, it):
                n = E1
                p, oh1, oh2, p2 = rt[2][:], rt[3][:], rt[4][:], rt[5][:]
                dv.wait_ge(s.r_exp.sem, s.r_exp.at(it, 1))
                then(nc.vector.tensor_reduce(rs[1][:], rt[1][:], AX, ALU.add), it)
                then(nc.vector.reciprocal(rs[1][:], rs[1][:]), it)
                then(tt(p, rt[1][:], rs[1][:].unsqueeze(2).to_broadcast((128, SEQS, n)), ALU.mult), it)
                first_of_max(p, n, rs[0], oh1, it)
                then(stt(p2, oh1, -2.0, p, ALU.mult, ALU.add), it)
                first_of_max(p2, n, rs[0], oh2, it)
                then(tt(oh1, oh1, oh2, ALU.add), it)
                nc.vector.memset(coef[:, :, 0], 0.5)
                then(stt(coef[:, :, 1:1 + n], oh1, 0.5, p, ALU.mult, ALU.mult), it)

            def experts(s, it, unit):
                kind, *k = unit
                if kind == "split":
                    dv.wait_ge(s.xT_hi.sem, s.xT_hi.at(it, 1))
                    tt(ffn.xT_lo[:], GATE[:], ffn.xT_hi[:].bitcast(f32), ALU.subtract).then_inc(s.xT_lo.sem, 1)
                elif kind == "router":
                    (logits0 if s.name == "F0" else logits1)(s, it)
                elif kind == "coef":
                    (coef0 if s.name == "F0" else coef1)(s, it)
                elif kind == "up":
                    u, = k
                    n = s.chunks[u][3]
                    dv.wait_ge(s.tanh.sem, s.tanh.at(it, u + 1))
                    stt(gate[0:n, u % 2, :], gate[0:n, u % 2, :], 1.0, GATE[0:n, :], ALU.add, ALU.mult).then_inc(s.silu.sem, 1)
                    if u >= 2:
                        dv.wait_ge(s.down.sem, s.down.at(it, sum(p[1] <= u - 2 for p in s.pieces)))
                    dv.wait_ge(s.up_ps.sem, s.up_ps.at(it, u + 1))
                    dv.wait_ge(s.silu.sem, s.silu.at(it, u + 1))
                    tt(hidden[0:n, u % 2, :], UP[0:n, :], gate[0:n, u % 2, :], ALU.mult).then_inc(s.hid.sem, 1)
                elif kind == "down" and s.pieces[k[0]][7]:
                    e = s.pieces[k[0]][0]
                    dv.wait_ge(s.down.sem, s.down.at(it, k[0] + 1))
                    if e:
                        dv.wait_ge(s.comb.sem, s.comb.at(it, e))
                    for b in range(SEQS):
                        last = stt(x[:, s.g, b, :], DOWN[:, b * C:(b + 1) * C], coef[:, b, e:e + 1],
                                   x[:, s.g, b, :], ALU.mult, ALU.add)
                    last.then_inc(s.comb.sem, 1)
                elif kind == "stats":
                    dv.wait_ge(s.comb.sem, s.comb.at(it, s.n))
                    stats(s, ffn, s.g, it)
                elif kind == "norm":
                    normalise_x(s, ffn, s.g, it)

            for n in range(n_stages):
                dv.wait_ge(ld_stage[n % 2], 16 * (n // 2 + 1))
                cols = slice(n * STAGE, (n + 1) * STAGE)
                nc.vector.tensor_copy(w_hi[:, cols], stage[:, n % 2, :]).then_inc(st_hi, 1)
                dv.wait_ge(st_hi, n + 1)
                tt(w_lo[:, cols], stage[:, n % 2, :], w_hi[:, cols].bitcast(f32), ALU.subtract).then_inc(st_lo, 1)
            dv.wait_ge(ld_const, 48)
            for i, m in enumerate((W("A0_qkv"), K("A0_bqkv"))):
                for j in range(2):
                    part = m[:, j * C:(j + 1) * C]
                    nc.vector.tensor_reduce(wsum[:, 0:1], part, AX, ALU.add).then_inc(centred_step, 1)
                    dv.wait_ge(centred_step, 3 * (2 * i + j) + 1)
                    ts(wsum[:, 1:2], wsum[:, 0:1], 1.0 / C, None, ALU.mult).then_inc(centred_step, 1)
                    dv.wait_ge(centred_step, 3 * (2 * i + j) + 2)
                    ts(part, part, wsum[:, 1:2], None, ALU.subtract).then_inc(centred_step, 1)
                    dv.wait_ge(centred_step, 3 * (2 * i + j) + 3)
            nc.vector.memset(wsum[:, 3:4], 0.0).then_inc(centred, 1)
            dv.wait_ge(fills, 1)
            for g in range(2):
                dv.wait_ge(x_free[g].sem, 16)
            nc.vector.memset(wsum[:, 4:5], 0.0).then_inc(slots[-1].second.normed.sem, 1)
            nc.vector.memset(wsum[:, 5:6], 0.0).then_inc(slots[-1].second.added.sem, 1)

            with dv.Fori(0, TURNS) as it:
                for s in slots:
                    beside = Beside(s.layer, s.ffn.units, lambda unit: experts(s.ffn, it, unit), 1)
                    if s.layer == 0:
                        linear(s.first, s.g, it, beside, s, s.second)
                    else:
                        softmax(s.first, s.g, it, beside, s, s.second)
                    softmax(s.second, s.g, it, beside)
                    beside.end()
            assert steps[0] == DVE_STEPS, steps[0]
            steps[0] = 0
            for unit in slots[0].ffn.units:
                experts(slots[0].ffn, TURNS, unit)


def _packed(parts, table, cols, rows=128):
    out = np.zeros((rows, cols), np.float32)
    for name, a in parts.items():
        c0, _ = table[name]
        out[:a.shape[0], c0:c0 + a.shape[1]] = a
    return out


def _slots(w):
    return w.reshape(w.shape[0], NJ, NG, D).transpose(0, 1, 3, 2).reshape(w.shape[0], C)


def _out_rows(w):
    return w.reshape(NJ, NG, D, C).transpose(1, 0, 2, 3).reshape(C, C)


def _chunk_rows(w):
    out = np.zeros((128, 3 * C), w.dtype)
    for i, (r0, n) in enumerate(CHUNKS0):
        out[:n, i * C:(i + 1) * C] = w[r0:r0 + n]
    return out


def _rows(v):
    return np.broadcast_to(v[None, :], (128, v.shape[0]))


def _layout(a):
    split = {
        "X0_q": _slots(a["L0_xattn_Wq"]), "X0_k": _slots(a["L0_xattn_Wk"]),
        "A1_q": _slots(a["L1_attn_Wq"]), "A1_k": _slots(a["L1_attn_Wk"]),
        "X1_q": _slots(a["L1_xattn_Wq"]), "X1_k": _slots(a["L1_xattn_Wk"]),
        "F0_gate0": a["L0_ffn_sw1"].T, "F0_up0": a["L0_ffn_sw3"].T,
        "F1_gate": np.concatenate([a["L1_ffn_shared_gate"], *a["L1_ffn_experts_gate"]], 1),
        "F1_up": np.concatenate([a["L1_ffn_shared_up"], *a["L1_ffn_experts_up"]], 1)}
    plain = {
        "A0_qkv": a["L0_attn_Wqkv"], "A0_out": a["L0_attn_Wln"],
        "X0_v": a["L0_xattn_Wv"], "X0_o": _out_rows(a["L0_xattn_Wo"]),
        "A1_v": a["L1_attn_Wv"], "A1_o": _out_rows(a["L1_attn_Wo"]),
        "X1_v": a["L1_xattn_Wv"], "X1_o": _out_rows(a["L1_xattn_Wo"]),
        "F0_router": a["L0_ffn_router_w"].T, "F1_router": a["L1_ffn_router"],
        "F0_down0": _chunk_rows(a["L0_ffn_sw2"].T),
        "F1_down": np.concatenate([a["L1_ffn_shared_down"], *a["L1_ffn_experts_down"].reshape(E1 // 2, 128, C)], 1)}
    for e in range(E0):
        split[f"F0_gate{e + 1}"] = a["L0_ffn_ew1"][e].T
        split[f"F0_up{e + 1}"] = a["L0_ffn_ew3"][e].T
        plain[f"F0_down{e + 1}"] = _chunk_rows(a["L0_ffn_ew2"][e].T)
    sums = np.zeros((128, NJ, SLOT), np.float32)
    for j in range(NJ):
        sums[:, j, D * j:D * (j + 1)] = 1
    bqkv = a["L0_attn_bqkv"]
    const = {
        "ident": np.eye(128, dtype=np.float32), "sum": sums.reshape(128, -1),
        "first": _rows(np.arange(8, 0, -1).astype(np.float32)),
        "A0_bqkv": _rows(bqkv), "A0_bout": _rows(a["L0_attn_bln"]), "X0_bv": _rows(a["L0_xattn_bv"]),
        "X0_bo": _rows(a["L0_xattn_bo"]), "F0_brouter": _rows(a["L0_ffn_routing_bias"]),
        "X0_bq": _slots(a["L0_xattn_bq"][None]).T, "X0_bk": _slots(a["L0_xattn_bk"][None]).T,
        "A0_bv": bqkv[2 * C:, None], "one": np.ones((128, 1), np.float32)}
    query, key = np.arange(N)[:, None], np.arange(N)[None, :]
    seen = (query - key >= 0) & (query - key < WIN)
    mask = np.where(seen, 0.0, MASKED)
    masks = np.concatenate([np.tile(mask, (1, NG)), np.tile(mask.T, (1, NG)), np.eye(N)], 1)
    return (_packed(split, SPLIT, SPLIT_COLS), _packed(plain, PLAIN, PLAIN_COLS),
            _packed(const, CONST, CONST_COLS), masks)


def kernel(**inputs):
    import numpy as _np
    import concourse.bacc as _bacc
    from concourse import mybir as _mybir
    from concourse.bass_utils import run_bass_kernel_spmd as _run

    a = {k: _np.asarray(v) for k, v in inputs.items()}
    split, plain, const, masks = _layout(a)
    bf16 = _mybir.dt.np(_mybir.dt.bfloat16)
    arrays = {"x": _np.ascontiguousarray(a["x"]), "ctx": _np.ascontiguousarray(a["ctx_768"]), "split": split, "plain": plain,
              "const": const, "masks": masks.astype(bf16)}
    nc = _bacc.Bacc("TRN2", target_bir_lowering=False, num_devices=1)
    args = [nc.dram_tensor(f"in_{n}", v.shape, _mybir.dt.from_np(v.dtype), kind="ExternalInput").ap() for n, v in arrays.items()]
    out = nc.dram_tensor("out_x", (B, N, C), _mybir.dt.float32, kind="ExternalOutput").ap()
    decoder_kernel(nc, *args, out)
    r = _run(nc, [{f"in_{n}": v for n, v in arrays.items()}], core_ids=[0])
    return r.results[0]["out_x"]
```

```python
from contextlib import ExitStack

import numpy as np

import concourse.bass as bass
from concourse import mybir

B, N, C, CTX = 32, 128, 128, 96
SEQS = 4
GROUPS = B // SEQS
T = SEQS * N
H, D = 16, 8
NJ, NG = 4, 4
WIN = 64
E0, I0 = 7, 352
E1, I1, S1 = 8, 64, 128
SCALE = D ** -0.5
EPS_LN = 1e-5
EPS_SUM = 1e-7
EPS_NORM2 = 1e-24
MASKED = -1e30
SLOT = 32

CHUNKS0 = [(0, 128), (128, 128), (256, 96)]


def _ranges(parts):
    at, out = 0, {}
    for name, n in parts:
        out[name] = (at, at + n)
        at += n
    return out, at


SPLIT, SPLIT_COLS = _ranges(
    [(f"{a}_{w}", 128) for a in ("X0", "A1", "X1") for w in ("q", "k")]
    + [(f"F0_{w}{e}", I0) for e in range(E0 + 1) for w in ("gate", "up")]
    + [("F1_gate", S1 + E1 * I1), ("F1_up", S1 + E1 * I1)])
PLAIN, PLAIN_COLS = _ranges(
    [("A0_qkv", 3 * C), ("A0_out", C)]
    + [(f"{a}_{w}", C) for a in ("X0", "A1", "X1") for w in ("v", "o")]
    + [("F0_router", 8), ("F1_router", 8)]
    + [(f"F0_down{e}", 3 * C) for e in range(E0 + 1)]
    + [("F1_down", 5 * C)])
CONST, CONST_COLS = _ranges(
    [("ident", 128), ("sum", NJ * SLOT), ("first", 8),
     ("A0_bqkv", 3 * C), ("A0_bout", C), ("X0_bv", C), ("X0_bo", C), ("F0_brouter", 8),
     ("X0_bq", 1), ("X0_bk", 1), ("A0_bv", 1), ("one", 1)])
MASK_COLS = 2 * NG * N + N

CHUNK_LIST0 = [(f"F0_gate{e}", f"F0_up{e}", c0, n) for e in range(E0 + 1) for c0, n in CHUNKS0]
PIECES0 = [(e, len(CHUNKS0) * e + i, 0, n, f"F0_down{e}", i * C, i == 0, i == len(CHUNKS0) - 1)
           for e in range(E0 + 1) for i, (_, n) in enumerate(CHUNKS0)]
CHUNK_LIST1 = [("F1_gate", "F1_up", 128 * p, 128) for p in range(1 + E1 // 2)]
PIECES1 = [(0, 0, 0, S1, "F1_down", 0, True, True)] + [
    (1 + 2 * p + i, 1 + p, I1 * i, I1, "F1_down", (1 + p) * C, True, True) for p in range(E1 // 2) for i in range(2)]


PAUSES = ((2, 1, 1), (3, 2, 0))


def _units(chunks, pieces, pauses):
    pause = ("pause",)
    units = [pause] * pauses[0] + [("split",), ("copy",)] + [pause] * pauses[1] + [("gate", 0), ("router",), ("up", 0), ("exp",), ("coef", 0), ("coef", 1)]
    for u in range(len(chunks)):
        if u + 1 < len(chunks):
            units += [("gate", u + 1), ("up", u + 1)]
        downs = [("down", k) for k, p in enumerate(pieces) if p[1] == u]
        units += downs if len(downs) == 1 else [downs[0], pause, downs[1], pause]
    return units + [("stats",), pause, ("norm",)] + [pause] * pauses[2]


UNITS0, UNITS1 = _units(CHUNK_LIST0, PIECES0, PAUSES[0]), _units(CHUNK_LIST1, PIECES1, PAUSES[1])

SLOTS = [(0, 0, 1, 1, 1), (1, 0, 0, 0, 0), (0, 1, 1, 0, 0), (1, 1, 0, 1, 0)]
TURNS = GROUPS // 2
AT_NORM, AT_SPLIT, AT_STACKS, AT_SQUARES = (6, 10), (1, 9), (10, 20), (8, 10)
AT_STEP = ((4, 3, 3, 2, 2, 2, 2), (2, 2, 3, 2, 2, 2, 2))
AT_LINEAR = 2


def _places(layer, ffn_layer):
    norm, split, stacks, squares = AT_NORM[ffn_layer], AT_SPLIT[ffn_layer], AT_STACKS[ffn_layer], AT_SQUARES[ffn_layer]
    softmax = split + stacks + sum(AT_STEP[ffn_layer]) * NG
    return norm + softmax + (softmax if layer else 10 * AT_LINEAR + squares)


MAX_ROW = 3
PO_QUADRANTS = 2
DVE_STEPS = 90


class Signal:

    def __init__(self, shared, base):
        self.all, self.base = shared, base
        self.sem = shared[0]

    def at(self, it, count, ago=0):
        return it * self.all[1] + (self.all[2] + self.base + count - ago * self.all[1])


def decoder_kernel(nc, x_d, ctx_d, split_d, plain_d, const_d, mask_d, out_d):
    f32, f32r, bf16 = mybir.dt.float32, mybir.dt.float32r, mybir.dt.bfloat16
    ALU = mybir.AluOpType
    ACT = mybir.ActivationFunctionType
    AX = mybir.AxisListType.X

    ctx = ExitStack()
    with ctx:
        def sb(name, shape, dt=f32):
            return ctx.enter_context(nc.sbuf_tensor(name, shape, dt))

        shared = {}

        def sig(name, own=1, lead=0):
            if name not in shared:
                shared[name] = [ctx.enter_context(nc.semaphore(name)), 0, lead]
            record = shared[name]
            record[1] += own
            return Signal(record, record[1] - own)

        w_hi = sb("w_hi", [128, SPLIT_COLS], f32r)
        w_lo = sb("w_lo", [128, SPLIT_COLS], f32r)
        plain = sb("plain", [128, PLAIN_COLS])
        const = sb("const", [128, CONST_COLS])
        masks = sb("masks", [128, MASK_COLS], bf16)
        STAGE, STAGES = 960, 4
        half = sb("half", [128, SEQS])
        wsum = sb("wsum", [128, 6])

        def W(name, rows=128):
            a, b = PLAIN[name]
            return plain[0:rows, a:b]

        def K(name):
            a, b = CONST[name]
            return const[:, a:b]

        ident = K("ident")
        one = K("one")

        x = sb("x", [128, 2, SEQS, C])
        x_in = sb("x_in", [128, SEQS, C])
        c_in = sb("c_in", [128, SEQS, CTX])
        cT = sb("cT", [CTX, T])
        cT_hi = sb("cT_hi", [CTX, T], f32r)
        cT_lo = sb("cT_lo", [CTX, T], f32r)

        class Stream:

            def __init__(s, name, xT):
                s.xT = xT
                s.xT_hi = sb(name + "_xT_hi", [128, T], f32r)
                s.xT_lo = sb(name + "_xT_lo", [128, T], f32r)
                s.bn = sb(name + "_bn", [128, SEQS, 6])
                s.mv = sb(name + "_mv", [128, SEQS, 2])
                s.var = sb(name + "_var", [128, SEQS])
                s.rstd = sb(name + "_rstd", [128, SEQS])

        gate = sb("gate", [128, 2, T])
        hidden = sb("hidden", [128, 2, T])
        att, ffn = Stream("att", sb("att_xT", [128, T])), Stream("ffn", hidden[:, 1])
        big = sb("big", [128, 8 * T])
        q_hi = sb("q_hi", [128, T], f32r)
        q_lo = sb("q_lo", [128, T], f32r)
        k_hi = sb("k_hi", [128, T], f32r)
        k_lo = sb("k_lo", [128, T], f32r)
        q_stack = sb("q_stack", [128, NG, T], f32r)
        k_stack = sb("k_stack", [128, NG, T], f32r)
        q_diag = sb("q_diag", [128, 3, NG, NJ, N], f32r)
        k_diag = sb("k_diag", [128, 2, NG, NJ, N], f32r)
        v_pad = sb("v_pad", [128, SEQS, H, SLOT])
        row_max = sb("row_max", [128, 2, H])
        maxT = q_lo[0:H, 0:2 * N].rearrange("p (i n) -> p i n", i=2)
        stage = big[:, 0:STAGES * STAGE].rearrange("p (i n) -> p i n", i=STAGES)
        probs = big[:].rearrange("p (i g j n) -> p i g j n", i=2, j=NJ, g=NG)
        rden = att.xT[:, 0:2 * N].rearrange("p (i n) -> p i n", i=2)
        attT = att.xT[:, 2 * N:4 * N].rearrange("p (i n) -> p i n", i=2)
        qkv = big[:, 0:3 * T].rearrange("p (b c) -> p b c", b=SEQS)
        sq = big[:, 3 * T:5 * T].rearrange("p (b i c) -> p b i c", b=SEQS, i=2)
        sqn = big[:, 5 * T:7 * T].rearrange("p (b i c) -> p b i c", b=SEQS, i=2)
        sq4 = sq
        kv = big[:, 7 * T:8 * T].rearrange("p (b c) -> p b c", b=SEQS)
        uT = big[:, 3 * T:4 * T]
        q2 = q_hi[:].bitcast(f32).rearrange("p (b c) -> p b c", b=SEQS)
        q2T = q_lo[:].bitcast(f32)
        ssum = sb("ssum", [128, SEQS, 2])
        rsum = sb("rsum", [128, SEQS, 2])
        qn2 = sb("qn2", [128, SEQS])
        qn2c = sb("qn2c", [128, SEQS])
        qr = sb("qr", [128, SEQS])
        kn2c = sb("kn2c", [128, SEQS])
        kr = sb("kr", [128, SEQS])
        rt = [sb(f"rt{i}", [128, SEQS, 8]) for i in range(6)]
        rs = [sb(f"rs{i}", [128, SEQS]) for i in range(4)]
        coef = sb("coef", [128, SEQS, 9])

        bank = [ctx.enter_context(nc.psum_tensor(f"bank{i}", [128, 512], f32)) for i in range(8)]
        S_BANKS = [bank[0], bank[3]]
        ST_BANK, HEADS, Y, GATE, UP, DOWN = bank[1], bank[2], *bank[4:]
        V_BANK, K_BANK, Q_BANK = bank[0], ST_BANK, HEADS
        A0_X, A0_KV, A0_U = bank[3], bank[3], bank[2]

        def heads(b):
            to = S_BANKS[1] if b == SEQS - 2 else HEADS
            return to[:, 0:N], to[:, N:2 * N]

        def score_bank(b, g):
            return S_BANKS[(b * (NG + 1) + g) % 2]

        def score_T_bank(b, g):
            return bank[0] if b >= SEQS - 2 and g % 2 else ST_BANK

        ld_const = ctx.enter_context(nc.semaphore("ld_const"))
        ld_stage = [ctx.enter_context(nc.semaphore(f"ld_stage{i}")) for i in range(STAGES)]
        st_hi = ctx.enter_context(nc.semaphore("st_hi"))
        st_lo = ctx.enter_context(nc.semaphore("st_lo"))
        fills = ctx.enter_context(nc.semaphore("fills"))
        centred = ctx.enter_context(nc.semaphore("centred"))
        centred_step = ctx.enter_context(nc.semaphore("centred_step"))
        dve_step = sig("dve_step", DVE_STEPS)
        x_free = [sig(f"x_free{i}", 16, 16) for i in range(2)]

        def norm_signals(s, of):
            s.stats = sig(of + "_stats")
            s.rstd = sig(of + "_rstd")
            s.normed = sig(of + "_normed", SEQS, SEQS if of == "att" else 0)

        def split_signals(s, of, whole=True):
            s.xT_ps = sig(of + "_xT_ps")
            s.xT_hi = sig(of + "_xT_hi")
            s.xT_lo = sig(of + "_xT_lo")
            s.xT_f = sig(of + "_xT_f") if whole else None

        class Context:

            def __init__(s):
                s.loaded = sig("c_loaded", 16)
                s.ps, s.hi, s.lo, s.f = sig("cT_ps"), sig("cT_hi"), sig("cT_lo"), sig("cT_f")

        class Linear:

            def __init__(s, g):
                s.g = g
                s.loaded = sig("x_loaded", 16)
                s.xT_ps, s.xT_f = sig("a0_xT_ps"), sig("a0_xT_f")
                s.qkv_ps = sig("a0_qkv_ps", SEQS)
                s.qkv = sig("a0_qkv", SEQS)
                s.sq = sig("a0_sq")
                s.sqn = sig("a0_sqn")
                s.sq4q, s.sq4k = sig("a0_sq4q"), sig("a0_sq4k")
                s.qn, s.qr = sig("a0_qn"), sig("a0_qr")
                s.kn_ps, s.kn, s.kr = sig("a0_kn_ps"), sig("a0_kn"), sig("a0_kr")
                s.q2, s.q2T_ps, s.q2T = sig("a0_q2"), sig("a0_q2T_ps"), sig("a0_q2T")
                s.kv_ps, s.kv = sig("a0_kv_ps"), sig("a0_kv")
                s.u_ps, s.u = sig("a0_u_ps"), sig("a0_u")
                s.xb = sig("a0_xb")
                s.y = sig("a0_y")
                s.added = sig("att_added", 1, 1)
                norm_signals(s, "att")
                s.late_norm = False

        class Softmax:

            def __init__(s, name, g, windowed, biased, cross):
                s.g = g
                s.name, s.windowed, s.biased, s.cross = name, windowed, biased, cross
                split_signals(s, "att", not cross)
                s.q_ps, s.k_ps, s.v_ps = sig("att_q_ps"), sig("att_k_ps"), sig("att_v_ps")
                s.q_hi, s.q_lo = sig("att_q_hi"), sig("att_q_lo")
                s.k_hi, s.k_lo = sig("att_k_hi"), sig("att_k_lo")
                s.v_sb = sig("att_v_sb")
                s.q_in = sig("att_q_in", 3 * 16)
                s.k_in = sig("att_k_in", 3 * 16)
                s.k_diag = sig("att_k_diag", SEQS)
                s.k_diag_po = sig("att_k_diag_po", SEQS * PO_QUADRANTS)
                s.q_diag = sig("att_q_diag", SEQS)
                s.s_ps = sig("att_s_ps", SEQS * NG)
                s.max = sig("att_max", SEQS * NG)
                s.m_ps = sig("att_m_ps", SEQS)
                s.m_sb = sig("att_m_sb", SEQS)
                s.m_in = [sig(f"att_m_in{i}", 16 * SEQS // 2) for i in range(2)]
                s.t_ps = sig("att_t_ps", SEQS * NG)
                s.exp = sig("att_exp", SEQS * NG)
                s.pv = sig("att_pv", SEQS)
                s.rden = sig("att_rden", SEQS)
                s.att = sig("att_att", SEQS)
                s.y = sig("att_y")
                s.xb = sig("x0_xb") if biased else None
                s.added = sig("att_added", 1, 1)
                norm_signals(s, "att")
                s.late_norm = False

        class Experts:

            def __init__(s, g, layer, ago):
                s.g, s.ago, s.layer, s.name = g, ago, layer, f"F{layer}"
                s.chunks, s.pieces = (CHUNK_LIST0, PIECES0) if layer == 0 else (CHUNK_LIST1, PIECES1)
                s.units = UNITS0 if layer == 0 else UNITS1
                s.n = 1 + max(p[0] for p in s.pieces)
                split_signals(s, "ffn")
                s.r_ps = sig("ffn_r_ps")
                s.r_arg = sig("ffn_r_arg")
                s.r_exp = sig("ffn_r_exp")
                s.gate_ps = sig("ffn_gate_ps", len(s.chunks))
                s.up_ps = sig("ffn_up_ps", len(s.chunks))
                s.tanh = sig("ffn_tanh", len(s.chunks))
                s.silu = sig("ffn_silu", len(s.chunks))
                s.hid = sig("ffn_hid", len(s.chunks))
                s.down = sig("ffn_down", len(s.pieces))
                s.comb = sig("ffn_comb", s.n)
                norm_signals(s, "ffn")

        class Slot:
            def __init__(s, g, layer, ffn_g, ffn_layer, ago):
                s.g, s.layer = g, layer
                s.c = Context()
                s.first = Linear(g) if layer == 0 else Softmax("A1", g, True, False, False)
                s.second = Softmax(f"X{layer}", g, False, layer == 0, True)
                s.ffn = Experts(ffn_g, ffn_layer, ago)

        slots = [Slot(*s) for s in SLOTS]
        for i, s in enumerate(slots):
            s.before, s.before_ago = slots[i - 1].second, 1 if i == 0 else 0
            s.ffn.input = slots[i - 1].second
            if s.layer == 1:
                s.input = slots[i - 1].ffn
                s.before.late_norm = True

        class Beside:

            def __init__(s, slot, emit, lag=0):
                s.places, s.units = _places(slot.layer, slot.ffn.layer), slot.ffn.units
                s.norm, s.split, s.stacks, s.squares = (
                    w[slot.ffn.layer] for w in (AT_NORM, AT_SPLIT, AT_STACKS, AT_SQUARES))
                s.step = AT_STEP[slot.ffn.layer]
                s.emit, s.lag, s.at, s.done = emit, lag, 0, 0

            def __call__(s, places=AT_LINEAR):
                s.at += places
                while s.done < len(s.units) * s.at // s.places:
                    if s.done >= s.lag:
                        s.emit(s.units[s.done - s.lag])
                    s.done += 1
                if s.at == s.places and s.lag:
                    s.emit(s.units[-1])

            def end(s):
                assert s.at == s.places, (s.at, s.places)

        block = ctx.enter_context(nc.Block())
        n_stages = SPLIT_COLS // STAGE
        assert n_stages * STAGE == SPLIT_COLS

        @block.sync
        def _(sp):
            def rows(d, first):
                return d[bass.ds(first, SEQS)].rearrange("b n c -> n b c")

            sp.dma_start(const[:], const_d).then_inc(ld_const, 16)
            sp.dma_start(masks[:], mask_d).then_inc(ld_const, 16)
            for n in range(n_stages):
                if n == STAGES:
                    sp.dma_start(plain[:], plain_d).then_inc(ld_const, 16)
                if n >= STAGES:
                    sp.wait_ge(st_lo, n - STAGES + 1)
                sp.dma_start(stage[:, n % STAGES, :], split_d[:, n * STAGE:(n + 1) * STAGE]).then_inc(ld_stage[n % STAGES], 16)
            for g in range(2):
                sp.dma_start(x[:, g], rows(x_d, 0)).then_inc(x_free[g].sem, 16)
            sp.dma_start(x_in[:], rows(x_d, 0)).then_inc(slots[0].first.loaded.sem, 16)
            sp.dma_start(c_in[:], rows(ctx_d, 0)).then_inc(slots[0].c.loaded.sem, 16)
            sp.wait_ge(fills, 1)

            def load_context(c, group, it):
                sp.wait_ge(c.ps.sem, c.ps.at(it, 1))
                sp.dma_start(c_in[:], rows(ctx_d, group * SEQS)).then_inc(c.loaded.sem, 16)

            def softmax(s, it, following=None):
                sp.wait_ge(s.k_hi.sem, s.k_hi.at(it, 1))
                sp.dma_start(k_stack[0::4].bitcast(f32), k_hi[:].bitcast(f32)).then_inc(s.k_in.sem, 16)
                sp.dma_start(k_stack[2::4].bitcast(f32), k_hi[:].bitcast(f32)).then_inc(s.k_in.sem, 16)
                sp.wait_ge(s.k_lo.sem, s.k_lo.at(it, 1))
                sp.dma_start(k_stack[1::4].bitcast(f32), k_lo[:].bitcast(f32)).then_inc(s.k_in.sem, 16)
                sp.wait_ge(s.q_hi.sem, s.q_hi.at(it, 1))
                sp.dma_start(q_stack[0::4].bitcast(f32), q_hi[:].bitcast(f32)).then_inc(s.q_in.sem, 16)
                sp.dma_start(q_stack[1::4].bitcast(f32), q_hi[:].bitcast(f32)).then_inc(s.q_in.sem, 16)
                sp.wait_ge(s.q_lo.sem, s.q_lo.at(it, 1))
                sp.dma_start(q_stack[2::4].bitcast(f32), q_lo[:].bitcast(f32)).then_inc(s.q_in.sem, 16)
                if following:
                    load_context(*following)
                for b in range(SEQS):
                    sp.wait_ge(s.q_diag.sem, s.q_diag.at(it, b + 1))
                    sp.wait_ge(s.m_sb.sem, s.m_sb.at(it, b + 1))
                    to = q_diag[MAX_ROW:MAX_ROW + 1, b % 3].rearrange("p g j n -> p (g j) n")
                    sp.dma_start(to.bitcast(f32), maxT[:, b % 2, :].bitcast(f32)).then_inc(s.m_in[b % 2].sem, 16)

            def store(s, group, it):
                sp.wait_ge(s.normed.sem, s.normed.at(it, SEQS))
                sp.dma_start(rows(out_d, group * SEQS), x[:, s.g]).then_inc(x_free[s.g].sem, 16)

            with sp.Fori(0, TURNS) as it:
                for i, s in enumerate(slots):
                    group = (it * 2 + (1, 0, 1, 2)[i]) % GROUPS
                    if s.layer == 0:
                        load_context(s.c, group, it)
                        sp.wait_ge(s.first.xT_ps.sem, s.first.xT_ps.at(it, 1))
                        sp.wait_ge(s.first.xb.sem, s.first.xb.at(it, 1))
                        group = (it * 2 + 1 + i) % GROUPS
                        sp.dma_start(x_in[:], rows(x_d, group * SEQS)).then_inc(s.first.loaded.sem, 16)
                    else:
                        softmax(s.first, it, (s.c, group, it))
                    softmax(s.second, it)
                    if s.ffn.name == "F1":
                        store(s.ffn, (it * 2 + GROUPS - 1) % GROUPS if i == 0 else it * 2, it)
            store(slots[0].ffn, GROUPS - 1, TURNS)
            sp.wait_ge(x_free[0].sem, 16 * (TURNS + 1))
            sp.wait_ge(x_free[1].sem, 16 * (TURNS + 2))
            sp.wait_ge(slots[0].first.loaded.sem, slots[0].first.loaded.at(TURNS, 16))
            sp.wait_ge(slots[0].c.loaded.sem, slots[0].c.loaded.at(TURNS, 16))

        @block.tensor
        def _(pe):
            mm = nc.tensor.matmul

            def split_matmul(out, wname, c0, n, hi, lo, rows=128, lo_made=None):
                a = SPLIT[wname][0] + c0
                wh, wl = w_hi[0:rows, a:a + n], w_lo[0:rows, a:a + n]
                mm(out, wl, hi[:], start=True, stop=False)
                mm(out, wh, hi[:], start=False, stop=False)
                if lo_made:
                    pe.wait_ge(*lo_made)
                return mm(out, wh, lo[:], start=False, stop=True)

            def transposes(to, src, rows=128, normed=None, it=0, ago=0):
                for b in range(SEQS):
                    if normed:
                        pe.wait_ge(normed.sem, normed.at(it, b + 1, ago))
                    last = nc.tensor.transpose(to[0:rows, b * N:(b + 1) * N], src[:, b, :], ident)
                return last

            def context(s, it):
                pe.wait_ge(s.c.loaded.sem, s.c.loaded.at(it, 16))
                transposes(Y, c_in, CTX).then_inc(s.c.ps.sem, 1)

            def keys(s, it, lo_made=None):
                hi, lo, rows = (cT_hi, cT_lo, CTX) if s.cross else (att.xT_hi, att.xT_lo, C)
                split_matmul(K_BANK[:], s.name + "_k", 0, 128, hi, lo, rows, lo_made).then_inc(s.k_ps.sem, 1)

            def values(s, it):
                src, rows = (cT, CTX) if s.cross else (att.xT, C)
                for b in range(SEQS):
                    last = mm(V_BANK[:, b * C:(b + 1) * C], src[:, b * N:(b + 1) * N], W(s.name + "_v", rows), start=True, stop=True)
                last.then_inc(s.v_ps.sem, 1)

            def linear(s, it, beside, c, following):
                pe.wait_ge(s.loaded.sem, s.loaded.at(it, 16))
                transposes(A0_X, x_in).then_inc(s.xT_ps.sem, 1)
                beside()
                pe.wait_ge(s.xT_f.sem, s.xT_f.at(it, 1))
                for b in range(SEQS):
                    mm(bank[b][:, 0:3 * C], att.xT[:, b * N:(b + 1) * N], W("A0_qkv"), start=True, stop=True).then_inc(s.qkv_ps.sem, 1)
                    beside()
                pe.wait_ge(c.before.added.sem, c.before.added.at(it, 1, c.before_ago))
                context(c, it)
                beside(beside.squares)
                pe.wait_ge(c.c.f.sem, c.c.f.at(it, 1))
                pe.wait_ge(s.qkv.sem, s.qkv.at(it, 2))
                keys(following, it)
                values(following, it)
                pe.wait_ge(s.sqn.sem, s.sqn.at(it, 1))
                for b in range(SEQS):
                    last = mm(A0_KV[:, b * C:(b + 1) * C], sqn[:, b, 1, :], qkv[:, b, 2 * C:3 * C], start=True, stop=True)
                last.then_inc(s.kv_ps.sem, 1)
                beside()
                pe.wait_ge(s.sq4k.sem, s.sq4k.at(it, 1))
                for b in range(SEQS):
                    last = mm(Y[:, b:b + 1], sq4[:, b, 1, :], one, start=True, stop=True)
                last.then_inc(s.kn_ps.sem, 1)
                beside()
                mm(A0_U[:], W("A0_qkv")[:, 2 * C:3 * C], att.xT[:], start=True, stop=False)
                pe.wait_ge(s.q2.sem, s.q2.at(it, 1))
                transposes(Y, q2).then_inc(s.q2T_ps.sem, 1)
                beside()
                pe.wait_ge(s.kv.sem, s.kv.at(it, 1))
                pe.wait_ge(s.q2T.sem, s.q2T.at(it, 1))
                for b in range(SEQS):
                    last = mm(A0_U[:, b * N:(b + 1) * N], kv[:, b, :], q2T[:, b * N:(b + 1) * N], start=False, stop=b == SEQS - 1)
                last.then_inc(s.u_ps.sem, 1)
                beside()
                pe.wait_ge(s.u.sem, s.u.at(it, 1))
                for b in range(SEQS):
                    last = mm(Y[:, b * C:(b + 1) * C], uT[:, b * N:(b + 1) * N], W("A0_out"), start=True, stop=True)
                last.then_inc(s.y.sem, 1)
                beside()
                beside(beside.norm)

            def softmax(s, it, beside, inputs, slot=None, following=None):
                transposes(Y, x[:, s.g], normed=inputs.normed, it=it).then_inc(s.xT_ps.sem, 1)
                beside(beside.split)
                pe.wait_ge(s.xT_hi.sem, s.xT_hi.at(it, 1))
                lo_made = s.xT_lo.sem, s.xT_lo.at(it, 1)
                if not s.cross:
                    keys(s, it, lo_made)
                split_matmul(Q_BANK[:], s.name + "_q", 0, 128, att.xT_hi, att.xT_lo,
                             lo_made=lo_made if s.cross else None).then_inc(s.q_ps.sem, 1)
                if not s.cross:
                    pe.wait_ge(s.xT_f.sem, s.xT_f.at(it, 1))
                    values(s, it)
                if following:
                    pe.wait_ge(s.xT_f.sem, s.xT_f.at(it, 1))
                    context(slot, it)
                beside(beside.stacks)

                def score(b, g):
                    u = b * NG + g
                    if g == 0:
                        pe.wait_ge(s.k_diag.sem, s.k_diag.at(it, b + 1))
                        pe.wait_ge(s.k_diag_po.sem, s.k_diag_po.at(it, PO_QUADRANTS * (b + 1)))
                    if u == 0:
                        pe.wait_ge(s.v_sb.sem, s.v_sb.at(it, 1))
                        pe.wait_ge(s.q_in.sem, s.q_in.at(it, 3 * 16))
                    elif g == 1 and b >= 1:
                        pe.wait_ge(s.m_sb.sem, s.m_sb.at(it, b))
                    elif u >= 2:
                        pe.wait_ge(s.max.sem, s.max.at(it, u if g == 0 else u - 1))
                    to = score_bank(b, g)
                    if s.windowed:
                        mm(to[:], masks[:, 2 * NG * N:], masks[:, 0:NG * N], start=True, stop=False)
                    mm(to[:], q_stack[:, g, b * N:(b + 1) * N], k_diag[:, b % 2, g].rearrange("p j n -> p (j n)"),
                       start=not s.windowed, stop=True).then_inc(s.s_ps.sem, 1)

                def transpose_max(b):
                    pe.wait_ge(s.max.sem, s.max.at(it, NG * (b + 1)))
                    nc.tensor.transpose(score_bank(b, NG)[0:H, 0:N], row_max[:, b % 2, :], ident).then_inc(s.m_ps.sem, 1)

                def score_T(b, g):
                    u = b * NG + g
                    if g == 0:
                        pe.wait_ge(s.m_in[b % 2].sem, s.m_in[b % 2].at(it, 16 * (b // 2 + 1)))
                    if u >= 1:
                        pe.wait_ge(s.exp.sem, s.exp.at(it, u - 1 if u > NG * (SEQS - 2) else u))
                    to = score_T_bank(b, g)
                    if s.windowed:
                        mm(to[:], masks[:, 2 * NG * N:], masks[:, NG * N:2 * NG * N], start=True, stop=False)
                    mm(to[:], k_stack[:, g, b * N:(b + 1) * N], q_diag[:, b % 3, g].rearrange("p j n -> p (j n)"),
                       start=not s.windowed, stop=True).then_inc(s.t_ps.sem, 1)

                def probs_v(b, j):
                    if j == 0:
                        pe.wait_ge(s.exp.sem, s.exp.at(it, NG * (b + 1)))
                        if b == SEQS - 2:
                            pe.wait_ge(s.m_sb.sem, s.m_sb.at(it, SEQS))
                        elif b >= 1:
                            pe.wait_ge(s.att.sem, s.att.at(it, b - 1 if b == SEQS - 1 else b))
                    num, den = heads(b)
                    a = CONST["sum"][0]
                    for g in range(NG):
                        mm(den[SLOT * g:SLOT * (g + 1)], const[:, a + SLOT * j:a + SLOT * (j + 1)], probs[:, b % 2, g, j, :],
                           start=j == 0, stop=j == NJ - 1, skip_group_check=True)
                    for g in range(NG):
                        last = mm(num[SLOT * g:SLOT * (g + 1)], v_pad[:, b, 4 * j + g, :], probs[:, b % 2, g, j, :],
                                  start=False, stop=j == NJ - 1, skip_group_check=True)
                    if j == NJ - 1:
                        last.then_inc(s.pv.sem, 1)

                def project(b):
                    pe.wait_ge(s.att.sem, s.att.at(it, b + 1))
                    if b == 0 and following:
                        pe.wait_ge(slot.c.f.sem, slot.c.f.at(it, 1))
                    return mm(Y[:, b * C:(b + 1) * C], attT[:, b % 2, :], W(s.name + "_o"), start=True, stop=True)

                for step in range(SEQS + 3):
                    for g in range(NG):
                        if 0 <= step - 2 < SEQS:
                            score_T(step - 2, g)
                        if g == 0 and 0 <= step - 1 < SEQS:
                            transpose_max(step - 1)
                        if step < SEQS:
                            score(step, g)
                        if g >= 1 and step >= 3:
                            probs_v(step - 3, g - 1)
                        if g == NG - 1 and step >= 3:
                            probs_v(step - 3, NJ - 1)
                        if g == NG - 1 and step >= 4:
                            project(step - 4)
                        beside(beside.step[step])
                if following:
                    keys(following, it)
                    values(following, it)
                project(SEQS - 1).then_inc(s.y.sem, 1)
                if following:
                    beside(beside.norm)

            def experts(s, it, unit):
                kind, *k = unit
                if kind == "split":
                    transposes(DOWN, x[:, s.g], normed=s.input.normed, it=it, ago=s.ago).then_inc(s.xT_ps.sem, 1)
                elif kind == "router":
                    pe.wait_ge(s.xT_f.sem, s.xT_f.at(it, 1))
                    for b in range(SEQS):
                        last = mm(DOWN[:, b * 8:(b + 1) * 8], ffn.xT[:, b * N:(b + 1) * N], W(s.name + "_router"), start=True, stop=True)
                    last.then_inc(s.r_ps.sem, 1)
                elif kind == "gate":
                    u, = k
                    wg, _, c0, n = s.chunks[u]
                    if u == 0:
                        pe.wait_ge(s.xT_lo.sem, s.xT_lo.at(it, 1))
                    else:
                        pe.wait_ge(s.silu.sem, s.silu.at(it, u))
                    split_matmul(GATE[0:n, :], wg, c0, n, ffn.xT_hi, ffn.xT_lo).then_inc(s.gate_ps.sem, 1)
                elif kind == "up":
                    u, = k
                    _, wu, c0, n = s.chunks[u]
                    if u >= 1:
                        pe.wait_ge(s.hid.sem, s.hid.at(it, u))
                    split_matmul(UP[0:n, :], wu, c0, n, ffn.xT_hi, ffn.xT_lo).then_inc(s.up_ps.sem, 1)
                elif kind == "down":
                    e, u, r0, n, wname, col, first, end = s.pieces[k[0]]
                    pe.wait_ge(s.hid.sem, s.hid.at(it, u + 1))
                    if k[0] == 0:
                        pe.wait_ge(s.r_arg.sem, s.r_arg.at(it, 1))
                    if first and e >= 1:
                        pe.wait_ge(s.comb.sem, s.comb.at(it, e))
                    for b in range(SEQS):
                        last = mm(DOWN[:, b * C:(b + 1) * C], hidden[r0:r0 + n, u % 2, b * N:(b + 1) * N],
                                  W(wname)[r0:r0 + n, col:col + C], start=first and b == 0, stop=end, skip_group_check=True)
                    last.then_inc(s.down.sem, 1)

            pe.wait_ge(ld_const, 48)
            pe.wait_ge(centred, 1)
            pe.wait_ge(st_lo, n_stages)
            pe.wait_ge(fills, 1)
            with pe.Fori(0, TURNS) as it:
                for s in slots:
                    beside = Beside(s, lambda unit: experts(s.ffn, it, unit))
                    if s.layer == 0:
                        linear(s.first, it, beside, s, s.second)
                    else:
                        pe.wait_ge(s.before.added.sem, s.before.added.at(it, 1, s.before_ago))
                        softmax(s.first, it, beside, s.input, s, s.second)
                    softmax(s.second, it, beside, s.first)
                    beside.end()
            for unit in slots[0].ffn.units:
                experts(slots[0].ffn, TURNS, unit)

        @block.scalar
        def _(sc):
            act_fn = nc.scalar.activation

            def context(s, it):
                sc.wait_ge(s.c.ps.sem, s.c.ps.at(it, 1))
                act_fn(cT_hi[:], Y[0:CTX, :], ACT.Copy).then_inc(s.c.hi.sem, 1)
                sc.wait_ge(s.c.lo.sem, s.c.lo.at(it, 1))
                act_fn(cT[:], Y[0:CTX, :], ACT.Copy).then_inc(s.c.f.sem, 1)

            def keys(s, it):
                sc.wait_ge(s.k_ps.sem, s.k_ps.at(it, 1))
                act_fn(k_hi[:], K_BANK[:], ACT.Identity, bias=K("X0_bk") if s.biased else 0.0).then_inc(s.k_hi.sem, 1)

            def linear(s, it, beside, c, following):
                sc.wait_ge(s.xT_ps.sem, s.xT_ps.at(it, 1))
                act_fn(att.xT[:], A0_X[:], ACT.Copy).then_inc(s.xT_f.sem, 1)
                beside()
                for b in range(SEQS):
                    sc.wait_ge(s.qkv.sem, s.qkv.at(it, b + 1))
                    for i in range(2):
                        last = act_fn(sq[:, b, i, :], qkv[:, b, i * C:(i + 1) * C], ACT.Square, accum_out=ssum[:, b, i:i + 1])
                    if b == SEQS - 1:
                        last.then_inc(s.sq.sem, 1)
                    beside()
                context(c, it)
                beside(beside.squares)
                keys(following, it)
                sc.wait_ge(s.sqn.sem, s.sqn.at(it, 1))
                act_fn(sq4[:, :, 1, :], sqn[:, :, 1, :], ACT.Square).then_inc(s.sq4k.sem, 1)
                for b in range(SEQS):
                    last = act_fn(sq4[:, b, 0, :], sqn[:, b, 0, :], ACT.Square, accum_out=qn2[:, b:b + 1])
                last.then_inc(s.sq4q.sem, 1)
                beside()
                beside()
                sc.wait_ge(s.q2T_ps.sem, s.q2T_ps.at(it, 1))
                act_fn(q2T, Y[:], ACT.Copy).then_inc(s.q2T.sem, 1)
                beside()
                sc.wait_ge(s.u_ps.sem, s.u_ps.at(it, 1))
                act_fn(uT, A0_U[:], ACT.Identity, bias=K("A0_bv")).then_inc(s.u.sem, 1)
                beside()
                beside()
                beside(beside.norm)

            def softmax(s, it, beside, slot=None, following=None):
                sc.wait_ge(s.xT_ps.sem, s.xT_ps.at(it, 1))
                act_fn(att.xT_hi[:], Y[:], ACT.Copy).then_inc(s.xT_hi.sem, 1)
                if not s.cross:
                    sc.wait_ge(s.xT_lo.sem, s.xT_lo.at(it, 1))
                    act_fn(att.xT[:], Y[:], ACT.Copy).then_inc(s.xT_f.sem, 1)
                beside(beside.split)
                if not s.cross:
                    keys(s, it)
                sc.wait_ge(s.q_ps.sem, s.q_ps.at(it, 1))
                act_fn(q_hi[:], Q_BANK[:], ACT.Identity, bias=K("X0_bq") if s.biased else 0.0).then_inc(s.q_hi.sem, 1)
                if following:
                    context(slot, it)
                beside(beside.stacks)

                def max_out(b):
                    sc.wait_ge(s.m_ps.sem, s.m_ps.at(it, b + 1))
                    if b >= 2:
                        sc.wait_ge(s.m_in[b % 2].sem, s.m_in[b % 2].at(it, 16 * (b // 2)))
                    act_fn(maxT[:, b % 2, :], score_bank(b, NG)[0:H, 0:N], ACT.Copy).then_inc(s.m_sb.sem, 1)

                def diagonal(b, j):
                    if b == 0 and j == 0:
                        sc.wait_ge(s.q_in.sem, s.q_in.at(it, 3 * 16))
                    if b >= 3 and j == 0:
                        sc.wait_ge(s.t_ps.sem, s.t_ps.at(it, NG * (b - 2)))
                    rows = slice(SLOT * j, SLOT * (j + 1))
                    last = act_fn(q_diag[rows, b % 3, :, j, :], q_stack[rows, :, b * N:(b + 1) * N].bitcast(f32), ACT.Copy)
                    if j == NJ - 1:
                        last.then_inc(s.q_diag.sem, 1)

                def exp(b, g):
                    if g == 0 and b >= 2:
                        sc.wait_ge(s.pv.sem, s.pv.at(it, b - 1))
                    u = b * NG + g
                    sc.wait_ge(s.t_ps.sem, s.t_ps.at(it, u + 1))
                    act_fn(probs[:, b % 2, g].rearrange("p j n -> p (j n)"), score_T_bank(b, g)[:], ACT.Exp, scale=SCALE).then_inc(s.exp.sem, 1)

                for step in range(SEQS + 3):
                    for g in range(NG):
                        if 0 <= step - 2 < SEQS:
                            exp(step - 2, g)
                        beside(beside.step[step])
                        if g == 0 and 0 <= step - 1 < SEQS:
                            max_out(step - 1)
                        if step < SEQS:
                            diagonal(step, g)
                if following:
                    keys(following, it)
                    beside(beside.norm)

            def experts(s, it, unit):
                kind, *k = unit
                if kind == "split":
                    sc.wait_ge(s.xT_ps.sem, s.xT_ps.at(it, 1))
                    act_fn(ffn.xT_hi[:], DOWN[:], ACT.Copy).then_inc(s.xT_hi.sem, 1)
                elif kind == "copy":
                    sc.wait_ge(s.xT_lo.sem, s.xT_lo.at(it, 1))
                    act_fn(ffn.xT, DOWN[:], ACT.Copy).then_inc(s.xT_f.sem, 1)
                elif kind == "exp":
                    sc.wait_ge(s.r_arg.sem, s.r_arg.at(it, 1))
                    act_fn(rt[1][:], rt[0][:], ACT.Exp, scale=-1.0 if s.name == "F0" else 1.0).then_inc(s.r_exp.sem, 1)
                elif kind == "gate":
                    u, = k
                    n = s.chunks[u][3]
                    sc.wait_ge(s.gate_ps.sem, s.gate_ps.at(it, u + 1))
                    if u >= 2:
                        sc.wait_ge(s.hid.sem, s.hid.at(it, u - 1))
                    act_fn(gate[0:n, u % 2, :], GATE[0:n, :], ACT.Tanh, scale=0.5).then_inc(s.tanh.sem, 1)

            sc.wait_ge(ld_const, 48)
            with sc.Fori(0, TURNS) as it:
                for s in slots:
                    beside = Beside(s, lambda unit: experts(s.ffn, it, unit), 1)
                    if s.layer == 0:
                        linear(s.first, it, beside, s, s.second)
                    else:
                        softmax(s.first, it, beside, s, s.second)
                    softmax(s.second, it, beside)
                    beside.end()
            for unit in slots[0].ffn.units:
                experts(slots[0].ffn, TURNS, unit)

        @block.gpsimd
        def _(po):
            po.memset(v_pad[:], 0.0)
            po.memset(q_stack[:].bitcast(f32), 0.0)
            po.memset(k_stack[:].bitcast(f32), -1.0)
            po.memset(q_diag[:].bitcast(f32), 0.0)
            po.memset(k_diag[:].bitcast(f32), 0.0)
            po.memset(half[:], -0.5).then_inc(fills, 1)

            def rstd_of(s, scratch, it):
                po.wait_ge(s.stats.sem, s.stats.at(it, 1))
                po.tensor_tensor(scratch.rstd[:], scratch.var[:], half[:], ALU.pow).then_inc(s.rstd.sem, 1)

            def diagonal(s, b, it):
                if b == 0:
                    po.wait_ge(s.k_in.sem, s.k_in.at(it, 3 * 16))
                if b >= 2:
                    po.wait_ge(s.s_ps.sem, s.s_ps.at(it, NG * (b - 1)))
                for j in range(PO_QUADRANTS):
                    rows = slice(SLOT * j, SLOT * (j + 1))
                    src = k_stack[rows, :, b * N:(b + 1) * N].bitcast(f32)
                    ones = one[rows].unsqueeze(2).to_broadcast((SLOT, NG, N))
                    po.tensor_tensor(k_diag[rows, b % 2, :, j, :], src, ones, ALU.mult).then_inc(s.k_diag_po.sem, 1)
                    po.wait_ge(s.k_diag_po.sem, s.k_diag_po.at(it, b * PO_QUADRANTS + j + 1))

            def add_bias(to, src, name):
                bias = K(name).unsqueeze(1).to_broadcast((128, SEQS, C))
                return po.tensor_tensor(to, src, bias, ALU.add)

            po.wait_ge(ld_const, 48)
            with po.Fori(0, TURNS) as it:
                for s in slots:
                    if s.layer == 0:
                        a = s.first
                        po.wait_ge(a.loaded.sem, a.loaded.at(it, 16))
                        po.wait_ge(x_free[s.g].sem, it * 16 + 16 * (1 + s.g))
                        add_bias(x[:, s.g], x_in[:], "A0_bout").then_inc(a.xb.sem, 1)
                        po.wait_ge(a.qn.sem, a.qn.at(it, 1))
                        po.tensor_tensor(qr[:], qn2c[:], half[:], ALU.pow).then_inc(a.qr.sem, 1)
                        po.wait_ge(a.kn.sem, a.kn.at(it, 1))
                        po.tensor_tensor(kr[:], kn2c[:], half[:], ALU.pow).then_inc(a.kr.sem, 1)
                    else:
                        for b in range(SEQS):
                            diagonal(s.first, b, it)
                    rstd_of(s.first, att, it)
                    diagonal(s.second, 0, it)
                    if s.layer == 0:
                        po.wait_ge(s.second.xT_ps.sem, s.second.xT_ps.at(it, 1))
                        add_bias(x[:, s.g], x[:, s.g], "X0_bo").then_inc(s.second.xb.sem, 1)
                    for b in range(1, SEQS):
                        diagonal(s.second, b, it)
                    rstd_of(s.ffn, ffn, it)
                    rstd_of(s.second, att, it)
            rstd_of(slots[0].ffn, ffn, TURNS)

        @block.vector
        def _(dv):
            tt, ts, stt = nc.vector.tensor_tensor, nc.vector.tensor_scalar, nc.vector.scalar_tensor_tensor
            steps = [0]

            def then(ins, it):
                steps[0] += 1
                ins.then_inc(dve_step.sem, 1)
                dv.wait_ge(dve_step.sem, dve_step.at(it, steps[0]))

            def stats(s, r, g, it):
                for b in range(SEQS):
                    last = nc.vector.bn_stats(r.bn[:, b, :], x[:, g, b, :])
                then(last, it)
                nc.vector.memset(wsum[:, 2:3], 0.0)
                for b in range(SEQS):
                    last = nc.vector.bn_aggr(r.mv[:, b, :], r.bn[:, b, :])
                then(last, it)
                ts(r.var[:], r.mv[:, :, 1], EPS_LN, None, ALU.add).then_inc(s.stats.sem, 1)

            def normalise_x(s, r, g, it):
                dv.wait_ge(s.rstd.sem, s.rstd.at(it, 1))
                for b in range(SEQS):
                    ts(x[:, g, b, :], x[:, g, b, :], r.mv[:, b, 0:1], r.rstd[:, b:b + 1],
                       ALU.subtract, ALU.mult).then_inc(s.normed.sem, 1)

            def flat(g):
                return x[:, g].rearrange("p b c -> p (b c)")

            def add_output(s, g, it, beside, following):
                dv.wait_ge(s.y.sem, s.y.at(it, 1))
                tt(flat(g), Y[:], flat(g), ALU.add).then_inc(s.added.sem, 1)
                dv.wait_ge(s.added.sem, s.added.at(it, 1))
                stats(s, att, g, it)
                if following:
                    beside(beside.norm)
                if not s.late_norm:
                    normalise_x(s, att, g, it)

            def context(s, it):
                dv.wait_ge(s.c.hi.sem, s.c.hi.at(it, 1))
                tt(cT_lo[:], Y[0:CTX, :], cT_hi[:].bitcast(f32), ALU.subtract).then_inc(s.c.lo.sem, 1)

            def keys(s, it):
                dv.wait_ge(s.k_hi.sem, s.k_hi.at(it, 1))
                stt(k_lo[:], K_BANK[:], K("X0_bk") if s.biased else 0.0, k_hi[:].bitcast(f32), ALU.add, ALU.subtract).then_inc(s.k_lo.sem, 1)

            def values(s, it):
                dv.wait_ge(s.v_ps.sem, s.v_ps.at(it, 1))
                for j in range(NJ):
                    to = v_pad[:, :, NG * j:NG * (j + 1), D * j:D * (j + 1)]
                    src = V_BANK[:].rearrange("p (b j g d) -> p b j g d", b=SEQS, j=NJ, g=NG)[:, :, j]
                    if s.biased:
                        bv = K("X0_bv").rearrange("p (j g d) -> p j g d", j=NJ, g=NG)[:, j].unsqueeze(1)
                        last = tt(to, src, bv.to_broadcast((128, SEQS, NG, D)), ALU.add)
                    else:
                        last = nc.vector.tensor_copy(to, src)
                last.then_inc(s.v_sb.sem, 1)

            def linear(s, g, it, beside, c, following):
                beside()
                for b in range(SEQS):
                    dv.wait_ge(s.qkv_ps.sem, s.qkv_ps.at(it, b + 1))
                    tt(qkv[:, b, :], bank[b][:, 0:3 * C], K("A0_bqkv"), ALU.add).then_inc(s.qkv.sem, 1)
                    beside()
                context(c, it)
                beside(beside.squares)
                dv.wait_ge(s.sq.sem, s.sq.at(it, 1))
                then(ts(rsum[:], ssum[:], EPS_SUM, None, ALU.add), it)
                then(nc.vector.reciprocal(rsum[:], rsum[:]), it)
                tt(sqn.rearrange("p b i c -> p (b i) c"), sq.rearrange("p b i c -> p (b i) c"),
                   rsum[:].rearrange("p b i -> p (b i)").unsqueeze(2).to_broadcast((128, SEQS * 2, C)), ALU.mult).then_inc(s.sqn.sem, 1)
                keys(following, it)
                values(following, it)
                beside()
                dv.wait_ge(s.sq4q.sem, s.sq4q.at(it, 1))
                ts(qn2c[:], qn2[:], EPS_NORM2, None, ALU.max).then_inc(s.qn.sem, 1)
                dv.wait_ge(s.kn_ps.sem, s.kn_ps.at(it, 1))
                ts(kn2c[:], Y[:, 0:SEQS], EPS_NORM2, None, ALU.max).then_inc(s.kn.sem, 1)
                beside()
                dv.wait_ge(s.qr.sem, s.qr.at(it, 1))
                tt(q2, sqn[:, :, 0, :], qr[:].unsqueeze(2).to_broadcast((128, SEQS, C)), ALU.mult).then_inc(s.q2.sem, 1)
                dv.wait_ge(s.kr.sem, s.kr.at(it, 1))
                dv.wait_ge(s.kv_ps.sem, s.kv_ps.at(it, 1))
                for b in range(SEQS):
                    last = ts(kv[:, b, :], A0_KV[:, b * C:(b + 1) * C], kr[:, b:b + 1], float(N) ** -0.5, ALU.mult, ALU.mult)
                last.then_inc(s.kv.sem, 1)
                beside()
                beside()
                beside()
                dv.wait_ge(s.xb.sem, s.xb.at(it, 1))
                add_output(s, g, it, beside, following)

            def softmax(s, g, it, beside, slot=None, following=None, before=None):
                dv.wait_ge(s.xT_hi.sem, s.xT_hi.at(it, 1))
                tt(att.xT_lo[:], Y[:], att.xT_hi[:].bitcast(f32), ALU.subtract).then_inc(s.xT_lo.sem, 1)
                if before:
                    normalise_x(before, att, before.g, it)
                beside(beside.split)

                def diagonal(b, j):
                    if j == PO_QUADRANTS and b >= 2:
                        dv.wait_ge(s.s_ps.sem, s.s_ps.at(it, NG * (b - 1)))
                    rows = slice(SLOT * j, SLOT * (j + 1))
                    last = nc.vector.tensor_copy(k_diag[rows, b % 2, :, j, :], k_stack[rows, :, b * N:(b + 1) * N].bitcast(f32))
                    if j == NJ - 1:
                        last.then_inc(s.k_diag.sem, 1)

                def maximum(b, g):
                    if g == 0 and b >= 2:
                        dv.wait_ge(s.m_ps.sem, s.m_ps.at(it, b - 1))
                    dv.wait_ge(s.s_ps.sem, s.s_ps.at(it, b * NG + g + 1))
                    nc.vector.tensor_reduce(row_max[:, b % 2, NJ * g:NJ * (g + 1)],
                                            score_bank(b, g)[:].rearrange("p (j k) -> p j k", j=NJ), AX, ALU.max).then_inc(s.max.sem, 1)

                def normalise(b):
                    dv.wait_ge(s.pv.sem, s.pv.at(it, b + 1))
                    num, den = heads(b)
                    nc.vector.reciprocal(rden[:, b % 2, :], den).then_inc(s.rden.sem, 1)
                    dv.wait_ge(s.rden.sem, s.rden.at(it, b + 1))
                    tt(attT[:, b % 2, :], num, rden[:, b % 2, :], ALU.mult).then_inc(s.att.sem, 1)

                if s.cross:
                    dv.wait_ge(s.k_in.sem, s.k_in.at(it, 3 * 16))
                    for j in range(PO_QUADRANTS, NJ):
                        diagonal(0, j)
                else:
                    keys(s, it)
                dv.wait_ge(s.q_hi.sem, s.q_hi.at(it, 1))
                stt(q_lo[:], Q_BANK[:], K("X0_bq") if s.biased else 0.0, q_hi[:].bitcast(f32), ALU.add, ALU.subtract).then_inc(s.q_lo.sem, 1)
                if not s.cross:
                    values(s, it)
                if following:
                    context(slot, it)
                beside(beside.stacks)
                if not s.cross:
                    dv.wait_ge(s.k_in.sem, s.k_in.at(it, 3 * 16))
                    for j in range(PO_QUADRANTS, NJ):
                        diagonal(0, j)
                for step in range(SEQS + 3):
                    for j in range(NG):
                        if step < SEQS:
                            maximum(step, j)
                        if step + 1 < SEQS and j >= PO_QUADRANTS:
                            diagonal(step + 1, j)
                        if j == NJ - 1 and step >= 3:
                            normalise(step - 3)
                        beside(beside.step[step])
                if following:
                    keys(following, it)
                    values(following, it)
                if s.biased:
                    dv.wait_ge(s.xb.sem, s.xb.at(it, 1))
                add_output(s, g, it, beside, following)

            def first_of_max(p, n, mx, onehot, it):
                first = K("first")[:, 0:n].unsqueeze(1).to_broadcast((128, SEQS, n))
                then(nc.vector.tensor_reduce(mx[:], p, AX, ALU.max), it)
                then(tt(onehot, p, mx[:].unsqueeze(2).to_broadcast((128, SEQS, n)), ALU.is_equal), it)
                then(tt(onehot, onehot, first, ALU.mult), it)
                then(nc.vector.tensor_reduce(rs[3][:], onehot, AX, ALU.max), it)
                then(tt(onehot, rs[3][:].unsqueeze(2).to_broadcast((128, SEQS, n)), first, ALU.is_equal), it)

            def logits0(s, it):
                dv.wait_ge(s.r_ps.sem, s.r_ps.at(it, 1))
                then(tt(rt[0][:], DOWN[:, 0:SEQS * 8].rearrange("p (b e) -> p b e", e=8),
                        K("F0_brouter").unsqueeze(1).to_broadcast((128, SEQS, 8)), ALU.add), it)
                ts(rt[0][:], rt[0][:], -50.0, 50.0, ALU.max, ALU.min).then_inc(s.r_arg.sem, 1)

            def coef0(s, it, part):
                n = E0
                p, oh = rt[2][:, :, 0:n], rt[3][:, :, 0:n]
                if part == 0:
                    choose0(s, p, oh, it)
                    return
                then(ts(rs[0][:], rs[0][:], 1e-8, 1.0 - 1e-8, ALU.max, ALU.min), it)
                then(ts(rs[1][:], rs[0][:], 0.5, 1e-8, ALU.add, ALU.add), it)
                then(ts(rs[1][:], rs[1][:], 0.5, 2.0, ALU.max, ALU.min), it)
                then(nc.vector.reciprocal(rs[1][:], rs[1][:]), it)
                ts(coef[:, :, 0], rs[1][:], 0.5, 0.5, ALU.mult, ALU.mult)
                then(stt(rs[2][:], rs[0][:], 0.5, rs[1][:], ALU.mult, ALU.mult), it)
                then(tt(coef[:, :, 1:1 + n], oh, rs[2][:].unsqueeze(2).to_broadcast((128, SEQS, n)), ALU.mult), it)

            def choose0(s, p, oh, it):
                dv.wait_ge(s.r_exp.sem, s.r_exp.at(it, 1))
                then(ts(rt[2][:], rt[1][:], 1.0, None, ALU.add), it)
                then(nc.vector.reciprocal(rt[2][:], rt[2][:]), it)
                first_of_max(p, n, rs[0], oh, it)

            def logits1(s, it):
                dv.wait_ge(s.r_ps.sem, s.r_ps.at(it, 1))
                ps = DOWN[:, 0:SEQS * 8].rearrange("p (b e) -> p b e", e=8)
                then(nc.vector.tensor_reduce(rs[0][:], ps, AX, ALU.max), it)
                tt(rt[0][:], ps, rs[0][:].unsqueeze(2).to_broadcast((128, SEQS, E1)), ALU.subtract).then_inc(s.r_arg.sem, 1)

            def coef1(s, it, part):
                n = E1
                p, oh1, oh2, p2 = rt[2][:], rt[3][:], rt[4][:], rt[5][:]
                if part == 1:
                    then(stt(p2, oh1, -2.0, p, ALU.mult, ALU.add), it)
                    first_of_max(p2, n, rs[0], oh2, it)
                    then(tt(oh1, oh1, oh2, ALU.add), it)
                    nc.vector.memset(coef[:, :, 0], 0.5)
                    then(stt(coef[:, :, 1:1 + n], oh1, 0.5, p, ALU.mult, ALU.mult), it)
                    return
                dv.wait_ge(s.r_exp.sem, s.r_exp.at(it, 1))
                then(nc.vector.tensor_reduce(rs[1][:], rt[1][:], AX, ALU.add), it)
                then(nc.vector.reciprocal(rs[1][:], rs[1][:]), it)
                then(tt(p, rt[1][:], rs[1][:].unsqueeze(2).to_broadcast((128, SEQS, n)), ALU.mult), it)
                first_of_max(p, n, rs[0], oh1, it)

            def experts(s, it, unit):
                kind, *k = unit
                if kind == "split":
                    dv.wait_ge(s.xT_hi.sem, s.xT_hi.at(it, 1))
                    tt(ffn.xT_lo[:], DOWN[:], ffn.xT_hi[:].bitcast(f32), ALU.subtract).then_inc(s.xT_lo.sem, 1)
                elif kind == "router":
                    (logits0 if s.name == "F0" else logits1)(s, it)
                elif kind == "coef":
                    (coef0 if s.name == "F0" else coef1)(s, it, k[0])
                elif kind == "gate":
                    u, = k
                    n = s.chunks[u][3]
                    dv.wait_ge(s.tanh.sem, s.tanh.at(it, u + 1))
                    stt(gate[0:n, u % 2, :], gate[0:n, u % 2, :], 1.0, GATE[0:n, :], ALU.add, ALU.mult).then_inc(s.silu.sem, 1)
                elif kind == "up":
                    u, = k
                    n = s.chunks[u][3]
                    if u >= 2:
                        dv.wait_ge(s.down.sem, s.down.at(it, sum(p[1] <= u - 2 for p in s.pieces)))
                    dv.wait_ge(s.up_ps.sem, s.up_ps.at(it, u + 1))
                    dv.wait_ge(s.silu.sem, s.silu.at(it, u + 1))
                    tt(hidden[0:n, u % 2, :], UP[0:n, :], gate[0:n, u % 2, :], ALU.mult).then_inc(s.hid.sem, 1)
                elif kind == "down" and s.pieces[k[0]][7]:
                    e = s.pieces[k[0]][0]
                    dv.wait_ge(s.down.sem, s.down.at(it, k[0] + 1))
                    if e:
                        dv.wait_ge(s.comb.sem, s.comb.at(it, e))
                    for b in range(SEQS):
                        last = stt(x[:, s.g, b, :], DOWN[:, b * C:(b + 1) * C], coef[:, b, e:e + 1],
                                   x[:, s.g, b, :], ALU.mult, ALU.add)
                    last.then_inc(s.comb.sem, 1)
                elif kind == "stats":
                    dv.wait_ge(s.comb.sem, s.comb.at(it, s.n))
                    stats(s, ffn, s.g, it)
                elif kind == "norm":
                    normalise_x(s, ffn, s.g, it)

            for n in range(n_stages):
                dv.wait_ge(ld_stage[n % STAGES], 16 * (n // STAGES + 1))
                cols = slice(n * STAGE, (n + 1) * STAGE)
                nc.vector.tensor_copy(w_hi[:, cols], stage[:, n % STAGES, :]).then_inc(st_hi, 1)
                dv.wait_ge(st_hi, n + 1)
                tt(w_lo[:, cols], stage[:, n % STAGES, :], w_hi[:, cols].bitcast(f32), ALU.subtract).then_inc(st_lo, 1)
            dv.wait_ge(ld_const, 48)
            for i, m in enumerate((W("A0_qkv"), K("A0_bqkv"))):
                for j in range(2):
                    part = m[:, j * C:(j + 1) * C]
                    nc.vector.tensor_reduce(wsum[:, 0:1], part, AX, ALU.add).then_inc(centred_step, 1)
                    dv.wait_ge(centred_step, 3 * (2 * i + j) + 1)
                    ts(wsum[:, 1:2], wsum[:, 0:1], 1.0 / C, None, ALU.mult).then_inc(centred_step, 1)
                    dv.wait_ge(centred_step, 3 * (2 * i + j) + 2)
                    ts(part, part, wsum[:, 1:2], None, ALU.subtract).then_inc(centred_step, 1)
                    dv.wait_ge(centred_step, 3 * (2 * i + j) + 3)
            nc.vector.memset(wsum[:, 3:4], 0.0).then_inc(centred, 1)
            dv.wait_ge(fills, 1)
            for g in range(2):
                dv.wait_ge(x_free[g].sem, 16)
            nc.vector.memset(wsum[:, 4:5], 0.0).then_inc(slots[-1].second.normed.sem, SEQS)
            nc.vector.memset(wsum[:, 5:6], 0.0).then_inc(slots[-1].second.added.sem, 1)

            with dv.Fori(0, TURNS) as it:
                for s in slots:
                    beside = Beside(s, lambda unit: experts(s.ffn, it, unit), 1)
                    if s.layer == 0:
                        linear(s.first, s.g, it, beside, s, s.second)
                    else:
                        softmax(s.first, s.g, it, beside, s, s.second, s.before)
                    softmax(s.second, s.g, it, beside)
                    beside.end()
            assert steps[0] == DVE_STEPS, steps[0]
            steps[0] = 0
            for unit in slots[0].ffn.units:
                experts(slots[0].ffn, TURNS, unit)


def _packed(parts, table, cols, rows=128):
    out = np.zeros((rows, cols), np.float32)
    for name, a in parts.items():
        c0, _ = table[name]
        out[:a.shape[0], c0:c0 + a.shape[1]] = a
    return out


def _slots(w):
    return w.reshape(w.shape[0], NJ, NG, D).transpose(0, 1, 3, 2).reshape(w.shape[0], C)


def _out_rows(w):
    return w.reshape(NJ, NG, D, C).transpose(1, 0, 2, 3).reshape(C, C)


def _chunk_rows(w):
    out = np.zeros((128, 3 * C), w.dtype)
    for i, (r0, n) in enumerate(CHUNKS0):
        out[:n, i * C:(i + 1) * C] = w[r0:r0 + n]
    return out


def _rows(v):
    return np.broadcast_to(v[None, :], (128, v.shape[0]))


def _layout(a):
    split = {
        "X0_q": _slots(a["L0_xattn_Wq"]), "X0_k": _slots(a["L0_xattn_Wk"]),
        "A1_q": _slots(a["L1_attn_Wq"]), "A1_k": _slots(a["L1_attn_Wk"]),
        "X1_q": _slots(a["L1_xattn_Wq"]), "X1_k": _slots(a["L1_xattn_Wk"]),
        "F0_gate0": a["L0_ffn_sw1"].T, "F0_up0": a["L0_ffn_sw3"].T,
        "F1_gate": np.concatenate([a["L1_ffn_shared_gate"], *a["L1_ffn_experts_gate"]], 1),
        "F1_up": np.concatenate([a["L1_ffn_shared_up"], *a["L1_ffn_experts_up"]], 1)}
    plain = {
        "A0_qkv": a["L0_attn_Wqkv"], "A0_out": a["L0_attn_Wln"],
        "X0_v": a["L0_xattn_Wv"], "X0_o": _out_rows(a["L0_xattn_Wo"]),
        "A1_v": a["L1_attn_Wv"], "A1_o": _out_rows(a["L1_attn_Wo"]),
        "X1_v": a["L1_xattn_Wv"], "X1_o": _out_rows(a["L1_xattn_Wo"]),
        "F0_router": a["L0_ffn_router_w"].T, "F1_router": a["L1_ffn_router"],
        "F0_down0": _chunk_rows(a["L0_ffn_sw2"].T),
        "F1_down": np.concatenate([a["L1_ffn_shared_down"], *a["L1_ffn_experts_down"].reshape(E1 // 2, 128, C)], 1)}
    for e in range(E0):
        split[f"F0_gate{e + 1}"] = a["L0_ffn_ew1"][e].T
        split[f"F0_up{e + 1}"] = a["L0_ffn_ew3"][e].T
        plain[f"F0_down{e + 1}"] = _chunk_rows(a["L0_ffn_ew2"][e].T)
    sums = np.zeros((128, NJ, SLOT), np.float32)
    for j in range(NJ):
        sums[:, j, D * j:D * (j + 1)] = 1
    bqkv = a["L0_attn_bqkv"]
    const = {
        "ident": np.eye(128, dtype=np.float32), "sum": sums.reshape(128, -1),
        "first": _rows(np.arange(8, 0, -1).astype(np.float32)),
        "A0_bqkv": _rows(bqkv), "A0_bout": _rows(a["L0_attn_bln"]), "X0_bv": _rows(a["L0_xattn_bv"]),
        "X0_bo": _rows(a["L0_xattn_bo"]), "F0_brouter": _rows(a["L0_ffn_routing_bias"]),
        "X0_bq": _slots(a["L0_xattn_bq"][None]).T, "X0_bk": _slots(a["L0_xattn_bk"][None]).T,
        "A0_bv": bqkv[2 * C:, None], "one": np.ones((128, 1), np.float32)}
    query, key = np.arange(N)[:, None], np.arange(N)[None, :]
    seen = (query - key >= 0) & (query - key < WIN)
    mask = np.where(seen, 0.0, MASKED)
    masks = np.concatenate([np.tile(mask, (1, NG)), np.tile(mask.T, (1, NG)), np.eye(N)], 1)
    return (_packed(split, SPLIT, SPLIT_COLS), _packed(plain, PLAIN, PLAIN_COLS),
            _packed(const, CONST, CONST_COLS), masks)


def kernel(**inputs):
    import numpy as _np
    import concourse.bacc as _bacc
    from concourse import mybir as _mybir
    from concourse.bass_utils import run_bass_kernel_spmd as _run

    a = {k: _np.asarray(v) for k, v in inputs.items()}
    split, plain, const, masks = _layout(a)
    bf16 = _mybir.dt.np(_mybir.dt.bfloat16)
    arrays = {"x": _np.ascontiguousarray(a["x"]), "ctx": _np.ascontiguousarray(a["ctx_768"]), "split": split, "plain": plain,
              "const": const, "masks": masks.astype(bf16)}
    nc = _bacc.Bacc("TRN2", target_bir_lowering=False, num_devices=1)
    args = [nc.dram_tensor(f"in_{n}", v.shape, _mybir.dt.from_np(v.dtype), kind="ExternalInput").ap() for n, v in arrays.items()]
    out = nc.dram_tensor("out_x", (B, N, C), _mybir.dt.float32, kind="ExternalOutput").ap()
    decoder_kernel(nc, *args, out)
    r = _run(nc, [{f"in_{n}": v for n, v in arrays.items()}], core_ids=[0])
    return r.results[0]["out_x"]
```
